# Optimizing a Trainium2 kernel written in Bass

```python
import numpy as np
import jax
import jax.numpy as jnp

def _softmax(x, axis=-1):
    return jax.nn.softmax(x, axis=axis)

def _gelu(x):
    return jax.nn.gelu(x, approximate=True)

def _silu(x):
    return jax.nn.silu(x)

def _sigmoid(x):
    return jax.nn.sigmoid(x)

def _layernorm(x, axis=-1, eps=1e-05):
    m = jnp.mean(x, axis=axis, keepdims=True)
    v = jnp.var(x, axis=axis, keepdims=True)
    return (x - m) / jnp.sqrt(v + eps)

def _scatter_add(tgt, idx, src, axis=0):
    return tgt.at[idx].add(src)

def _segment_sum(src, seg, n):
    return jax.ops.segment_sum(src, seg, n)
kernel_name = 'mk_adaln_d1_jaxref_r8_ce1d22'

def setup_inputs(seed: int=0):
    np.random.seed(seed)
    _w = jnp.asarray

    def _L0_attn_setup():
        import jax, jax.numpy as jnp
        import numpy as np
        D_MODEL = 128
        NHEAD = 16
        HEAD_DIM = D_MODEL // NHEAD
        GN_EPS = 0.00064
        NORM_EPS = 1e-06
        B, T = (4, 128)

        def _xavier(key, shape):
            lim = float(np.sqrt(6.0 / (shape[0] + shape[1])))
            return jax.random.uniform(key, shape, jnp.float32, -lim, lim)

        def _l2norm(t):
            n = jnp.linalg.norm(t, axis=-1, keepdims=True)
            return t / jnp.maximum(n, NORM_EPS)
        key = jax.random.key(seed)
        ks = jax.random.split(key, 10)
        D = D_MODEL
        ddd = jnp.linspace(0.0, 1.0, D, dtype=jnp.float32)
        inp = {'x': jax.random.normal(ks[0], (B, T, D), jnp.float32), 'x_r': 1.0 - ddd ** 0.2, 'x_w': 1.0 - ddd ** 0.9, 'x_k': 1.0 - ddd ** 0.7, 'x_v': 1.0 - ddd ** 0.7, 'x_a': 1.0 - ddd ** 0.9, 'x_b': 1.0 - ddd ** 0.9, 'x_g': 1.0 - ddd ** 0.2, 'W_r': _xavier(ks[1], (D, D)), 'W_w': _xavier(ks[2], (D, D)), 'W_k': _xavier(ks[3], (D, D)), 'W_v': _xavier(ks[4], (D, D)), 'W_a': _xavier(ks[5], (D, D)), 'W_b': _xavier(ks[6], (D, D)), 'W_g': _xavier(ks[7], (D, D)), 'W_o': _xavier(ks[8], (D, D)) * 0.1, 'b_o': jnp.zeros((D,), jnp.float32), 'gn_w': jnp.ones((D,), jnp.float32), 'gn_b': jnp.zeros((D,), jnp.float32)}
        return inp
    _L0_attn_in = _L0_attn_setup()

    def _L0_ffn_setup():
        import jax, jax.numpy as jnp
        import numpy as np
        B, T, C = (2, 64, 128)
        I = 512
        E = 8
        K = 2
        key = jax.random.key(seed)
        ks = jax.random.split(key, 8)
        s = 0.02
        return {'x': jax.random.normal(ks[0], (B, T, C), jnp.float32), 'Wr1': jax.random.normal(ks[1], (C, C // 4), jnp.float32) * s, 'br1': jnp.zeros((C // 4,), jnp.float32), 'Wr2': jax.random.normal(ks[2], (C // 4, E), jnp.float32) * s, 'br2': jnp.zeros((E,), jnp.float32), 'Ws1': jax.random.normal(ks[3], (C, I), jnp.float32) * s, 'bs1': jnp.zeros((I,), jnp.float32), 'Ws2': jax.random.normal(ks[4], (I, C), jnp.float32) * s, 'bs2': jnp.zeros((C,), jnp.float32), 'We1': jax.random.normal(ks[5], (E, C, I), jnp.float32) * s, 'be1': jnp.zeros((E, I), jnp.float32), 'We2': jax.random.normal(ks[6], (E, I, C), jnp.float32) * s, 'be2': jnp.zeros((E, C), jnp.float32)}
    _L0_ffn_in = _L0_ffn_setup()
    _L0_c = _w((lambda *s: np.random.randn(*s).astype(np.float32) * 0.05)(4, 128))
    _L0_wmod = _w((lambda *s: np.random.randn(*s).astype(np.float32) * 0.05)(128, 6 * 128) * 128 ** (-0.5))
    _d = {'L0_attn_x': _L0_attn_in['x'], 'L0_attn_x_r': _L0_attn_in['x_r'], 'L0_attn_x_w': _L0_attn_in['x_w'], 'L0_attn_x_k': _L0_attn_in['x_k'], 'L0_attn_x_v': _L0_attn_in['x_v'], 'L0_attn_x_a': _L0_attn_in['x_a'], 'L0_attn_x_b': _L0_attn_in['x_b'], 'L0_attn_x_g': _L0_attn_in['x_g'], 'L0_attn_W_r': _L0_attn_in['W_r'], 'L0_attn_W_w': _L0_attn_in['W_w'], 'L0_attn_W_k': _L0_attn_in['W_k'], 'L0_attn_W_v': _L0_attn_in['W_v'], 'L0_attn_W_a': _L0_attn_in['W_a'], 'L0_attn_W_b': _L0_attn_in['W_b'], 'L0_attn_W_g': _L0_attn_in['W_g'], 'L0_attn_W_o': _L0_attn_in['W_o'], 'L0_attn_b_o': _L0_attn_in['b_o'], 'L0_attn_gn_w': _L0_attn_in['gn_w'], 'L0_attn_gn_b': _L0_attn_in['gn_b'], 'L0_ffn_Wr1': _L0_ffn_in['Wr1'], 'L0_ffn_br1': _L0_ffn_in['br1'], 'L0_ffn_Wr2': _L0_ffn_in['Wr2'], 'L0_ffn_br2': _L0_ffn_in['br2'], 'L0_ffn_Ws1': _L0_ffn_in['Ws1'], 'L0_ffn_bs1': _L0_ffn_in['bs1'], 'L0_ffn_Ws2': _L0_ffn_in['Ws2'], 'L0_ffn_bs2': _L0_ffn_in['bs2'], 'L0_ffn_We1': _L0_ffn_in['We1'], 'L0_ffn_be1': _L0_ffn_in['be1'], 'L0_ffn_We2': _L0_ffn_in['We2'], 'L0_ffn_be2': _L0_ffn_in['be2'], 'L0_c': _L0_c, 'L0_wmod': _L0_wmod}
    _x0 = _d['L0_attn_x']
    _d['L0_attn_x'] = jax.random.normal(jax.random.fold_in(jax.random.key(seed), 1), (4, 1024, 128), dtype=_x0.dtype)
    del _x0
    return _d

def reference(L0_attn_x, L0_attn_x_r, L0_attn_x_w, L0_attn_x_k, L0_attn_x_v, L0_attn_x_a, L0_attn_x_b, L0_attn_x_g, L0_attn_W_r, L0_attn_W_w, L0_attn_W_k, L0_attn_W_v, L0_attn_W_a, L0_attn_W_b, L0_attn_W_g, L0_attn_W_o, L0_attn_b_o, L0_attn_gn_w, L0_attn_gn_b, L0_ffn_Wr1, L0_ffn_br1, L0_ffn_Wr2, L0_ffn_br2, L0_ffn_Ws1, L0_ffn_bs1, L0_ffn_Ws2, L0_ffn_bs2, L0_ffn_We1, L0_ffn_be1, L0_ffn_We2, L0_ffn_be2, L0_c, L0_wmod):

    def _L0_attn_ref(x, x_r, x_w, x_k, x_v, x_a, x_b, x_g, W_r, W_w, W_k, W_v, W_a, W_b, W_g, W_o, b_o, gn_w, gn_b):
        import jax, jax.numpy as jnp
        import numpy as np
        D_MODEL = 128
        NHEAD = 16
        HEAD_DIM = D_MODEL // NHEAD
        GN_EPS = 0.00064
        NORM_EPS = 1e-06
        B, T = (4, 128)

        def _xavier(key, shape):
            lim = float(np.sqrt(6.0 / (shape[0] + shape[1])))
            return jax.random.uniform(key, shape, jnp.float32, -lim, lim)

        def _l2norm(t):
            n = jnp.linalg.norm(t, axis=-1, keepdims=True)
            return t / jnp.maximum(n, NORM_EPS)
        Bs, Ts, D = x.shape
        H, K = (NHEAD, HEAD_DIM)
        prev = jnp.concatenate([jnp.zeros_like(x[:, :1]), x[:, :-1]], axis=1)
        xx = prev - x

        def proj(mix, W):
            return jnp.einsum('btd,ed->bte', x + xx * mix, W)
        heads = lambda t: t.reshape(Bs, Ts, H, K)
        r = heads(proj(x_r, W_r))
        w = -jax.nn.softplus(heads(proj(x_w, W_w)))
        k = jnp.tanh(heads(proj(x_k, W_k)))
        v = heads(proj(x_v, W_v))
        a = _l2norm(heads(proj(x_a, W_a)))
        b = _l2norm(heads(proj(x_b, W_b)))
        g = jax.nn.sigmoid(proj(x_g, W_g))

        def step(S, ins):
            r_t, w_t, k_t, v_t, a_t, b_t = ins
            Sa = jnp.einsum('bhvk,bhk->bhv', S, a_t)
            S = S * jnp.exp(w_t)[:, :, None, :] + Sa[..., None] * b_t[:, :, None, :] + v_t[..., None] * k_t[:, :, None, :]
            o = jnp.einsum('bhvk,bhk->bhv', S, r_t)
            return (S, o)
        tm = lambda t: jnp.moveaxis(t, 1, 0)
        S0 = jnp.zeros((Bs, H, K, K), jnp.float32)
        _, o = jax.lax.scan(step, S0, (tm(r), tm(w), tm(k), tm(v), tm(a), tm(b)))
        mixed = jnp.moveaxis(o, 0, 1).reshape(Bs, Ts, D)
        gm = mixed.reshape(Bs * Ts, H, K)
        mu = gm.mean(-1, keepdims=True)
        var = gm.var(-1, keepdims=True)
        normed = ((gm - mu) * jax.lax.rsqrt(var + GN_EPS)).reshape(Bs * Ts, D)
        normed = (normed * gn_w + gn_b).reshape(Bs, Ts, D)
        return jnp.einsum('btd,ed->bte', normed * g, W_o) + b_o

    def _L0_ffn_ref(x, Wr1, br1, Wr2, br2, Ws1, bs1, Ws2, bs2, We1, be1, We2, be2):
        import jax, jax.numpy as jnp
        import numpy as np
        B, T, C = (2, 64, 128)
        I = 512
        E = 8
        K = 2
        Bb, Tt, Cc = x.shape
        xf = x.reshape(-1, Cc)
        logits = jax.nn.relu(xf @ Wr1 + br1) @ Wr2 + br2
        gates = jax.nn.softmax(logits, axis=-1)
        tg, ti = jax.lax.top_k(gates, K)
        tg = jax.nn.softmax(tg / K, axis=-1)
        out = jax.nn.silu(xf @ Ws1 + bs1) @ Ws2 + bs2
        for e in range(E):
            h = jax.nn.silu(xf @ We1[e] + be1[e]) @ We2[e] + be2[e]
            w = jnp.sum(tg * (ti == e), axis=-1)
            out = out + w[:, None] * h
        return out.reshape(Bb, Tt, Cc)
    x = L0_attn_x
    mod = (_silu(L0_c) @ L0_wmod).reshape(L0_c.shape[0], 6, 1, -1)
    sa, ca, ga, sb, cb, gb = (mod[:, 0], mod[:, 1], mod[:, 2], mod[:, 3], mod[:, 4], mod[:, 5])
    ga = (2 * (ga >= 0) - 1) * jnp.maximum(jnp.abs(ga), 0.25)
    gb = (2 * (gb >= 0) - 1) * jnp.maximum(jnp.abs(gb), 0.25)
    h = _layernorm(x, axis=-1) * (1 + ca) + sa
    x = x + ga * _L0_attn_ref(h, L0_attn_x_r, L0_attn_x_w, L0_attn_x_k, L0_attn_x_v, L0_attn_x_a, L0_attn_x_b, L0_attn_x_g, L0_attn_W_r, L0_attn_W_w, L0_attn_W_k, L0_attn_W_v, L0_attn_W_a, L0_attn_W_b, L0_attn_W_g, L0_attn_W_o, L0_attn_b_o, L0_attn_gn_w, L0_attn_gn_b)
    h = _layernorm(x, axis=-1) * (1 + cb) + sb
    x = x + gb * _L0_ffn_ref(h, L0_ffn_Wr1, L0_ffn_br1, L0_ffn_Wr2, L0_ffn_br2, L0_ffn_Ws1, L0_ffn_bs1, L0_ffn_Ws2, L0_ffn_bs2, L0_ffn_We1, L0_ffn_be1, L0_ffn_We2, L0_ffn_be2)
    return x

_drawn_inputs = setup_inputs


def setup_inputs(seed=0):
    import zlib

    import numpy as np

    out = dict(_drawn_inputs(seed))
    spreads = {'L0_attn_b_o': (0.0, 0.306),
     'L0_attn_gn_w': (1.0, 0.6),
     'L0_attn_gn_b': (0.0, 0.8),
     'L0_ffn_br1': (0.0, 0.8),
     'L0_ffn_br2': (0.0, 0.331),
     'L0_ffn_bs1': (0.0, 0.8),
     'L0_ffn_bs2': (0.0, 0.336),
     'L0_ffn_be1': (0.0, 0.8),
     'L0_ffn_be2': (0.0, 0.467)}
    factors = {'L0_attn_x_r': 8.0,
     'L0_attn_x_w': 8.0,
     'L0_attn_x_k': 6.899,
     'L0_attn_x_v': 7.61,
     'L0_attn_x_a': 8.0,
     'L0_attn_x_b': 8.0,
     'L0_attn_x_g': 8.0,
     'L0_attn_W_r': 4.136,
     'L0_attn_W_w': 8.0,
     'L0_attn_W_k': 4.149,
     'L0_attn_W_v': 4.144,
     'L0_attn_W_a': 8.0,
     'L0_attn_W_b': 8.0,
     'L0_attn_W_g': 8.0,
     'L0_attn_W_o': 4.114,
     'L0_ffn_Wr1': 7.191,
     'L0_ffn_Wr2': 4.356,
     'L0_ffn_Ws1': 4.329,
     'L0_ffn_Ws2': 3.949,
     'L0_ffn_We1': 6.148,
     'L0_ffn_We2': 5.666}
    for name, (base, spread) in spreads.items():
        noise = np.random.default_rng([zlib.crc32(name.encode()), seed]).standard_normal(out[name].shape)
        drawn = base * np.exp(spread * noise) if base else spread * noise
        out[name] = jnp.asarray(drawn.astype(out[name].dtype))
    for name, factor in factors.items():
        out[name] = (out[name] * factor).astype(out[name].dtype)
    return out
```

```python
from contextlib import ExitStack

import numpy as np

import concourse.bass as bass
from concourse import mybir

BATCH, TIME, D = 4, 1024, 128
HEADS, K = 16, 8
HIDDEN, EXPERTS = 512, 8
ROUTER = D // 4
STEPS = 64
L = 4
TILES = TIME // STEPS
C = STEPS // L
CB = C * BATCH
N = BATCH * STEPS
TG = N // 128
HB = HIDDEN // 128
VH = K // 2
NG = L * (L - 1) // 2
Y0 = 0
X0 = Y0 + C * (L + 1)
B0 = X0 + STEPS
K0 = B0 + STEPS
G0 = K0 + STEPS
SENT = G0 + C * NG
RX = K + L - 1
SLOTS = 20
LN_EPS, GN_EPS, NORM_EPS, GATE_MIN = 1e-5, 6.4e-4, 1e-6, 0.25
PROJ = ["w", "a", "b", "r", "k", "v", "g"]
MIX0, BO, GNW, GNB, BR1, BE1 = 0, 7, 8, 9, 10, 11
VECS = BE1 + (EXPERTS + 1) * HB
LAG_PROJ, LAG_CHUNK, LAG_SCAN, LAG_GN, LAG_LN2, LAG_FFN, LAG_OUT = -2, -1, 0, 1, 2, 3, 4


class Tile:
    def __init__(self, half, par):
        self.half, self.par, self.t = half, par, half * 2 + par


class Round:

    def __init__(self, i, tile_of):
        self.i, self.tile_of = i, tile_of

    def __call__(self, lag):
        return self.tile_of(lag)

    def before(self, lag):
        n = self.i - lag
        return max(0, min(TILES, n)) if isinstance(n, int) else n

    def through(self, lag):
        n = self.i - lag + 1
        return max(0, min(TILES, n)) if isinstance(n, int) else n


def run_tiles(eng, work):
    def fixed(i):
        def tile_of(lag):
            t = i - lag
            return Tile(t // 2, t % 2) if 0 <= t < TILES else None
        return Round(i, tile_of)

    first = LAG_OUT + 2
    last = TILES + LAG_PROJ
    for i in range(LAG_PROJ, first):
        work(fixed(i))
    with eng.Fori(first // 2, last // 2) as pair:
        for u in range(2):
            work(Round(pair * 2 + u, lambda lag, u=u: Tile(pair + (u - lag) // 2, (u - lag) % 2)))
    for i in range(last, TILES + LAG_OUT):
        work(fixed(i))


def build(nc, x_d, w_d, vec_d, cond_d, wmod_d, wr1_d, wr2_d, w1_d, w2_d, be2_d, out_d):
    F32, U32 = mybir.dt.float32, mybir.dt.uint32
    ALU, ACT, AX = mybir.AluOpType, mybir.ActivationFunctionType, mybir.AxisListType
    ctx = ExitStack()
    with ctx:
        def sb(name, shape, dt=F32):
            return ctx.enter_context(nc.sbuf_tensor(name, shape, dt))

        def two(name, shape, dt=F32):
            return [sb(f"{name}{i}", shape, dt) for i in range(2)]

        def sem(name):
            return ctx.enter_context(nc.semaphore(name))

        w_proj = sb("w_proj", [128, 8, 128])
        vec = sb("vec", [128, VECS])
        cond = sb("cond", [128, BATCH])
        cond_act = sb("cond_act", [128, BATCH])
        wmod = sb("wmod", [128, 6 * 128])
        wr1 = sb("wr1", [128, ROUTER])
        wr2 = sb("wr2", [ROUTER + 1, EXPERTS])
        w1 = sb("w1", [128, EXPERTS + 1, HIDDEN])
        w2 = sb("w2", [128, EXPERTS + 1, HB, 128])
        be2 = sb("be2", [EXPERTS + 1, 128])
        ones_ch = sb("ones_ch", [128, 128])
        ones_hd = sb("ones_hd", [128, 128])
        mean_hd = sb("mean_hd", [128, 128])
        band = sb("band", [128, 128])
        ident = sb("ident", [128, 128])
        iota_i = sb("iota_i", [128, EXPERTS], mybir.dt.int32)
        iota_f = sb("iota_f", [128, EXPERTS])
        eps_ln = sb("eps_ln", [128, 1])
        eps_gn = sb("eps_gn", [128, 1])
        mod = sb("mod", [128, 6, BATCH])
        mod_sign = sb("mod_sign", [128, 2, BATCH])
        mod_abs = sb("mod_abs", [128, 2, BATCH])
        ga_bo = sb("ga_bo", [128, BATCH])

        x_in = two("x_in", [128, N])
        ln1_c = sb("ln1_c", [128, N])
        ln1_sq = sb("ln1_sq", [128, N])
        ln1_sd = sb("ln1_sd", [128, N])
        ln1_n = sb("ln1_n", [128, N])
        h1 = two("h1", [128, BATCH, STEPS + 1])
        shift = sb("shift", [128, BATCH, STEPS])
        mixed = sb("mixed", [128, 7, N])
        w_tanh = sb("w_tanh", [128, N])
        g_tanh = sb("g_tanh", [128, N])
        gate = two("gate", [128, N])
        gate_late = two("gate_late", [128, N])
        ab_raw = sb("ab_raw", [128, 2, N])
        ab_sq = sb("ab_sq", [128, 2, N])
        ab_norm = sb("ab_norm", [128, 2 * N])
        dec = two("dec", [128, CB, L])
        b_raw = two("b_raw", [128, CB, L])
        k_raw = two("k_raw", [128, CB, L])
        r_raw = two("r_raw", [128, CB, L])
        ar = two("ar", [128, 2, CB, L])
        v_send = two("v_send", [128, BATCH, STEPS])
        q = sb("q", [128, 2, CB, L])
        q_mul = sb("q_mul", [128, 2 * CB * (L - 1)])
        q_rank = sb("q_rank", [128, 2 * CB * (L - 1)])
        q_dec = sb("q_dec", [128, 2 * CB * (L - 1)])
        kb = sb("kb", [128, 2, CB, L])
        k_mul = sb("k_mul", [128, 2 * CB * (L - 1)])
        k_rank = sb("k_rank", [128, CB * (L - 1)])
        lam = sb("lam", [128, CB, L])
        send = sb("send", [128, BATCH, SENT])
        ops = two("ops", [128, K, SENT])
        vals = two("vals", [128, VH, STEPS])
        terms = sb("terms", [128, C, L + 2, VH * K])
        u_mul = sb("u_mul", [128, C, VH, K])
        z = two("z", [128, C, L * VH])
        state = two("state", [128, C + 1, VH * K])
        o_terms = sb("o_terms", [128, C * L * VH, RX])
        o_scan = two("o_scan", [128, VH, STEPS])
        o_ch = two("o_ch", [128, N])
        gn_c = sb("gn_c", [128, N])
        gn_sq = sb("gn_sq", [128, N])
        gn_sd = sb("gn_sd", [128, N])
        gn_n = sb("gn_n", [128, N])
        gn_a = sb("gn_a", [128, N])
        gn_g = sb("gn_g", [128, N])
        x_res = two("x_res", [128, N])
        x_bias = sb("x_bias", [128, N])
        x2 = two("x2", [128, N])
        x2_late = two("x2_late", [128, N])
        ln2_c = sb("ln2_c", [128, N])
        ln2_sq = sb("ln2_sq", [128, N])
        ln2_sd = sb("ln2_sd", [128, N])
        ln2_n = sb("ln2_n", [128, N])
        h2 = two("h2", [128, N])
        rt_h = sb("rt_h", [ROUTER + 1, N])
        rt_lg = sb("rt_lg", [128, TG, EXPERTS + 1])
        rt_top = sb("rt_top", [128, TG, 8])
        rt_ix = sb("rt_ix", [128, TG, 8], U32)
        rt_ixf = sb("rt_ixf", [128, TG, 8])
        rt_d = sb("rt_d", [128, TG, EXPERTS + 1])
        rt_th = sb("rt_th", [128, TG, EXPERTS + 1])
        rt_num = sb("rt_num", [128, TG, EXPERTS + 1])
        rt_den = sb("rt_den", [128, TG, EXPERTS + 1])
        rt_inv = sb("rt_inv", [128, TG, EXPERTS + 1])
        rt_exp = sb("rt_exp", [128, TG, EXPERTS + 1])
        rt_sum = sb("rt_sum", [128, TG])
        rt_sinv = sb("rt_sinv", [128, TG])
        rt_gap = sb("rt_gap", [128, TG])
        rt_u = sb("rt_u", [128, TG])
        rt_ut = sb("rt_ut", [128, TG])
        rt_w1 = sb("rt_w1", [128, TG])
        rt_w2 = sb("rt_w2", [128, TG])
        rt_a = sb("rt_a", [128, TG, EXPERTS])
        rt_w = two("rt_wgt", [128, TG, EXPERTS])
        rt_b = sb("rt_b", [128, TG, EXPERTS])
        rt_wt = two("rt_wt", [EXPERTS + 1, N])
        hid = two("hid", [128, HB, N])
        acc = [two(f"acc{p}_", [128, TG * 128]) for p in range(2)]
        y_out = two("y_out", [128, N])

        bank = [ctx.enter_context(nc.psum_tensor(f"bank{i}", [128, 512], F32)) for i in range(8)]
        ps_hid = [bank[m // 2][:, (m % 2) * N:(m % 2) * N + N] for m in range(HB)]
        ps_y = [bank[2][:, 0:N], bank[3][:, 0:N]]
        ps_proj = [bank[4 + (m // 2) % 2][:, (m % 2) * N:(m % 2) * N + N] for m in range(7)]
        ps_out = bank[4][:, 0:N]
        ps_ln1, ps_ln2, ps_gn = bank[6][:, 0:N], bank[6][:, N:2 * N], bank[6][:, 0:N]
        ps_sum, ps_rt = bank[7], bank[7][:, 0:N]

        S = {}

        def ev(name):
            if name not in S:
                S[name] = sem(name)
            return S[name]

        s_names = """w_loaded x_loaded0 x_loaded1 xr_loaded0 xr_loaded1 sent0 sent1 vsent0 vsent1 o_back0 o_back1 stored0 stored1
            const pconst cond_silu mod_mm mod_ready
            ln1_mean ln1_center ln1_square ln1_var ln1_sqrt ln1_recip ln1_norm h1_ready shift_ready mix_ready proj_done
            w_tanh_done d_ready ab_copied ab_squared r_ready k_ready v_ready g_tanh_done g_ready norm_sum norm_sqrt
            norm_max norm_recip a_ready b_ready
            q_copied kb_copied pull_mul pull_sum pull_rank pull_dec pull_add push_mul push_sum push_rank push_dec push_add
            score_out lam_mul packed ar_r x_packed
            u_first u_mul_done u_add gv_done dots z_done outer state_ready state_copied s_terms o_reduced
            gn_mean gn_center gn_square gn_var gn_sqrt gn_recip gn_norm gn_affine gn_gated wo_done x_biased x2_ready
            ln2_mean ln2_center ln2_square ln2_var ln2_sqrt ln2_recip ln2_norm h2_ready
            rt_hid rt_relu rt_logit rt_copied rt_topped rt_indexed rt_ix_f rt_gap1 rt_tanh1 rt_n rt_dn rt_i rt_e rt_s rt_si
            rt_gapped rt_uu rt_tanh2 rt_weights rt_wa rt_wb rt_ready rt_turned rt_wt_ready
            hid_mm hid_act y_mm y_acc out_turned out_ready""".split()
        for n_ in s_names:
            ev(n_)

        def wait(eng, sem_, value):
            if isinstance(value, int):
                if value > 0:
                    eng.wait_ge(sem_, value)
                return
            eng.wait_ge(sem_, value)
            if eng.engine in (nc.gpsimd.engine, nc.sync.engine):
                eng.sem_inc(ev("passed"))

        def bt(ap):
            return ap.rearrange("p (b t) -> p b t", b=BATCH)

        def bc(ap, shape):
            return ap.to_broadcast(shape)

        def per_chunk(ap, j, n):
            return bc(ap[:, :, j:j + 1], [128, CB, n])

        def per_chunk2(ap, j, n):
            return bc(ap[:, :, j:j + 1].rearrange("p (o c) l -> p o c l", o=1), [128, 2, CB, n])

        def cols(ap, *dims):
            m = int(np.prod(dims))
            v = ap[:, 0:m]
            if len(dims) == 2:
                return v.rearrange("p (a b) -> p a b", a=dims[0])
            return v.rearrange("p (a b c) -> p a b c", a=dims[0], b=dims[1])

        def sent_view(at, width):
            return send[:, :, at:at + C * width].rearrange("p b (c w) -> p b c w", w=width)

        def bcl(ap, lo, hi):
            return ap[:, :, lo:hi].rearrange("p (b c) l -> p b c l", b=BATCH)

        def op_view(par, at, width, lo, hi):
            return ops[par][:, :, at:at + C * width].rearrange("p k (c w) -> p k c w", w=width)[:, :, :, lo:hi]

        PULLS = list(range(L - 2, -1, -1))
        PUSHES = list(range(1, L))
        block = ctx.enter_context(nc.Block())

        @block.sync
        def _(sp):
            for dst, src in ((cond[:, :], cond_d[:, :]), (wmod[:, :], wmod_d[:, :]), (vec[:, :], vec_d[:, :])):
                sp.dma_start(dst, src).then_inc(ev("w_loaded"), 16)
            loaded_rest = [False]

            def work(at):
                t = at(LAG_PROJ)
                if t is not None:
                    wait(sp, ev("ln1_center"), t.t - 1)
                    sp.dma_start(x_in[t.par][:, :], x_d[:, bass.ds(t.t * N, N)]).then_inc(ev(f"x_loaded{t.par}"), 16)
                if not loaded_rest[0]:
                    loaded_rest[0] = True
                    for dst, src in ((w_proj[:, :, :], w_d[:, :, :]), (wr1[:, :], wr1_d[:, :]), (wr2[:, :], wr2_d[:, :]),
                                     (be2[:, :], be2_d[:, :]), (w1[:, :, :], w1_d[:, :, :]), (w2[:, :, :, :], w2_d[:, :, :, :])):
                        sp.dma_start(dst, src).then_inc(ev("rest_loaded"), 16)
                t = at(LAG_GN)
                if t is not None:
                    wait(sp, ev("x_biased"), (t.t - 1) * BATCH)
                    sp.dma_start(x_res[t.par][:, :], x_d[:, bass.ds(t.t * N, N)]).then_inc(ev(f"xr_loaded{t.par}"), 16)
                    wait(sp, ev("o_reduced"), (t.t + 1) * L)
                    wait(sp, ev("gn_center"), t.t - 1)
                    for b in range(BATCH):
                        for hf in range(2):
                            p0 = 32 * b + 16 * hf
                            sp.dma_start(o_ch[t.par][64 * hf:64 * hf + 64, b * STEPS:(b + 1) * STEPS], o_scan[t.par][p0:p0 + 16, :, :]).then_inc(ev(f"o_back{t.par}"), 16)
                t = at(LAG_OUT)
                if t is not None:
                    wait(sp, ev("out_ready"), (t.t + 1) * BATCH)
                    sp.dma_start(out_d[:, bass.ds(t.t * N, N)], y_out[t.par][:, :]).then_inc(ev(f"stored{t.par}"), 16)
                t = at(LAG_CHUNK)
                if t is not None:
                    wait(sp, ev("v_ready"), t.t + 1)
                    wait(sp, ev("gv_done"), (t.t - 1) * (L - 1))
                    for b in range(BATCH):
                        for hf in range(2):
                            p0 = 32 * b + 16 * hf
                            sp.dma_start(vals[t.par][p0:p0 + 16, :, :], v_send[t.par][64 * hf:64 * hf + 64, b, :]).then_inc(ev(f"vsent{t.par}"), 16)
                    wait(sp, ev("packed"), (t.t + 1) * 4)
                    wait(sp, ev("x_packed"), t.t + 1)
                    wait(sp, ev("score_out"), (t.t + 1) * (L - 1))
                    wait(sp, ev("outer"), (t.t - 1) * C)
                    wait(sp, ev("s_terms"), (t.t - 1) * L)
                    for b in range(BATCH):
                        for hf in range(2):
                            p0 = 32 * b + 16 * hf
                            sp.dma_start(ops[t.par][p0:p0 + 16, :, :],
                                         send[:, b, :]).then_inc(ev(f"sent{t.par}"), 16)

            run_tiles(sp, work)
            sp.wait_ge(ev("stored0"), 16 * (TILES // 2))
            sp.wait_ge(ev("stored1"), 16 * (TILES // 2))

        @block.tensor
        def _(pe):
            pe.wait_ge(ev("w_loaded"), 16 * 3)
            pe.wait_ge(ev("rest_loaded"), 16 * 6)
            pe.wait_ge(ev("pconst"), 8)
            pe.wait_ge(ev("cond_silu"), 1)
            for m in range(6):
                last = pe.matmul(ps_rt[:, m * BATCH:(m + 1) * BATCH], wmod[:, m * 128:(m + 1) * 128], cond_act[:, :],
                                 start=True, stop=True)
            last.then_inc(ev("mod_mm"), 1)

            def stats(ps, src, ones, name):
                pe.matmul(ps, ones, src, start=True, stop=True).then_inc(ev(name), 1)

            def hidden(t, e):
                if e == 0:
                    wait(pe, ev("h2_ready"), (t.t + 1) * BATCH)
                for m in range(HB):
                    if m % 2 == 0:
                        wait(pe, ev("hid_act"), (t.t * (EXPERTS + 1) + e - 1) * HB + m + 2)
                    last = pe.matmul(ps_hid[m], w1[:, e, m * 128:(m + 1) * 128], h2[t.par][:, :], start=True, stop=True)
                    if m % 2 == 1:
                        last.then_inc(ev("hid_mm"), 1)

            def down(t, e):
                last_e = EXPERTS
                wait(pe, ev("y_acc"), (t.t * (EXPERTS + 1) + e - 1) * TG)
                for g in range(TG):
                    out = ps_y[(t.par + e) % 2][:, g * 128:(g + 1) * 128]
                    for m in range(HB):
                        if g == 0:
                            wait(pe, ev("hid_act"), (t.t * (EXPERTS + 1) + e) * HB + m + 1)
                        last = pe.matmul(out, hid[(t.par + e) % 2][:, m, g * 128:(g + 1) * 128], w2[:, e, m, :],
                                         start=(m == 0), stop=(m == HB - 1 and e != last_e))
                    if e == last_e:
                        wait(pe, ev("rt_wt_ready"), t.t + 1)
                        last = pe.matmul(out, rt_wt[t.par][:, g * 128:(g + 1) * 128], be2[:, :], start=False, stop=True)
                last.then_inc(ev("y_mm"), 1)

            def work(at):
                A, B, G, N2, E, O = (at(x) for x in (LAG_PROJ, LAG_CHUNK, LAG_GN, LAG_LN2, LAG_FFN, LAG_OUT))
                for s in range(SLOTS):
                    if E is not None:
                        if s == 0:
                            hidden(E, 0)
                        if s % 2 == 1 and (s + 1) // 2 <= EXPERTS:
                            hidden(E, (s + 1) // 2)
                        if s % 2 == 0 and 2 <= s:
                            down(E, (s - 2) // 2)
                    if O is not None and s == 1:
                        wait(pe, ev("y_acc"), (O.t + 1) * (EXPERTS + 1) * TG)
                        wait(pe, ev("v_ready"), at.before(LAG_PROJ))
                        for g in range(TG):
                            last = pe.matmul(ps_out[:, g * 128:(g + 1) * 128],
                                             acc[O.par][EXPERTS % 2][:, g * 128:(g + 1) * 128], ident[:, :],
                                             start=True, stop=True)
                        last.then_inc(ev("out_turned"), 1)
                    if s == 0:
                        wait(pe, ev("x2_ready"), at.before(LAG_GN) * BATCH)
                        wait(pe, ev("ln1_sqrt"), at.before(LAG_PROJ))
                        wait(pe, ev("ln2_sqrt"), at.before(LAG_LN2))
                        if A is not None:
                            wait(pe, ev(f"x_loaded{A.par}"), 16 * (A.half + 1))
                            stats(ps_ln1, x_in[A.par][:, :], ones_ch[:, :], "ln1_mean")
                        if N2 is not None:
                            wait(pe, ev("x2_ready"), (N2.t + 1) * BATCH)
                            stats(ps_ln2, x2[N2.par][:, :], ones_ch[:, :], "ln2_mean")
                    if s == 2:
                        wait(pe, ev("ln1_center"), at.through(LAG_PROJ))
                        wait(pe, ev("ln2_center"), at.through(LAG_LN2))
                        if A is not None:
                            wait(pe, ev("ln1_square"), A.t + 1)
                            stats(ps_ln1, ln1_sq[:, :], ones_ch[:, :], "ln1_var")
                        if N2 is not None:
                            wait(pe, ev("ln2_square"), N2.t + 1)
                            stats(ps_ln2, ln2_sq[:, :], ones_ch[:, :], "ln2_var")
                    if G is not None:
                        if s == 8:
                            wait(pe, ev(f"o_back{G.par}"), 16 * 8 * (G.half + 1))
                            wait(pe, ev("ln1_sqrt"), at.through(LAG_PROJ))
                            wait(pe, ev("ln2_sqrt"), at.through(LAG_LN2))
                            wait(pe, ev("x2_ready"), G.t * BATCH)
                            stats(ps_gn, o_ch[G.par][:, :], mean_hd[:, :], "gn_mean")
                        if s == 11:
                            wait(pe, ev("gn_square"), G.t + 1)
                            wait(pe, ev("gn_center"), G.t + 1)
                            stats(ps_gn, gn_sq[:, :], mean_hd[:, :], "gn_var")
                        if s == 17:
                            wait(pe, ev("gn_gated"), G.t + 1)
                            wait(pe, ev("gn_sqrt"), G.t + 1)
                            stats(ps_gn, gn_g[:, :], w_proj[:, 7, :], "wo_done")
                    if A is not None and 8 <= s <= 11:
                        for m in ((0, 1), (2, 3), (4, 5), (6,))[s - 8]:
                            wait(pe, ev("mix_ready"), A.t * 7 + m + 1)
                            if m == 0:
                                wait(pe, ev("v_ready"), A.t)
                                wait(pe, ev("out_ready"), at.through(LAG_OUT) * BATCH)
                            if m == 2:
                                wait(pe, ev("g_tanh_done"), A.t)
                            if m == 4:
                                wait(pe, ev("ab_squared"), A.t * 2 + 1)
                            if m == 6:
                                wait(pe, ev("r_ready"), A.t + 1)
                            last = pe.matmul(ps_proj[m], w_proj[:, m, :], mixed[:, m, :], start=True, stop=True)
                        last.then_inc(ev("proj_done"), 1)
                    if B is not None:
                        for n_, j in enumerate(PULLS):
                            if s == 1 + 2 * n_:
                                m = 2 * CB * (L - 1 - j)
                                wait(pe, ev("pull_mul"), B.t * (L - 1) + n_ + 1)
                                if n_ == 0:
                                    wait(pe, ev("norm_sqrt"), at.before(LAG_PROJ))
                                    wait(pe, ev("rt_wt_ready"), at.before(LAG_LN2))
                                wait(pe, ev("score_out"), B.t * (L - 1) + n_)
                                pe.matmul(ps_sum[:, 0:m], ones_hd[:, :], q_mul[:, 0:m], start=True, stop=True)\
                                    .then_inc(ev("pull_sum"), 1)
                        for n_, j in enumerate(PUSHES):
                            if s == 2 + 2 * n_:
                                m = 2 * CB * j
                                wait(pe, ev("push_mul"), B.t * (L - 1) + n_ + 1)
                                wait(pe, ev("pull_rank"), B.t * (L - 1) + n_ + 1)
                                pe.matmul(ps_sum[:, 0:m], ones_hd[:, :], k_mul[:, 0:m], start=True, stop=True)\
                                    .then_inc(ev("push_sum"), 1)
                    if N2 is not None:
                        if s == 8:
                            wait(pe, ev("h2_ready"), (N2.t + 1) * BATCH)
                            wait(pe, ev("score_out"), at.through(LAG_CHUNK) * (L - 1))
                            wait(pe, ev("norm_sqrt"), at.before(LAG_PROJ))
                            wait(pe, ev("rt_wt_ready"), N2.t)
                            pe.matmul(ps_rt[0:ROUTER, :], wr1[:, :], h2[N2.par][:, :], start=True, stop=True)\
                                .then_inc(ev("rt_hid"), 1)
                        if s == 10:
                            wait(pe, ev("rt_relu"), N2.t + 1)
                            for g in range(TG):
                                last = pe.matmul(ps_rt[:, g * EXPERTS:(g + 1) * EXPERTS], rt_h[:, g * 128:(g + 1) * 128],
                                                 wr2[:, :], start=True, stop=True)
                            last.then_inc(ev("rt_logit"), 1)
                    if A is not None and s == 13:
                        wait(pe, ev("ab_squared"), (A.t + 1) * 2)
                        wait(pe, ev("score_out"), at.through(LAG_CHUNK) * (L - 1))
                        wait(pe, ev("rt_copied"), at.through(LAG_LN2))
                        wait(pe, ev("rt_wt_ready"), at.before(LAG_LN2))
                        pe.matmul(ps_sum[:, :], ones_hd[:, :], ab_sq[:, :, :].rearrange("p a n -> p (a n)"),
                                  start=True, stop=True).then_inc(ev("norm_sum"), 1)
                    if N2 is not None and s == 16:
                        wait(pe, ev("rt_ready"), N2.t + 1)
                        wait(pe, ev("norm_sqrt"), at.through(LAG_PROJ))
                        for g in range(TG):
                            last = pe.matmul(ps_rt[0:EXPERTS, g * 128:(g + 1) * 128], rt_w[N2.par][:, g, :], ident[:, :],
                                             start=True, stop=True)
                        last.then_inc(ev("rt_turned"), 1)

            run_tiles(pe, work)

        @block.scalar
        def _(act):
            act.wait_ge(ev("w_loaded"), 16 * 3)
            act.activation(cond_act[:, :], cond[:, :], ACT.Silu).then_inc(ev("cond_silu"), 1)
            act.wait_ge(ev("mod_mm"), 1)
            act.activation(mod[:, :, :].rearrange("p m b -> p (m b)"), ps_rt[:, 0:6 * BATCH], ACT.Copy).then_inc(ev("const"), 1)
            act.wait_ge(ev("const"), 1)
            for n_, m in enumerate((2, 5)):
                act.activation(mod_abs[:, n_, :], mod[:, m, :], ACT.Abs).then_inc(ev("const"), 1)
            act.wait_ge(ev("pconst"), 8)

            def work(at):
                A, B, G, N2, E = (at(x) for x in (LAG_PROJ, LAG_CHUNK, LAG_GN, LAG_LN2, LAG_FFN))

                def silu(e):
                    for m in range(HB):
                        if m % 2 == 0:
                            wait(act, ev("hid_mm"), (E.t * (EXPERTS + 1) + e) * 2 + m // 2 + 1)
                        wait(act, ev("y_mm"), E.t * (EXPERTS + 1) + e - 1)
                        act.activation(hid[(E.par + e) % 2][:, m, :], ps_hid[m], ACT.Silu,
                                       bias=vec[:, BE1 + e * HB + m:BE1 + e * HB + m + 1]).then_inc(ev("hid_act"), 1)


                for s in range(SLOTS):
                    if E is not None:
                        if s == 0:
                            silu(0)
                        if s % 2 == 1 and (s + 1) // 2 <= EXPERTS:
                            silu((s + 1) // 2)
                    if N2 is not None:
                        if s == 9:
                            wait(act, ev("rt_hid"), N2.t + 1)
                            wait(act, ev("rt_logit"), N2.t)
                            act.activation(rt_h[0:ROUTER, :], ps_rt[0:ROUTER, :], ACT.Relu, bias=vec[0:ROUTER, BR1:BR1 + 1])\
                                .then_inc(ev("rt_relu"), 1)
                        if s == 12:
                            wait(act, ev("rt_gap1"), (N2.t + 1) * 2)
                            act.activation(rt_th[:, :, :], rt_d[:, :, :], ACT.Tanh, scale=0.5).then_inc(ev("rt_tanh1"), 1)
                        if s == 14:
                            wait(act, ev("rt_uu"), N2.t + 1)
                            act.activation(rt_ut[:, :], rt_u[:, :], ACT.Tanh, scale=0.25).then_inc(ev("rt_tanh2"), 1)
                        if s == 17:
                            wait(act, ev("rt_turned"), N2.t + 1)
                            wait(act, ev("y_mm"), (N2.t - 1) * (EXPERTS + 1))
                            act.activation(rt_wt[N2.par][0:EXPERTS, :], ps_rt[0:EXPERTS, :], ACT.Copy).then_inc(ev("rt_wt_ready"), 1)
                    if s == 2:
                        if A is not None:
                            wait(act, ev("ln1_center"), A.t + 1)
                            act.activation(ln1_sq[:, :], ln1_c[:, :], ACT.Square).then_inc(ev("ln1_square"), 1)
                        if N2 is not None:
                            wait(act, ev("ln2_center"), N2.t + 1)
                            act.activation(ln2_sq[:, :], ln2_c[:, :], ACT.Square).then_inc(ev("ln2_square"), 1)
                    if s == 4:
                        wait(act, ev("ln1_var"), at.through(LAG_PROJ))
                        wait(act, ev("ln2_var"), at.through(LAG_LN2))
                        if A is not None:
                            act.activation(ln1_sd[:, :], ps_ln1, ACT.Sqrt, bias=eps_ln[:, 0:1]).then_inc(ev("ln1_sqrt"), 1)
                        if N2 is not None:
                            act.activation(ln2_sd[:, :], ps_ln2, ACT.Sqrt, bias=eps_ln[:, 0:1]).then_inc(ev("ln2_sqrt"), 1)
                    if A is not None and 9 <= s <= 12:
                        for m in ((0, 1), (2, 3), (4, 5), (6,))[s - 9]:
                            what = PROJ[m]
                            wait(act, ev("proj_done"), A.t * 4 + m // 2 + 1)
                            if what == "w":
                                wait(act, ev("d_ready"), A.t)
                                act.activation(w_tanh[:, :], ps_proj[m], ACT.Tanh, scale=-0.5).then_inc(ev("w_tanh_done"), 1)
                            elif what in "ab":
                                wait(act, ev("a_ready" if what == "a" else "b_ready"), A.t)
                                wait(act, ev("norm_sum"), A.t)
                                act.activation(ab_raw[:, m - 1, :], ps_proj[m], ACT.Copy).then_inc(ev("ab_copied"), 1)
                                act.activation(ab_sq[:, m - 1, :], ps_proj[m], ACT.Square).then_inc(ev("ab_squared"), 1)
                            elif what == "r":
                                wait(act, ev("x_packed"), A.t - 1)
                                wait(act, ev("ar_r"), A.t - 1)
                                act.activation(r_raw[A.par][:, :, :].rearrange("p c l -> p (c l)"), ps_proj[m], ACT.Copy)\
                                    .then_inc(ev("r_ready"), 1)
                            elif what == "k":
                                wait(act, ev("kb_copied"), (A.t - 1) * 2)
                                act.activation(k_raw[A.par][:, :, :].rearrange("p c l -> p (c l)"), ps_proj[m], ACT.Tanh)\
                                    .then_inc(ev("k_ready"), 1)
                            elif what == "v":
                                wait(act, ev(f"vsent{A.par}"), 16 * 8 * A.half)
                                act.activation(v_send[A.par][:, :, :], bt(ps_proj[m]), ACT.Copy).then_inc(ev("v_ready"), 1)
                            else:
                                wait(act, ev("g_ready"), A.t)
                                act.activation(g_tanh[:, :], ps_proj[m], ACT.Tanh, scale=0.5).then_inc(ev("g_tanh_done"), 1)
                    if B is not None:
                        for n_, j in enumerate(PUSHES):
                            if s == 2 + 2 * n_:
                                wait(act, ev("push_sum"), B.t * (L - 1) + n_ + 1)
                                wait(act, ev("push_rank"), B.t * (L - 1) + n_ + 1)
                                if n_ == 0:
                                    wait(act, ev(f"sent{1 - B.par}"), 16 * 8 * (B.half + B.par))
                                src = ps_sum[:, CB * j:2 * CB * j].rearrange("p (b c s) -> p b c s", b=BATCH, s=j)
                                act.activation(sent_view(G0, NG)[:, :, :, j * (j - 1) // 2:j * (j + 1) // 2], src, ACT.Copy)\
                                    .then_inc(ev("score_out"), 1)
                    if G is not None and s == 10:
                        wait(act, ev("gn_center"), G.t + 1)
                        act.activation(gn_sq[:, :], gn_c[:, :], ACT.Square).then_inc(ev("gn_square"), 1)
                    if s == 14:
                        if G is not None:
                            wait(act, ev("gn_var"), G.t + 1)
                            act.activation(gn_sd[:, :], ps_gn, ACT.Sqrt, bias=eps_gn[:, 0:1]).then_inc(ev("gn_sqrt"), 1)
                        if A is not None:
                            wait(act, ev("norm_sum"), A.t + 1)
                            wait(act, ev("b_ready"), A.t)
                            act.activation(ab_norm[:, :], ps_sum[:, :], ACT.Sqrt).then_inc(ev("norm_sqrt"), 1)

            run_tiles(act, work)

        @block.gpsimd
        def _(pool):
            pool.memset(ones_ch[:, :], 1.0 / D).then_inc(ev("pconst"), 1)
            pool.memset(ones_hd[:, :], 1.0)
            pool.memset(mean_hd[:, :], 1.0 / K)
            pool.memset(band[:, :], 1.0 / K)
            pool.memset(ident[:, :], 0.0)
            pool.memset(rt_h[:, :], 1.0)
            pool.memset(rt_wt[0][:, :], 1.0)
            pool.memset(rt_wt[1][:, :], 1.0)
            pool.memset(eps_ln[:, :], LN_EPS).then_inc(ev("pconst"), 1)
            pool.memset(eps_gn[:, :], GN_EPS).then_inc(ev("pconst"), 1)
            pool.memset(o_terms[:, :, :], 0.0)
            for i in range(2):
                pool.memset(h1[i][:, :, :], 0.0)
                pool.memset(state[i][:, :, :], 0.0)
            pool.iota(iota_i[:, :], pattern=[[1, EXPERTS]], base=0, channel_multiplier=0).then_inc(ev("pconst"), 1)
            pool.wait_ge(ev("pconst"), 4)
            pool.tensor_copy(iota_f[:, :], iota_i[:, :]).then_inc(ev("pconst"), 1)
            groups = [(ones_hd[:, :].rearrange("p (h k) -> p h k", k=K), [[K, HEADS], [0, K]], 0, K)]
            for f, m in enumerate((mean_hd, band)):
                groups.append((m[:, :].rearrange("p (f h v) -> p f h v", f=2, v=VH), [[0, 2], [VH, HEADS], [0, VH]], 64 * f, VH))
            for v, pattern, at0, size in groups:
                pool.affine_select(out=v, in_=v, compare_op=ALU.is_ge, fill=0.0, base=-at0,
                                   pattern=[[-st, n_] for st, n_ in pattern], channel_multiplier=1).then_inc(ev("band_low"), 1)
            pool.wait_ge(ev("band_low"), 3)
            for v, pattern, at0, size in groups:
                pool.affine_select(out=v, in_=v, compare_op=ALU.is_ge, fill=0.0, base=at0 + size - 1,
                                   pattern=pattern, channel_multiplier=-1).then_inc(ev("band_high"), 1)
            pool.wait_ge(ev("band_high"), 3)
            pool.tensor_tensor(mean_hd[:, :], mean_hd[:, :], band[:, :], ALU.add).then_inc(ev("pconst"), 2)
            pool.affine_select(out=ident[:, :], in_=ident[:, :], compare_op=ALU.not_equal, fill=1.0, base=0,
                               pattern=[[-1, 128]], channel_multiplier=1).then_inc(ev("pconst"), 1)

            pool.wait_ge(ev("pconst"), 8)
            pool.wait_ge(ev("mod_ready"), 1)

            def affine(dst, src, scale, shift_, name):
                for b in range(BATCH):
                    pool.tensor_scalar(dst(b), src[:, b * STEPS:(b + 1) * STEPS], scale[:, b:b + 1], shift_[:, b:b + 1],
                                       ALU.mult, ALU.add).then_inc(ev(name), 1)

            def work(at):
                A, B, R, G, N2 = (at(x) for x in (LAG_PROJ, LAG_CHUNK, LAG_SCAN, LAG_GN, LAG_LN2))
                for s in range(SLOTS):
                    if R is not None:
                        if s == 0:
                            wait(pool, ev(f"sent{R.par}"), 16 * 8 * (R.half + 1))
                            wait(pool, ev(f"vsent{R.par}"), 16 * 8 * (R.half + 1))
                            wait(pool, ev("state_ready"), R.t * C)
                        if s < 2:
                            for j in range(s * L // 2, (s + 1) * L // 2):
                                slot = terms[:, :, L + 1, :].rearrange("p c (v k) -> p c v k", v=VH)
                                val = bc(vals[R.par][:, :, :].rearrange("p v (c l) -> p c v l", l=L)[:, :, :, j:j + 1], [128, C, VH, K])
                                key = bc(op_view(R.par, K0, L, j, j + 1).rearrange("p k c o -> p c o k"), [128, C, VH, K])
                                if j == 0:
                                    pool.tensor_tensor(slot, val, key, ALU.mult).then_inc(ev("u_first"), 1)
                                    wait(pool, ev("u_first"), R.t + 1)
                                else:
                                    if j == 1:
                                        wait(pool, ev("u_add"), R.t * (L - 1))
                                    else:
                                        wait(pool, ev("u_add"), R.t * (L - 1) + j - 1)
                                    pool.tensor_tensor(u_mul[:, :, :, :], val, key, ALU.mult).then_inc(ev("u_mul_done"), 1)
                                    wait(pool, ev("u_mul_done"), R.t * (L - 1) + j)
                                    pool.tensor_tensor(slot, slot, u_mul[:, :, :, :], ALU.add).then_inc(ev("u_add"), 1)
                        if s == 10:
                            wait(pool, ev("g_ready"), R.t + 1)
                            wait(pool, ev("gn_gated"), R.t - 1)
                            pool.tensor_copy(gate_late[R.par][:, :], gate[R.par][:, :]).then_inc(ev("gate_copied"), 1)
                        if s == 12:
                            wait(pool, ev("o_reduced"), R.t * L)
                            ot = o_terms[:, :, :].rearrange("p (c j v) x -> p c j v x", c=C, j=L)
                            for c_ in range(L - 1):
                                for j in range(c_, L - 1):
                                    g_at = j * (j + 1) // 2 + c_
                                    sc = bc(op_view(R.par, G0, NG, g_at, g_at + 1)[:, 0, :, :], [128, C, VH])
                                    vv = vals[R.par][:, :, :].rearrange("p v (c l) -> p c v l", l=L)[:, :, :, c_]
                                    last = pool.tensor_tensor(ot[:, :, j, :, K + c_], sc, vv, ALU.mult)
                                last.then_inc(ev("gv_done"), 1)
                    if G is not None and s in (2, 3):
                        if s == 2:
                            wait(pool, ev("state_ready"), (G.t + 1) * C)
                            wait(pool, ev("s_terms"), G.t * L)
                            pool.tensor_copy(state[G.par][:, 0, :], state[1 - G.par][:, C, :]).then_inc(ev("state_copied"), 1)
                            wait(pool, ev("state_copied"), G.t + 1)
                            wait(pool, ev("o_reduced"), G.t * L)
                        ot = o_terms[:, :, :].rearrange("p (c j v) x -> p c j v x", c=C, j=L)
                        for j in range((s - 2) * L // 2, (s - 1) * L // 2):
                            c0 = 1 if j == L - 1 else 0
                            st = state[G.par][:, c0:c0 + C, :].rearrange("p c (v k) -> p c v k", v=VH)
                            xv = bc(op_view(G.par, X0, L, j, j + 1).rearrange("p k c o -> p c o k"), [128, C, VH, K])
                            pool.tensor_tensor(ot[:, :, j, :, 0:K], st, xv, ALU.mult).then_inc(ev("s_terms"), 1)
                    if A is not None:
                        if s == 6:
                            wait(pool, ev("ln1_norm"), A.t + 1)
                            wait(pool, ev("mix_ready"), A.t * 7)
                            wait(pool, ev("shift_ready"), A.t)
                            affine(lambda b: h1[A.par][:, b, 1:STEPS + 1], ln1_n, mod[:, 1, :], mod[:, 0, :], "h1_ready")
                            if not (isinstance(A.t, int) and A.t == 0):
                                pool.tensor_copy(h1[A.par][:, :, 0:1], h1[1 - A.par][:, :, STEPS:STEPS + 1])\
                                    .then_inc(ev("h1_edge"), 1)
                                wait(pool, ev("h1_edge"), A.t)
                            wait(pool, ev("h1_ready"), (A.t + 1) * BATCH)
                            pool.tensor_tensor(shift[:, :, :], h1[A.par][:, :, 0:STEPS], h1[A.par][:, :, 1:STEPS + 1], ALU.subtract)\
                                .then_inc(ev("shift_ready"), 1)
                        if s == 11:
                            wait(pool, ev("w_tanh_done"), A.t + 1)
                            wait(pool, ev("pull_dec"), (A.t - 1) * (L - 1))
                            wait(pool, ev("lam_mul"), (A.t - 1) * L)
                            wait(pool, ev("push_dec"), (A.t - 1) * (L - 1))
                            pool.tensor_scalar(dec[A.par][:, :, :].rearrange("p c l -> p (c l)"), w_tanh[:, :], 0.5, 0.5,
                                               ALU.mult, ALU.add).then_inc(ev("d_ready"), 1)
                        if s == 13:
                            wait(pool, ev("g_tanh_done"), A.t + 1)
                            wait(pool, ev("gate_copied"), A.t - 1)
                            pool.tensor_scalar(gate[A.par][:, :], g_tanh[:, :], 0.5, 0.5, ALU.mult, ALU.add)\
                                .then_inc(ev("g_ready"), 1)
                            wait(pool, ev("r_ready"), A.t + 1)
                            wait(pool, ev("q_copied"), A.t - 1)
                            wait(pool, ev("push_mul"), (A.t - 1) * (L - 1))
                            pool.tensor_copy(ar[A.par][:, 1, :, 1:L], r_raw[A.par][:, :, 0:L - 1]).then_inc(ev("ar_r"), 1)
                    if B is not None:
                        par = B.par
                        if s == 0:
                            wait(pool, ev("a_ready"), B.t + 1)
                            wait(pool, ev("ar_r"), B.t + 1)
                            wait(pool, ev("packed"), B.t * 4)
                            pool.tensor_copy(q[:, :, :, 1:L], ar[par][:, :, :, 1:L]).then_inc(ev("q_copied"), 1)
                            wait(pool, ev("b_ready"), B.t + 1)
                            wait(pool, ev("k_ready"), B.t + 1)
                            pool.tensor_copy(kb[:, 0, :, :], k_raw[par][:, :, :]).then_inc(ev("kb_copied"), 1)
                            pool.tensor_copy(kb[:, 1, :, :], b_raw[par][:, :, :]).then_inc(ev("kb_copied"), 1)
                            wait(pool, ev("q_copied"), B.t + 1)
                            wait(pool, ev("kb_copied"), (B.t + 1) * 2)
                        for n_, j in enumerate(PULLS):
                            if s == 0 + 2 * n_:
                                w_ = L - 1 - j
                                if n_ > 0:
                                    wait(pool, ev("pull_add"), B.t * (L - 1) + n_)
                                if n_ == 0:
                                    wait(pool, ev("pull_sum"), B.t * (L - 1))
                                pool.tensor_tensor(cols(q_mul, 2, CB, w_), q[:, :, :, j + 1:L], per_chunk2(b_raw[par], j, w_), ALU.mult)\
                                    .then_inc(ev("pull_mul"), 1)
                                pool.tensor_tensor(cols(q_dec, 2, CB, w_), q[:, :, :, j + 1:L], per_chunk2(dec[par], j, w_), ALU.mult)\
                                    .then_inc(ev("pull_dec"), 1)
                        for n_, j in enumerate(PUSHES):
                            if s == 1 + 2 * n_:
                                if n_ > 0:
                                    wait(pool, ev("push_add"), B.t * (L - 1) + n_)
                                    wait(pool, ev("push_dec"), B.t * (L - 1) + n_)
                                else:
                                    wait(pool, ev("push_sum"), B.t * (L - 1))
                                pool.tensor_tensor(cols(k_mul, 2, CB, j),
                                                   bc(kb[:, 0:1, :, 0:j], [128, 2, CB, j]),
                                                   bc(ar[par][:, :, :, j:j + 1], [128, 2, CB, j]), ALU.mult)\
                                    .then_inc(ev("push_mul"), 1)
                                wait(pool, ev("push_mul"), B.t * (L - 1) + n_ + 1)
                                pool.tensor_tensor(kb[:, :, :, 0:j], kb[:, :, :, 0:j], per_chunk2(dec[par], j, j), ALU.mult)\
                                    .then_inc(ev("push_dec"), 1)
                                if j == 1:
                                    wait(pool, ev("lam_mul"), B.t * L)
                                src = dec[par][:, :, 0:1] if j == 1 else lam[:, :, j - 1:j]
                                if j > 1:
                                    wait(pool, ev("lam_mul"), B.t * L + j - 1)
                                pool.tensor_tensor(lam[:, :, j:j + 1], src, dec[par][:, :, j:j + 1], ALU.mult)\
                                    .then_inc(ev("lam_mul"), 1)
                        if s == 7:
                            wait(pool, ev(f"sent{1 - par}"), 16 * 8 * (B.half + par))
                            wait(pool, ev("lam_mul"), B.t * L + L - 1)
                            pool.tensor_copy(sent_view(Y0, L + 1)[:, :, :, 0:1], bcl(lam, L - 1, L)).then_inc(ev("lam_mul"), 1)
                            pool.tensor_copy(sent_view(X0, L)[:, :, :, L - 1:L], bcl(r_raw[par], L - 1, L)).then_inc(ev("x_packed"), 1)
                            pool.tensor_copy(sent_view(Y0, L + 1)[:, :, :, 1:2], bcl(ar[par][:, 0], 0, 1)).then_inc(ev("y0_packed"), 1)
                            wait(pool, ev("pull_add"), (B.t + 1) * (L - 1))
                            pool.tensor_copy(sent_view(Y0, L + 1)[:, :, :, 2:L + 1], bcl(q[:, 0], 1, L)).then_inc(ev("packed"), 1)
                            pool.tensor_copy(sent_view(X0, L)[:, :, :, 0:L - 1], bcl(q[:, 1], 1, L)).then_inc(ev("packed"), 1)
                            wait(pool, ev("push_add"), (B.t + 1) * (L - 1))
                            wait(pool, ev("push_dec"), (B.t + 1) * (L - 1))
                            pool.tensor_copy(sent_view(K0, L), bcl(kb[:, 0], 0, L)).then_inc(ev("packed"), 1)
                            pool.tensor_copy(sent_view(B0, L), bcl(kb[:, 1], 0, L)).then_inc(ev("packed"), 1)
                    if G is not None:
                        if s == 8:
                            wait(pool, ev(f"xr_loaded{G.par}"), 16 * (G.half + 1))
                            wait(pool, ev("x2_ready"), G.t * BATCH)
                            for b in range(BATCH):
                                pool.tensor_scalar(x_bias[:, b * STEPS:(b + 1) * STEPS], x_res[G.par][:, b * STEPS:(b + 1) * STEPS],
                                                   1.0, ga_bo[:, b:b + 1], ALU.mult, ALU.add).then_inc(ev("x_biased"), 1)
                        if s == 16:
                            wait(pool, ev("gn_norm"), G.t + 1)
                            wait(pool, ev("gn_gated"), G.t)
                            pool.tensor_scalar(gn_a[:, :], gn_n[:, :], vec[:, GNW:GNW + 1], vec[:, GNB:GNB + 1], ALU.mult, ALU.add)\
                                .then_inc(ev("gn_affine"), 1)
                            wait(pool, ev("gn_affine"), G.t + 1)
                            wait(pool, ev("gate_copied"), G.t + 1)
                            wait(pool, ev("wo_done"), G.t)
                            pool.tensor_tensor(gn_g[:, :], gn_a[:, :], gate_late[G.par][:, :], ALU.mult).then_inc(ev("gn_gated"), 1)
                    if N2 is not None and s == 4:
                        wait(pool, ev("x2_ready"), (N2.t + 1) * BATCH)
                        wait(pool, ev("out_ready"), (N2.t - 1) * BATCH)
                        pool.tensor_copy(x2_late[N2.par][:, :], x2[N2.par][:, :]).then_inc(ev("x2_saved"), 1)
                    if N2 is not None and s == 6:
                        wait(pool, ev("ln2_norm"), N2.t + 1)
                        wait(pool, ev("rt_hid"), N2.t - 1)
                        wait(pool, ev("hid_mm"), (N2.t - 1) * (EXPERTS + 1) * 2)
                        affine(lambda b: h2[N2.par][:, b * STEPS:(b + 1) * STEPS], ln2_n, mod[:, 4, :], mod[:, 3, :], "h2_ready")

            run_tiles(pool, work)

        @block.vector
        def _(dve):
            dve.wait_ge(ev("const"), 3)
            for m in (1, 4):
                dve.tensor_scalar(mod[:, m, :], mod[:, m, :], 1.0, None, ALU.add).then_inc(ev("mod_step"), 1)
            for n_, m in enumerate((2, 5)):
                dve.tensor_scalar(mod_sign[:, n_, :], mod[:, m, :], 0.0, 2.0, ALU.is_ge, ALU.mult).then_inc(ev("mod_step"), 1)
            dve.wait_ge(ev("mod_step"), 4)
            dve.tensor_scalar(mod_sign[:, :, :], mod_sign[:, :, :], -1.0, None, ALU.add).then_inc(ev("mod_step"), 1)
            dve.tensor_scalar(mod_abs[:, :, :], mod_abs[:, :, :], GATE_MIN, None, ALU.max).then_inc(ev("mod_step"), 1)
            dve.wait_ge(ev("mod_step"), 6)
            for n_, m in enumerate((2, 5)):
                dve.tensor_tensor(mod[:, m, :], mod_sign[:, n_, :], mod_abs[:, n_, :], ALU.mult).then_inc(ev("mod_step"), 1)
            dve.wait_ge(ev("mod_step"), 8)
            dve.wait_ge(ev("w_loaded"), 16 * 3)
            dve.tensor_scalar(ga_bo[:, :], mod[:, 2, :], vec[:, BO:BO + 1], None, ALU.mult).then_inc(ev("mod_ready"), 1)
            dve.wait_ge(ev("pconst"), 8)

            def norm(t, ps, src, c, sd, n_out, name, stage, consumed):
                if stage == 0:
                    wait(dve, ev(f"{name}_mean"), t.t + 1)
                    dve.tensor_tensor(c[:, :], src, ps, ALU.subtract).then_inc(ev(f"{name}_center"), 1)
                else:
                    wait(dve, ev(f"{name}_sqrt"), t.t + 1)
                    dve.reciprocal(sd[:, :], sd[:, :]).then_inc(ev(f"{name}_recip"), 1)
                    dve.wait_ge(ev(f"{name}_recip"), t.t + 1)
                    wait(dve, consumed[0], consumed[1])
                    dve.tensor_tensor(n_out[:, :], c[:, :], sd[:, :], ALU.mult).then_inc(ev(f"{name}_norm"), 1)

            def chunk(R, c):
                par, n_ = R.par, R.t * C + c
                before = state[1 - par][:, C, :] if c == 0 else state[par][:, c, :]
                wait(dve, ev("state_ready"), n_)
                if c == 0:
                    wait(dve, ev(f"sent{par}"), 16 * 8 * (R.half + 1))
                sv = bc(before.rearrange("p (o v k) -> p o v k", o=1, v=VH), [128, L + 1, VH, K])
                yv = bc(ops[par][:, :, Y0 + c * (L + 1):Y0 + (c + 1) * (L + 1)].rearrange("p k (j o) -> p j o k", o=1), [128, L + 1, VH, K])
                dve.tensor_tensor(terms[:, c, 0:L + 1, :].rearrange("p j (v k) -> p j v k", v=VH), sv, yv, ALU.mult)\
                    .then_inc(ev("dots"), 1)
                dve.wait_ge(ev("dots"), n_ + 1)
                dve.tensor_reduce(z[par][:, c, :], terms[:, c, 1:L + 1, :].rearrange("p j (v k) -> p (j v) k", v=VH), AX.X, ALU.add)\
                    .then_inc(ev("z_done"), 1)
                dve.wait_ge(ev("z_done"), n_ + 1)
                zv = bc(z[par][:, c, :].rearrange("p (j v o) -> p j v o", j=L, o=1), [128, L, VH, K])
                bv = bc(ops[par][:, :, B0 + c * L:B0 + (c + 1) * L].rearrange("p k (j o) -> p j o k", o=1), [128, L, VH, K])
                dve.tensor_tensor(terms[:, c, 1:L + 1, :].rearrange("p j (v k) -> p j v k", v=VH), zv, bv, ALU.mult)\
                    .then_inc(ev("outer"), 1)
                dve.wait_ge(ev("outer"), n_ + 1)
                if c == C - 1:
                    wait(dve, ev("state_copied"), R.t)
                if c == 0:
                    wait(dve, ev("u_add"), (R.t + 1) * (L - 1))
                    wait(dve, ev("s_terms"), (R.t - 1) * L)
                dve.tensor_reduce(state[par][:, c + 1, :], terms[:, c, :, :].rearrange("p s a -> p a s"), AX.X, ALU.add)\
                    .then_inc(ev("state_ready"), 1)

            def expert_out(E, e):
                n_ = E.t * (EXPERTS + 1) + e
                wait(dve, ev("y_mm"), n_ + 1)
                if e == 0:
                    wait(dve, ev("rt_ready"), E.t + 1)
                    wait(dve, ev("out_turned"), E.t - 1)
                else:
                    dve.wait_ge(ev("y_acc"), n_ * TG)
                for g in range(TG):
                    cs = slice(g * 128, (g + 1) * 128)
                    if e == 0:
                        dve.tensor_scalar(acc[E.par][0][:, cs], ps_y[E.par][:, cs], rt_w[E.par][:, g, 0:1], None, ALU.mult).then_inc(ev("y_acc"), 1)
                    elif e < EXPERTS:
                        dve.scalar_tensor_tensor(out=acc[E.par][e % 2][:, cs], in0=ps_y[(E.par + e) % 2][:, cs], scalar=rt_w[E.par][:, g, e:e + 1],
                                                 in1=acc[E.par][(e - 1) % 2][:, cs], op0=ALU.mult, op1=ALU.add).then_inc(ev("y_acc"), 1)
                    else:
                        dve.tensor_tensor(acc[E.par][e % 2][:, cs], ps_y[(E.par + e) % 2][:, cs], acc[E.par][(e - 1) % 2][:, cs], ALU.add)\
                            .then_inc(ev("y_acc"), 1)

            def work(at):
                A, B, R, G, N2, E, O = (at(x) for x in (LAG_PROJ, LAG_CHUNK, LAG_SCAN, LAG_GN, LAG_LN2, LAG_FFN, LAG_OUT))
                for s in range(SLOTS):
                    if R is not None and 1 <= s <= 16:
                        for c in range((s - 1) * C // 16, s * C // 16):
                            chunk(R, c)
                    if s == 1:
                        wait(dve, ev("ln1_mean"), at.through(LAG_PROJ))
                        wait(dve, ev("ln2_mean"), at.through(LAG_LN2))
                    if A is not None:
                        if s == 1:
                            norm(A, ps_ln1, x_in[A.par][:, :], ln1_c, ln1_sd, ln1_n, "ln1", 0, None)
                        if s == 5:
                            norm(A, ps_ln1, None, ln1_c, ln1_sd, ln1_n, "ln1", 1, (ev("h1_ready"), A.t * BATCH))
                        if s in (7, 8):
                            wait(dve, ev("shift_ready"), A.t + 1)
                            for m in range(4) if s == 7 else range(4, 7):
                                wait(dve, ev("proj_done"), (A.t - 1) * 4 + m // 2 + 1)
                                dve.scalar_tensor_tensor(out=bt(mixed[:, m, :]), in0=shift[:, :, :],
                                                         scalar=vec[:, MIX0 + m:MIX0 + m + 1], in1=h1[A.par][:, :, 1:STEPS + 1],
                                                         op0=ALU.mult, op1=ALU.add).then_inc(ev("mix_ready"), 1)
                        if s == 16:
                            wait(dve, ev("norm_sqrt"), A.t + 1)
                            dve.tensor_scalar(ab_norm[:, :], ab_norm[:, :], NORM_EPS, None, ALU.max).then_inc(ev("norm_max"), 1)
                            dve.wait_ge(ev("norm_max"), A.t + 1)
                            dve.reciprocal(ab_norm[:, :], ab_norm[:, :]).then_inc(ev("norm_recip"), 1)
                        if s == 17:
                            dve.wait_ge(ev("norm_recip"), A.t + 1)
                            wait(dve, ev("ab_copied"), (A.t + 1) * 2)
                            wait(dve, ev("push_mul"), (A.t - 1) * (L - 1))
                            wait(dve, ev("y0_packed"), A.t - 1)
                            dve.tensor_tensor(ar[A.par][:, 0, :, :].rearrange("p c l -> p (c l)"), ab_raw[:, 0, :], ab_norm[:, 0:N], ALU.mult)\
                                .then_inc(ev("a_ready"), 1)
                            wait(dve, ev("pull_mul"), (A.t - 1) * (L - 1))
                            wait(dve, ev("kb_copied"), (A.t - 1) * 2)
                            dve.tensor_tensor(b_raw[A.par][:, :, :].rearrange("p c l -> p (c l)"), ab_raw[:, 1, :], ab_norm[:, N:2 * N], ALU.mult)\
                                .then_inc(ev("b_ready"), 1)
                    if N2 is not None:
                        if s == 1:
                            norm(N2, ps_ln2, x2[N2.par][:, :], ln2_c, ln2_sd, ln2_n, "ln2", 0, None)
                        if s == 5:
                            norm(N2, ps_ln2, None, ln2_c, ln2_sd, ln2_n, "ln2", 1, (ev("h2_ready"), N2.t * BATCH))
                    if B is not None:
                        par = B.par
                        for n_, j in enumerate(PULLS):
                            if s == 1 + 2 * n_:
                                w_ = L - 1 - j
                                wait(dve, ev("pull_sum"), B.t * (L - 1) + n_ + 1)
                                dve.tensor_tensor(cols(q_rank, 2, CB, w_), cols(ps_sum, 2, CB, w_), per_chunk2(ar[par][:, 0], j, w_), ALU.mult)\
                                    .then_inc(ev("pull_rank"), 1)
                                dve.wait_ge(ev("pull_rank"), B.t * (L - 1) + n_ + 1)
                                wait(dve, ev("pull_dec"), B.t * (L - 1) + n_ + 1)
                                dve.tensor_tensor(q[:, :, :, j + 1:L], cols(q_rank, 2, CB, w_), cols(q_dec, 2, CB, w_), ALU.add)\
                                    .then_inc(ev("pull_add"), 1)
                        for n_, j in enumerate(PUSHES):
                            if s == 2 + 2 * n_:
                                wait(dve, ev("push_sum"), B.t * (L - 1) + n_ + 1)
                                dve.tensor_tensor(cols(k_rank, CB, j), cols(ps_sum, CB, j), per_chunk(b_raw[par], j, j), ALU.mult)\
                                    .then_inc(ev("push_rank"), 1)
                                dve.wait_ge(ev("push_rank"), B.t * (L - 1) + n_ + 1)
                                wait(dve, ev("push_dec"), B.t * (L - 1) + n_ + 1)
                                dve.tensor_tensor(kb[:, 0, :, 0:j], kb[:, 0, :, 0:j], cols(k_rank, CB, j), ALU.add).then_inc(ev("push_add"), 1)
                    if G is not None:
                        if 3 <= s < 3 + L:
                            j = s - 3
                            wait(dve, ev("s_terms"), G.t * L + j + 1)
                            if j == 0:
                                wait(dve, ev("gv_done"), (G.t + 1) * (L - 1))
                                wait(dve, ev(f"o_back{G.par}"), 16 * 8 * G.half)
                            ot = o_terms[:, :, :].rearrange("p (c j v) x -> p j c v x", c=C, j=L)[:, j]
                            dst = o_scan[G.par][:, :, :].rearrange("p v (c j) -> p j c v", j=L)[:, j]
                            dve.tensor_reduce(dst, ot, AX.X, ALU.add).then_inc(ev("o_reduced"), 1)
                        if s == 9:
                            norm(G, ps_gn, o_ch[G.par][:, :], gn_c, gn_sd, gn_n, "gn", 0, None)
                        if s == 15:
                            norm(G, ps_gn, None, gn_c, gn_sd, gn_n, "gn", 1, (ev("gn_affine"), G.t))
                        if s == 18:
                            wait(dve, ev("wo_done"), G.t + 1)
                            wait(dve, ev("x_biased"), (G.t + 1) * BATCH)
                            wait(dve, ev("x2_saved"), G.t - 1)
                            wait(dve, ev("ln2_mean"), G.t - 1)
                            for b in range(BATCH):
                                cs = slice(b * STEPS, (b + 1) * STEPS)
                                dve.scalar_tensor_tensor(out=x2[G.par][:, cs], in0=ps_gn[:, cs], scalar=mod[:, 2, b:b + 1],
                                                         in1=x_bias[:, cs], op0=ALU.mult, op1=ALU.add).then_inc(ev("x2_ready"), 1)
                    if N2 is not None:
                        if s == 11:
                            wait(dve, ev("rt_logit"), N2.t + 1)
                            lg = ps_rt[:, 0:TG * EXPERTS].rearrange("p (g e) -> p g e", g=TG)
                            dve.tensor_copy(rt_lg[:, :, 0:EXPERTS], lg).then_inc(ev("rt_copied"), 1)
                            dve.wait_ge(ev("rt_copied"), N2.t + 1)
                            dve.sem_inc(ev("passed"))
                            for g in range(TG):
                                dve.max(rt_top[:, g, :], rt_lg[:, g, 0:EXPERTS]).then_inc(ev("rt_topped"), 1)
                            dve.wait_ge(ev("rt_topped"), (N2.t + 1) * TG)
                            dve.tensor_tensor(rt_d[:, :, 0:EXPERTS], rt_lg[:, :, 0:EXPERTS], bc(rt_top[:, :, 0:1], [128, TG, EXPERTS]),
                                              ALU.subtract).then_inc(ev("rt_gap1"), 1)
                            dve.tensor_tensor(rt_d[:, :, EXPERTS:EXPERTS + 1], rt_top[:, :, 1:2], rt_top[:, :, 0:1], ALU.subtract)\
                                .then_inc(ev("rt_gap1"), 1)
                            for g in range(TG):
                                dve.max_index(rt_ix[:, g, :], rt_top[:, g, :], rt_lg[:, g, 0:EXPERTS]).then_inc(ev("rt_indexed"), 1)
                            dve.wait_ge(ev("rt_indexed"), (N2.t + 1) * TG)
                            dve.tensor_copy(rt_ixf[:, :, :], rt_ix[:, :, :]).then_inc(ev("rt_ix_f"), 1)
                        if s == 13:
                            wait(dve, ev("rt_tanh1"), N2.t + 1)
                            dve.tensor_scalar(rt_den[:, :, :], rt_th[:, :, :], -1.0, 1.0, ALU.mult, ALU.add).then_inc(ev("rt_dn"), 1)
                            dve.tensor_scalar(rt_num[:, :, :], rt_th[:, :, :], 1.0, None, ALU.add).then_inc(ev("rt_n"), 1)
                            dve.wait_ge(ev("rt_dn"), N2.t + 1)
                            dve.reciprocal(rt_inv[:, :, :], rt_den[:, :, :]).then_inc(ev("rt_i"), 1)
                            dve.wait_ge(ev("rt_n"), N2.t + 1)
                            dve.wait_ge(ev("rt_i"), N2.t + 1)
                            dve.tensor_tensor(rt_exp[:, :, :], rt_num[:, :, :], rt_inv[:, :, :], ALU.mult).then_inc(ev("rt_e"), 1)
                            dve.wait_ge(ev("rt_e"), N2.t + 1)
                            dve.tensor_reduce(rt_sum[:, :], rt_exp[:, :, 0:EXPERTS], AX.X, ALU.add).then_inc(ev("rt_s"), 1)
                            dve.tensor_scalar(rt_gap[:, :], rt_exp[:, :, EXPERTS], -1.0, 1.0, ALU.mult, ALU.add).then_inc(ev("rt_gapped"), 1)
                            dve.wait_ge(ev("rt_s"), N2.t + 1)
                            dve.reciprocal(rt_sinv[:, :], rt_sum[:, :]).then_inc(ev("rt_si"), 1)
                            dve.wait_ge(ev("rt_si"), N2.t + 1)
                            dve.wait_ge(ev("rt_gapped"), N2.t + 1)
                            dve.tensor_tensor(rt_u[:, :], rt_gap[:, :], rt_sinv[:, :], ALU.mult).then_inc(ev("rt_uu"), 1)
                        if s == 15:
                            wait(dve, ev("rt_tanh2"), N2.t + 1)
                            dve.tensor_scalar(rt_w1[:, :], rt_ut[:, :], 0.5, 0.5, ALU.mult, ALU.add).then_inc(ev("rt_weights"), 1)
                            dve.tensor_scalar(rt_w2[:, :], rt_ut[:, :], -0.5, 0.5, ALU.mult, ALU.add).then_inc(ev("rt_weights"), 1)
                            dve.wait_ge(ev("rt_weights"), (N2.t + 1) * 2)
                            dve.wait_ge(ev("rt_ix_f"), N2.t + 1)
                            for g in range(TG):
                                dve.tensor_scalar(rt_a[:, g, :], iota_f[:, :], rt_ixf[:, g, 0:1], rt_w1[:, g:g + 1], ALU.is_equal, ALU.mult)\
                                    .then_inc(ev("rt_wa"), 1)
                                dve.tensor_scalar(rt_b[:, g, :], iota_f[:, :], rt_ixf[:, g, 1:2], rt_w2[:, g:g + 1], ALU.is_equal, ALU.mult)\
                                    .then_inc(ev("rt_wb"), 1)
                            dve.wait_ge(ev("rt_wa"), (N2.t + 1) * TG)
                            dve.wait_ge(ev("rt_wb"), (N2.t + 1) * TG)
                            dve.tensor_tensor(rt_w[N2.par][:, :, :], rt_a[:, :, :], rt_b[:, :, :], ALU.add).then_inc(ev("rt_ready"), 1)
                    if E is not None:
                        for e in range(EXPERTS + 1):
                            if s == 2 * e + 3:
                                expert_out(E, e)
                    if O is not None and s == 2:
                        wait(dve, ev("out_turned"), O.t + 1)
                        wait(dve, ev("x2_saved"), O.t + 1)
                        wait(dve, ev(f"stored{O.par}"), 16 * O.half)
                        for b in range(BATCH):
                            cs = slice(b * STEPS, (b + 1) * STEPS)
                            dve.scalar_tensor_tensor(out=y_out[O.par][:, cs], in0=ps_out[:, cs], scalar=mod[:, 5, b:b + 1],
                                                     in1=x2_late[O.par][:, cs], op0=ALU.mult, op1=ALU.add).then_inc(ev("out_ready"), 1)

            run_tiles(dve, work)


def kernel(**inputs):
    import concourse.bacc as bacc
    from concourse.bass_utils import run_bass_kernel_spmd

    def a(name):
        return np.asarray(inputs[name])

    attn = "L0_attn_"
    order = np.arange(D).reshape(HEADS, 2, VH).transpose(1, 0, 2).reshape(D)
    w_of = {p: a(attn + "W_" + p) for p in PROJ + ["o"]}
    w_of["v"], w_of["g"], w_of["o"] = w_of["v"][order], w_of["g"][order], w_of["o"][:, order]
    w = np.stack([w_of[p].T for p in PROJ + ["o"]], axis=1)
    vec = np.zeros((128, VECS), np.float32)
    for i, p in enumerate(PROJ):
        vec[:, MIX0 + i] = a(attn + "x_" + p)
    vec[:, BO], vec[:, GNW], vec[:, GNB] = a(attn + "b_o"), a(attn + "gn_w")[order], a(attn + "gn_b")[order]
    vec[:ROUTER, BR1] = a("L0_ffn_br1")
    be1 = np.concatenate([a("L0_ffn_be1"), a("L0_ffn_bs1")[None]])
    vec[:, BE1:] = be1.reshape((EXPERTS + 1) * HB, 128).T
    w1 = np.concatenate([a("L0_ffn_We1"), a("L0_ffn_Ws1")[None]]).transpose(1, 0, 2)
    w2 = np.concatenate([a("L0_ffn_We2"), a("L0_ffn_Ws2")[None]]).reshape(EXPERTS + 1, HB, 128, 128).transpose(2, 0, 1, 3)
    x = a("L0_attn_x").reshape(BATCH, TILES, STEPS, D).transpose(3, 1, 0, 2).reshape(D, TILES * N)
    arrays = {
        "x": x, "w": w, "vec": vec, "cond": a("L0_c").T, "wmod": a("L0_wmod"), "wr1": a("L0_ffn_Wr1"),
        "wr2": np.concatenate([a("L0_ffn_Wr2"), a("L0_ffn_br2")[None]]), "w1": w1, "w2": w2,
        "be2": np.concatenate([a("L0_ffn_be2"), a("L0_ffn_bs2")[None]]),
    }
    arrays = {"in_" + k: np.ascontiguousarray(v) for k, v in arrays.items()}
    nc = bacc.Bacc("TRN2", target_bir_lowering=False, num_devices=1)
    aps = [nc.dram_tensor(k, v.shape, mybir.dt.float32, kind="ExternalInput").ap() for k, v in arrays.items()]
    out = nc.dram_tensor("out", (D, TILES * N), mybir.dt.float32, kind="ExternalOutput").ap()
    build(nc, *aps, out)
    r = run_bass_kernel_spmd(nc, [arrays], core_ids=[0])
    y = r.results[0]["out"]
    return np.ascontiguousarray(y.reshape(D, TILES, BATCH, STEPS).transpose(2, 1, 3, 0).reshape(BATCH, TIME, D))
```

```python
from contextlib import ExitStack

import numpy as np

import concourse.bass as bass
from concourse import mybir

BATCH, TIME, D = 4, 1024, 128
HEADS, K = 16, 8
HIDDEN, EXPERTS = 512, 8
ROUTER = D // 4
STEPS = 64
L = 4
TILES = TIME // STEPS
C = STEPS // L
CB = C * BATCH
N = BATCH * STEPS
TG = N // 128
HB = HIDDEN // 128
VH = K // 2
NG = L * (L - 1) // 2
Y0 = 0
X0 = Y0 + C * (L + 1)
B0 = X0 + STEPS
K0 = B0 + STEPS
G0 = K0 + STEPS
SENT = G0 + C * NG
RX = K + L - 1
SLOTS = 20
LN_EPS, GN_EPS, NORM_EPS, GATE_MIN = 1e-5, 6.4e-4, 1e-6, 0.25
PROJ = ["w", "a", "b", "r", "k", "v", "g"]
MIX0, BO, GNW, GNB, BR1, BE1 = 0, 7, 8, 9, 10, 11
VECS = BE1 + (EXPERTS + 1) * HB
LAG_PROJ, LAG_CHUNK, LAG_SCAN, LAG_GN, LAG_LN2, LAG_FFN, LAG_OUT = -2, -1, 0, 1, 2, 3, 4


class Tile:
    def __init__(self, half, par):
        self.half, self.par, self.t = half, par, half * 2 + par


class Round:

    def __init__(self, i, tile_of):
        self.i, self.tile_of = i, tile_of

    def __call__(self, lag):
        return self.tile_of(lag)

    def before(self, lag):
        n = self.i - lag
        return max(0, min(TILES, n)) if isinstance(n, int) else n

    def through(self, lag):
        n = self.i - lag + 1
        return max(0, min(TILES, n)) if isinstance(n, int) else n


def run_tiles(eng, work):
    def fixed(i):
        def tile_of(lag):
            t = i - lag
            return Tile(t // 2, t % 2) if 0 <= t < TILES else None
        return Round(i, tile_of)

    first = LAG_OUT + 2
    last = TILES + LAG_PROJ
    for i in range(LAG_PROJ, first):
        work(fixed(i))
    with eng.Fori(first // 2, last // 2) as pair:
        for u in range(2):
            work(Round(pair * 2 + u, lambda lag, u=u: Tile(pair + (u - lag) // 2, (u - lag) % 2)))
    for i in range(last, TILES + LAG_OUT):
        work(fixed(i))


def build(nc, x_d, w_d, vec_d, cond_d, wmod_d, wr1_d, wr2_d, w1_d, w2_d, be2_d, out_d):
    F32, U32 = mybir.dt.float32, mybir.dt.uint32
    ALU, ACT, AX = mybir.AluOpType, mybir.ActivationFunctionType, mybir.AxisListType
    ctx = ExitStack()
    with ctx:
        def sb(name, shape, dt=F32):
            return ctx.enter_context(nc.sbuf_tensor(name, shape, dt))

        def two(name, shape, dt=F32):
            return [sb(f"{name}{i}", shape, dt) for i in range(2)]

        def sem(name):
            return ctx.enter_context(nc.semaphore(name))

        w_proj = sb("w_proj", [128, 8, 128])
        vec = sb("vec", [128, VECS])
        cond = sb("cond", [128, BATCH])
        cond_act = sb("cond_act", [128, BATCH])
        wr1 = sb("wr1", [128, ROUTER])
        wr2 = sb("wr2", [ROUTER + 1, EXPERTS])
        w1 = sb("w1", [128, EXPERTS + 1, HIDDEN])
        w2 = sb("w2", [128, EXPERTS + 1, HB, 128])
        be2 = sb("be2", [EXPERTS + 1, 128])
        ones_ch = sb("ones_ch", [128, 128])
        ones_hd = sb("ones_hd", [128, 128])
        mean_hd = sb("mean_hd", [128, 128])
        band = sb("band", [128, 128])
        ident = sb("ident", [128, 128])
        iota_i = sb("iota_i", [128, EXPERTS], mybir.dt.int32)
        iota_f = sb("iota_f", [128, EXPERTS])
        eps_ln = sb("eps_ln", [128, 1])
        eps_gn = sb("eps_gn", [128, 1])
        mod = sb("mod", [128, 6, BATCH])
        mod_sign = sb("mod_sign", [128, 2, BATCH])
        mod_abs = sb("mod_abs", [128, 2, BATCH])
        ga_bo = sb("ga_bo", [128, BATCH])

        x_in = two("x_in", [128, N])
        ln1_c = sb("ln1_c", [128, N])
        ln1_sd = sb("ln1_sd", [128, N])
        h1 = two("h1", [128, BATCH, STEPS + 1])
        shift = sb("shift", [128, BATCH, STEPS])
        mixed = sb("mixed", [128, 7, N])
        w_tanh = sb("w_tanh", [128, N])
        g_tanh = two("g_tanh", [128, N])
        gate_late = two("gate_late", [128, N])
        ab_raw = sb("ab_raw", [128, 2, N])
        ab_sq = sb("ab_sq", [128, 2, N])
        dec = two("dec", [128, CB, L])
        b_raw = two("b_raw", [128, CB, L])
        k_raw = two("k_raw", [128, CB, L])
        r_raw = two("r_raw", [128, CB, L])
        ar = two("ar", [128, 2, CB, L])
        v_send = two("v_send", [128, BATCH, STEPS])
        q = sb("q", [128, 2, CB, L])
        q_mul = sb("q_mul", [128, 2 * CB * (L - 1)])
        q_rank = sb("q_rank", [128, 2 * CB * (L - 1)])
        q_dec = sb("q_dec", [128, 2 * CB * (L - 1)])
        kb = sb("kb", [128, 2, CB, L])
        k_mul = sb("k_mul", [128, 2 * CB * (L - 1)])
        k_rank = sb("k_rank", [128, CB * (L - 1)])
        lam = sb("lam", [128, CB, L])
        send = sb("send", [128, BATCH, SENT])
        ops = two("ops", [128, K, SENT])
        vals = two("vals", [128, VH, STEPS])
        terms = two("terms", [128, C, L + 2, VH * K])
        u_mul = sb("u_mul", [128, C, VH, K])
        z = two("z", [128, C, L * VH])
        state = two("state", [128, C + 1, VH * K])
        o_terms = sb("o_terms", [128, C * L * VH, RX])
        o_scan = two("o_scan", [128, VH, STEPS])
        o_ch = two("o_ch", [128, N])
        gn_c = sb("gn_c", [128, N])
        gn_sd = sb("gn_sd", [128, N])
        gn_a = sb("gn_a", [128, N])
        gn_g = sb("gn_g", [128, N])
        x_res = two("x_res", [128, N])
        x_bias = sb("x_bias", [128, N])
        x2 = two("x2", [128, N])
        x2_late = two("x2_late", [128, N])
        ln2_c = sb("ln2_c", [128, N])
        ln2_sd = sb("ln2_sd", [128, N])
        h2 = two("h2", [128, N])
        rt_h = sb("rt_h", [ROUTER + 1, N])
        rt_lg = sb("rt_lg", [128, TG, EXPERTS + 1])
        rt_top = sb("rt_top", [128, TG, 8])
        rt_ix = sb("rt_ix", [128, TG, 8], U32)
        rt_ixf = sb("rt_ixf", [128, TG, 8])
        rt_d = sb("rt_d", [128, TG, EXPERTS + 1])
        rt_th = sb("rt_th", [128, TG, EXPERTS + 1])
        rt_num = sb("rt_num", [128, TG, EXPERTS + 1])
        rt_den = sb("rt_den", [128, TG, EXPERTS + 1])
        rt_inv = sb("rt_inv", [128, TG, EXPERTS + 1])
        rt_exp = sb("rt_exp", [128, TG, EXPERTS + 1])
        rt_sum = sb("rt_sum", [128, TG])
        rt_sinv = sb("rt_sinv", [128, TG])
        rt_gap = sb("rt_gap", [128, TG])
        rt_u = sb("rt_u", [128, TG])
        rt_ut = sb("rt_ut", [128, TG])
        rt_w1 = sb("rt_w1", [128, TG])
        rt_w2 = sb("rt_w2", [128, TG])
        rt_a = sb("rt_a", [128, TG, EXPERTS])
        rt_w = two("rt_wgt", [128, TG, EXPERTS])
        rt_b = sb("rt_b", [128, TG, EXPERTS])
        rt_wt = two("rt_wt", [EXPERTS + 1, N])
        hid = two("hid", [128, HB, N])
        wmod = hid[0][:, :, :].rearrange("p m n -> p (m n)")[:, 0:6 * 128]
        acc = [two(f"acc{p}_", [128, TG * 128]) for p in range(2)]
        y_out = two("y_out", [128, N])

        bank = [ctx.enter_context(nc.psum_tensor(f"bank{i}", [128, 512], F32)) for i in range(8)]
        ps_hid = [bank[m // 2][:, (m % 2) * N:(m % 2) * N + N] for m in range(HB)]
        ps_y = [bank[2][:, 0:N], bank[3][:, 0:N]]
        ps_proj = [bank[4 + (m // 2) % 2][:, (m % 2) * N:(m % 2) * N + N] for m in range(7)]
        ps_out = bank[4][:, 0:N]
        ps_ln1, ps_ln2, ps_gn = bank[6][:, 0:N], bank[6][:, N:2 * N], bank[6][:, 0:N]
        ps_sum, ps_rt = bank[7], bank[7][:, 0:N]

        S = {}

        def ev(name):
            if name not in S:
                S[name] = sem(name)
            return S[name]

        s_names = """w_loaded x_loaded0 x_loaded1 xr_loaded0 xr_loaded1 sent0 sent1 vsent0 vsent1 o_back0 o_back1 stored0 stored1
            const pconst cond_silu mod_mm mod_ready
            ln1_mean ln1_center ln1_square ln1_var ln1_sqrt ln1_recip ln1_norm h1_ready shift_ready mix_ready proj_done
            w_tanh_done d_ready ab_copied ab_squared r_ready k_ready v_ready g_tanh_done g_ready norm_sum norm_sqrt
            norm_max norm_recip a_ready b_ready
            q_copied kb_copied pull_mul pull_sum pull_rank pull_dec pull_add push_mul push_sum push_rank push_dec push_add
            score_out lam_mul packed ar_r x_packed
            u_first u_mul_done u_add gv_done dots z_done outer state_ready state_copied s_terms o_reduced
            gn_mean gn_center gn_square gn_var gn_sqrt gn_recip gn_norm gn_affine gn_gated wo_done x_biased x2_ready
            ln2_mean ln2_center ln2_square ln2_var ln2_sqrt ln2_recip ln2_norm h2_ready
            rt_hid rt_relu rt_logit rt_copied rt_topped rt_indexed rt_ix_f rt_gap1 rt_tanh1 rt_n rt_dn rt_i rt_e rt_s rt_si
            rt_gapped rt_uu rt_tanh2 rt_weights rt_wa rt_wb rt_ready rt_turned rt_wt_ready
            hid_mm hid_act y_mm y_acc out_turned out_ready""".split()
        for n_ in s_names:
            ev(n_)

        def wait(eng, sem_, value):
            if isinstance(value, int):
                if value > 0:
                    eng.wait_ge(sem_, value)
                return
            eng.wait_ge(sem_, value)
            if eng.engine in (nc.gpsimd.engine, nc.sync.engine):
                eng.sem_inc(ev("passed"))

        def bt(ap):
            return ap.rearrange("p (b t) -> p b t", b=BATCH)

        def bc(ap, shape):
            return ap.to_broadcast(shape)

        def per_chunk(ap, j, n):
            return bc(ap[:, :, j:j + 1], [128, CB, n])

        def per_chunk2(ap, j, n):
            return bc(ap[:, :, j:j + 1].rearrange("p (o c) l -> p o c l", o=1), [128, 2, CB, n])

        def cols(ap, *dims):
            m = int(np.prod(dims))
            v = ap[:, 0:m]
            if len(dims) == 2:
                return v.rearrange("p (a b) -> p a b", a=dims[0])
            return v.rearrange("p (a b c) -> p a b c", a=dims[0], b=dims[1])

        def sent_view(at, width):
            return send[:, :, at:at + C * width].rearrange("p b (c w) -> p b c w", w=width)

        def bcl(ap, lo, hi):
            return ap[:, :, lo:hi].rearrange("p (b c) l -> p b c l", b=BATCH)

        def op_view(par, at, width, lo, hi):
            return ops[par][:, :, at:at + C * width].rearrange("p k (c w) -> p k c w", w=width)[:, :, :, lo:hi]

        PULLS = list(range(L - 2, -1, -1))
        PUSHES = list(range(1, L))
        block = ctx.enter_context(nc.Block())

        @block.sync
        def _(sp):
            for dst, src in ((cond[:, :], cond_d[:, :]), (wmod[:, :], wmod_d[:, :]), (vec[:, :], vec_d[:, :])):
                sp.dma_start(dst, src).then_inc(ev("w_loaded"), 16)
            for dst, src, name in ((x_in[0][:, :], x_d[:, 0:N], "x_loaded0"), (w_proj[:, :, :], w_d[:, :, :], "small_loaded"),
                      (wr1[:, :], wr1_d[:, :], "small_loaded"), (wr2[:, :], wr2_d[:, :], "small_loaded"),
                      (be2[:, :], be2_d[:, :], "small_loaded")):
                sp.dma_start(dst, src).then_inc(ev(name), 16)

            def work(at):
                t = at(LAG_PROJ)
                if t is not None and not (isinstance(t.t, int) and t.t == 0):
                    wait(sp, ev("ln1_center"), t.t - 1)
                    sp.dma_start(x_in[t.par][:, :], x_d[:, bass.ds(t.t * N, N)]).then_inc(ev(f"x_loaded{t.par}"), 16)
                if t is not None and isinstance(t.t, int) and t.t == 1:
                    for dst, src in ((w1[:, :, :], w1_d[:, :, :]), (w2[:, :, :, :], w2_d[:, :, :, :])):
                        sp.dma_start(dst, src).then_inc(ev("experts_loaded"), 16)
                t = at(LAG_GN)
                if t is not None:
                    wait(sp, ev("x_biased"), (t.t - 1) * BATCH)
                    sp.dma_start(x_res[t.par][:, :], x_d[:, bass.ds(t.t * N, N)]).then_inc(ev(f"xr_loaded{t.par}"), 16)
                    wait(sp, ev("o_reduced"), (t.t + 1) * L)
                    wait(sp, ev("gn_center"), t.t - 1)
                    for b in range(BATCH):
                        for hf in range(2):
                            p0 = 32 * b + 16 * hf
                            sp.dma_start(o_ch[t.par][64 * hf:64 * hf + 64, b * STEPS:(b + 1) * STEPS], o_scan[t.par][p0:p0 + 16, :, :]).then_inc(ev(f"o_back{t.par}"), 16)
                t = at(LAG_OUT)
                if t is not None:
                    wait(sp, ev("out_ready"), (t.t + 1) * BATCH)
                    sp.dma_start(out_d[:, bass.ds(t.t * N, N)], y_out[t.par][:, :]).then_inc(ev(f"stored{t.par}"), 16)
                t = at(LAG_CHUNK)
                if t is not None:
                    wait(sp, ev("v_ready"), t.t + 1)
                    wait(sp, ev("gv_done"), (t.t - 1) * (L - 1))
                    for b in range(BATCH):
                        for hf in range(2):
                            p0 = 32 * b + 16 * hf
                            sp.dma_start(vals[t.par][p0:p0 + 16, :, :], v_send[t.par][64 * hf:64 * hf + 64, b, :]).then_inc(ev(f"vsent{t.par}"), 16)
                    wait(sp, ev("packed"), (t.t + 1) * 7)
                    wait(sp, ev("score_out"), (t.t + 1) * (L - 1))
                    wait(sp, ev("outer"), (t.t - 1) * C)
                    wait(sp, ev("s_terms"), (t.t - 1) * L)
                    for b in range(BATCH):
                        for hf in range(2):
                            p0 = 32 * b + 16 * hf
                            sp.dma_start(ops[t.par][p0:p0 + 16, :, :],
                                         send[:, b, :]).then_inc(ev(f"sent{t.par}"), 16)

            run_tiles(sp, work)
            sp.wait_ge(ev("stored0"), 16 * (TILES // 2))
            sp.wait_ge(ev("stored1"), 16 * (TILES // 2))

        @block.tensor
        def _(pe):
            pe.wait_ge(ev("w_loaded"), 16 * 3)
            pe.wait_ge(ev("small_loaded"), 16 * 4)
            pe.wait_ge(ev("pconst"), 8)
            pe.wait_ge(ev("cond_silu"), 1)
            for m in range(6):
                last = pe.matmul(ps_rt[:, m * BATCH:(m + 1) * BATCH], wmod[:, m * 128:(m + 1) * 128], cond_act[:, :],
                                 start=True, stop=True)
            last.then_inc(ev("mod_mm"), 1)

            def stats(ps, src, ones, name):
                pe.matmul(ps, ones, src, start=True, stop=True).then_inc(ev(name), 1)

            def hidden(t, e):
                if e == 0:
                    wait(pe, ev("h2_ready"), (t.t + 1) * BATCH)
                    if isinstance(t.t, int) and t.t == 0:
                        pe.wait_ge(ev("experts_loaded"), 16 * 2)
                for m in range(HB):
                    if m % 2 == 0:
                        wait(pe, ev("hid_act"), (t.t * (EXPERTS + 1) + e - 1) * HB + m + 2)
                    last = pe.matmul(ps_hid[m], w1[:, e, m * 128:(m + 1) * 128], h2[t.par][:, :], start=True, stop=True)
                    if m % 2 == 1:
                        last.then_inc(ev("hid_mm"), 1)

            def down(t, e):
                last_e = EXPERTS
                wait(pe, ev("y_acc"), (t.t * (EXPERTS + 1) + e - 1) * TG)
                for g in range(TG):
                    out = ps_y[(t.par + e) % 2][:, g * 128:(g + 1) * 128]
                    for m in range(HB):
                        if g == 0:
                            wait(pe, ev("hid_act"), (t.t * (EXPERTS + 1) + e) * HB + m + 1)
                        last = pe.matmul(out, hid[(t.par + e) % 2][:, m, g * 128:(g + 1) * 128], w2[:, e, m, :],
                                         start=(m == 0), stop=(m == HB - 1 and e != last_e))
                    if e == last_e:
                        wait(pe, ev("rt_wt_ready"), t.t + 1)
                        last = pe.matmul(out, rt_wt[t.par][:, g * 128:(g + 1) * 128], be2[:, :], start=False, stop=True)
                last.then_inc(ev("y_mm"), 1)

            def work(at):
                A, B, G, N2, E, O = (at(x) for x in (LAG_PROJ, LAG_CHUNK, LAG_GN, LAG_LN2, LAG_FFN, LAG_OUT))
                for s in range(SLOTS):
                    if E is not None:
                        if s == 0:
                            hidden(E, 0)
                        if s % 2 == 1 and (s + 1) // 2 <= EXPERTS:
                            hidden(E, (s + 1) // 2)
                        if s % 2 == 0 and 2 <= s:
                            down(E, (s - 2) // 2)
                    if O is not None and s == 1:
                        wait(pe, ev("y_acc"), (O.t + 1) * (EXPERTS + 1) * TG)
                        wait(pe, ev("v_ready"), at.before(LAG_PROJ))
                        for g in range(TG):
                            last = pe.matmul(ps_out[:, g * 128:(g + 1) * 128],
                                             acc[O.par][EXPERTS % 2][:, g * 128:(g + 1) * 128], ident[:, :],
                                             start=True, stop=True)
                        last.then_inc(ev("out_turned"), 1)
                    if s == 0:
                        wait(pe, ev("x2_ready"), at.before(LAG_GN) * BATCH)
                        wait(pe, ev("ln1_sqrt"), at.before(LAG_PROJ))
                        wait(pe, ev("ln2_sqrt"), at.before(LAG_LN2))
                        if A is not None:
                            wait(pe, ev(f"x_loaded{A.par}"), 16 * (A.half + 1))
                            stats(ps_ln1, x_in[A.par][:, :], ones_ch[:, :], "ln1_mean")
                        if N2 is not None:
                            wait(pe, ev("x2_ready"), (N2.t + 1) * BATCH)
                            stats(ps_ln2, x2[N2.par][:, :], ones_ch[:, :], "ln2_mean")
                    if s == 2:
                        wait(pe, ev("ln1_center"), at.through(LAG_PROJ))
                        wait(pe, ev("ln2_center"), at.through(LAG_LN2))
                        if A is not None:
                            wait(pe, ev("ln1_square"), A.t + 1)
                            stats(ps_ln1, ln1_sd[:, :], ones_ch[:, :], "ln1_var")
                        if N2 is not None:
                            wait(pe, ev("ln2_square"), N2.t + 1)
                            stats(ps_ln2, ln2_sd[:, :], ones_ch[:, :], "ln2_var")
                    if G is not None:
                        if s == 10:
                            wait(pe, ev(f"o_back{G.par}"), 16 * 8 * (G.half + 1))
                            wait(pe, ev("ln1_sqrt"), at.through(LAG_PROJ))
                            wait(pe, ev("ln2_sqrt"), at.through(LAG_LN2))
                            wait(pe, ev("x2_ready"), G.t * BATCH)
                            stats(ps_gn, o_ch[G.par][:, :], mean_hd[:, :], "gn_mean")
                        if s == 13:
                            wait(pe, ev("gn_square"), G.t + 1)
                            wait(pe, ev("gn_center"), G.t + 1)
                            stats(ps_gn, gn_sd[:, :], mean_hd[:, :], "gn_var")
                        if s == 17:
                            wait(pe, ev("gn_gated"), G.t + 1)
                            wait(pe, ev("gn_sqrt"), G.t + 1)
                            stats(ps_gn, gn_g[:, :], w_proj[:, 7, :], "wo_done")
                    if A is not None and 8 <= s <= 11:
                        for m in ((0, 1), (2, 3), (4, 5), (6,))[s - 8]:
                            wait(pe, ev("mix_ready"), A.t * 7 + m + 1)
                            if m == 0:
                                wait(pe, ev("v_ready"), A.t)
                                wait(pe, ev("out_ready"), at.through(LAG_OUT) * BATCH)
                            if m == 2:
                                wait(pe, ev("g_tanh_done"), A.t)
                            if m == 4:
                                wait(pe, ev("ab_squared"), A.t * 2 + 1)
                            if m == 6:
                                wait(pe, ev("r_ready"), A.t + 1)
                            last = pe.matmul(ps_proj[m], w_proj[:, m, :], mixed[:, m, :], start=True, stop=True)
                        last.then_inc(ev("proj_done"), 1)
                    if B is not None:
                        for n_, j in enumerate(PULLS):
                            if s == 1 + 2 * n_:
                                m = 2 * CB * (L - 1 - j)
                                wait(pe, ev("pull_mul"), B.t * (L - 1) + n_ + 1)
                                if n_ == 0:
                                    wait(pe, ev("norm_sqrt"), at.before(LAG_PROJ))
                                    wait(pe, ev("rt_wt_ready"), at.before(LAG_LN2))
                                wait(pe, ev("score_out"), B.t * (L - 1) + n_)
                                pe.matmul(ps_sum[:, 0:m], ones_hd[:, :], q_mul[:, 0:m], start=True, stop=True)\
                                    .then_inc(ev("pull_sum"), 1)
                        for n_, j in enumerate(PUSHES):
                            if s == 2 + 2 * n_:
                                m = 2 * CB * j
                                wait(pe, ev("push_mul"), B.t * (L - 1) + n_ + 1)
                                wait(pe, ev("pull_rank"), B.t * (L - 1) + n_ + 1)
                                pe.matmul(ps_sum[:, 0:m], ones_hd[:, :], k_mul[:, 0:m], start=True, stop=True)\
                                    .then_inc(ev("push_sum"), 1)
                    if N2 is not None:
                        if s == 8:
                            wait(pe, ev("h2_ready"), (N2.t + 1) * BATCH)
                            wait(pe, ev("score_out"), at.through(LAG_CHUNK) * (L - 1))
                            wait(pe, ev("norm_sqrt"), at.before(LAG_PROJ))
                            wait(pe, ev("rt_wt_ready"), N2.t)
                            pe.matmul(ps_rt[0:ROUTER, :], wr1[:, :], h2[N2.par][:, :], start=True, stop=True)\
                                .then_inc(ev("rt_hid"), 1)
                        if s == 10:
                            wait(pe, ev("rt_relu"), N2.t + 1)
                            for g in range(TG):
                                last = pe.matmul(ps_rt[:, g * EXPERTS:(g + 1) * EXPERTS], rt_h[:, g * 128:(g + 1) * 128],
                                                 wr2[:, :], start=True, stop=True)
                            last.then_inc(ev("rt_logit"), 1)
                    if A is not None and s == 13:
                        wait(pe, ev("ab_squared"), (A.t + 1) * 2)
                        wait(pe, ev("score_out"), at.through(LAG_CHUNK) * (L - 1))
                        wait(pe, ev("rt_copied"), at.through(LAG_LN2))
                        wait(pe, ev("rt_wt_ready"), at.before(LAG_LN2))
                        pe.matmul(ps_sum[:, :], ones_hd[:, :], ab_sq[:, :, :].rearrange("p a n -> p (a n)"),
                                  start=True, stop=True).then_inc(ev("norm_sum"), 1)
                    if N2 is not None and s == 16:
                        wait(pe, ev("rt_ready"), N2.t + 1)
                        wait(pe, ev("norm_sqrt"), at.through(LAG_PROJ))
                        for g in range(TG):
                            last = pe.matmul(ps_rt[0:EXPERTS, g * 128:(g + 1) * 128], rt_w[N2.par][:, g, :], ident[:, :],
                                             start=True, stop=True)
                        last.then_inc(ev("rt_turned"), 1)

            run_tiles(pe, work)

        @block.scalar
        def _(act):
            act.wait_ge(ev("w_loaded"), 16 * 3)
            act.activation(cond_act[:, :], cond[:, :], ACT.Silu).then_inc(ev("cond_silu"), 1)
            act.wait_ge(ev("mod_mm"), 1)
            act.activation(mod[:, :, :].rearrange("p m b -> p (m b)"), ps_rt[:, 0:6 * BATCH], ACT.Copy).then_inc(ev("const"), 1)
            act.wait_ge(ev("const"), 1)
            for n_, m in enumerate((2, 5)):
                act.activation(mod_abs[:, n_, :], mod[:, m, :], ACT.Abs).then_inc(ev("const"), 1)
            act.wait_ge(ev("pconst"), 8)
            act.wait_ge(ev("mod_ready"), 1)

            def work(at):
                A, B, R, G, N2, E = (at(x) for x in (LAG_PROJ, LAG_CHUNK, LAG_SCAN, LAG_GN, LAG_LN2, LAG_FFN))

                def affine(dst, src, scale, bias, name):
                    for b in range(BATCH):
                        act.activation(dst(b), src[:, b * STEPS:(b + 1) * STEPS], ACT.Identity, bias=bias[:, b:b + 1],
                                       scale=1.0 if scale is None else scale[:, b:b + 1]).then_inc(ev(name), 1)

                def silu(e):
                    for m in range(HB):
                        if m % 2 == 0:
                            wait(act, ev("hid_mm"), (E.t * (EXPERTS + 1) + e) * 2 + m // 2 + 1)
                        wait(act, ev("y_mm"), E.t * (EXPERTS + 1) + e - 1)
                        act.activation(hid[(E.par + e) % 2][:, m, :], ps_hid[m], ACT.Silu,
                                       bias=vec[:, BE1 + e * HB + m:BE1 + e * HB + m + 1]).then_inc(ev("hid_act"), 1)


                for s in range(SLOTS):
                    if E is not None:
                        if s == 0:
                            silu(0)
                        if s % 2 == 1 and (s + 1) // 2 <= EXPERTS:
                            silu((s + 1) // 2)
                    if N2 is not None:
                        if s == 9:
                            wait(act, ev("rt_hid"), N2.t + 1)
                            wait(act, ev("rt_logit"), N2.t)
                            act.activation(rt_h[0:ROUTER, :], ps_rt[0:ROUTER, :], ACT.Relu, bias=vec[0:ROUTER, BR1:BR1 + 1])\
                                .then_inc(ev("rt_relu"), 1)
                        if s == 12:
                            wait(act, ev("rt_gap1"), (N2.t + 1) * 2)
                            act.activation(rt_th[:, :, :], rt_d[:, :, :], ACT.Tanh, scale=0.5).then_inc(ev("rt_tanh1"), 1)
                        if s == 14:
                            wait(act, ev("rt_uu"), N2.t + 1)
                            act.activation(rt_ut[:, :], rt_u[:, :], ACT.Tanh, scale=0.25).then_inc(ev("rt_tanh2"), 1)
                        if s == 17:
                            wait(act, ev("rt_turned"), N2.t + 1)
                            wait(act, ev("y_mm"), (N2.t - 1) * (EXPERTS + 1))
                            act.activation(rt_wt[N2.par][0:EXPERTS, :], ps_rt[0:EXPERTS, :], ACT.Copy).then_inc(ev("rt_wt_ready"), 1)
                    if s == 2:
                        if A is not None:
                            wait(act, ev("ln1_center"), A.t + 1)
                            act.activation(ln1_sd[:, :], ln1_c[:, :], ACT.Square).then_inc(ev("ln1_square"), 1)
                        if N2 is not None:
                            wait(act, ev("ln2_center"), N2.t + 1)
                            act.activation(ln2_sd[:, :], ln2_c[:, :], ACT.Square).then_inc(ev("ln2_square"), 1)
                    if s == 4:
                        wait(act, ev("ln1_var"), at.through(LAG_PROJ))
                        wait(act, ev("ln2_var"), at.through(LAG_LN2))
                        if A is not None:
                            act.activation(ln1_sd[:, :], ps_ln1, ACT.Sqrt, bias=eps_ln[:, 0:1]).then_inc(ev("ln1_sqrt"), 1)
                        if N2 is not None:
                            act.activation(ln2_sd[:, :], ps_ln2, ACT.Sqrt, bias=eps_ln[:, 0:1]).then_inc(ev("ln2_sqrt"), 1)
                        if N2 is not None:
                            wait(act, ev("x2_ready"), (N2.t + 1) * BATCH)
                            wait(act, ev("out_ready"), (N2.t - 1) * BATCH)
                            act.activation(x2_late[N2.par][:, :], x2[N2.par][:, :], ACT.Copy).then_inc(ev("x2_saved"), 1)
                    if s == 6:
                        if A is not None:
                            wait(act, ev("ln1_norm"), A.t + 1)
                            wait(act, ev("mix_ready"), (A.t - 1) * 7)
                            wait(act, ev("h1_edge"), A.t - 1)
                            wait(act, ev("shift_ready"), A.t - 1)
                            affine(lambda b: h1[A.par][:, b, 1:STEPS + 1], ln1_c, mod[:, 1, :], mod[:, 0, :], "h1_ready")
                        if N2 is not None:
                            wait(act, ev("ln2_norm"), N2.t + 1)
                            wait(act, ev("rt_hid"), N2.t - 1)
                            wait(act, ev("hid_mm"), (N2.t - 1) * (EXPERTS + 1) * 2)
                            affine(lambda b: h2[N2.par][:, b * STEPS:(b + 1) * STEPS], ln2_c, mod[:, 4, :], mod[:, 3, :], "h2_ready")
                    if R is not None and s == 10:
                        wait(act, ev("g_tanh_done"), R.t + 1)
                        wait(act, ev("gn_gated"), R.t - 1)
                        act.activation(gate_late[R.par][:, :], g_tanh[R.par][:, :], ACT.Copy, bias=0.5, scale=0.5)\
                            .then_inc(ev("gate_copied"), 1)
                    if G is not None and s == 8:
                        wait(act, ev(f"xr_loaded{G.par}"), 16 * (G.half + 1))
                        wait(act, ev("x2_ready"), G.t * BATCH)
                        affine(lambda b: x_bias[:, b * STEPS:(b + 1) * STEPS], x_res[G.par], None, ga_bo, "x_biased")
                    if B is not None and s == 7:
                        wait(act, ev("lam_mul"), (B.t + 1) * (L - 1))
                        act.activation(sent_view(Y0, L + 1)[:, :, :, 0:1], bcl(lam, L - 1, L), ACT.Copy).then_inc(ev("packed"), 1)
                        act.activation(sent_view(X0, L)[:, :, :, L - 1:L], bcl(r_raw[B.par], L - 1, L), ACT.Copy).then_inc(ev("packed"), 1)
                        act.activation(sent_view(Y0, L + 1)[:, :, :, 1:2], bcl(ar[B.par][:, 0], 0, 1), ACT.Copy).then_inc(ev("packed"), 1)
                        wait(act, ev("pull_add"), (B.t + 1) * (L - 1))
                        act.activation(sent_view(Y0, L + 1)[:, :, :, 2:L + 1], bcl(q[:, 0], 1, L), ACT.Copy).then_inc(ev("packed"), 1)
                        act.activation(sent_view(X0, L)[:, :, :, 0:L - 1], bcl(q[:, 1], 1, L), ACT.Copy).then_inc(ev("packed"), 1)
                        wait(act, ev("push_add"), (B.t + 1) * (L - 1))
                        wait(act, ev("push_dec"), (B.t + 1) * (L - 1))
                        act.activation(sent_view(K0, L), bcl(kb[:, 0], 0, L), ACT.Copy).then_inc(ev("packed"), 1)
                        act.activation(sent_view(B0, L), bcl(kb[:, 1], 0, L), ACT.Copy).then_inc(ev("packed"), 1)
                    if A is not None and 9 <= s <= 12:
                        for m in ((0, 1), (2, 3), (4, 5), (6,))[s - 9]:
                            what = PROJ[m]
                            wait(act, ev("proj_done"), A.t * 4 + m // 2 + 1)
                            if what == "w":
                                act.activation(w_tanh[:, :], ps_proj[m], ACT.Tanh, scale=-0.5).then_inc(ev("w_tanh_done"), 1)
                                act.wait_ge(ev("w_tanh_done"), A.t + 1)
                                wait(act, ev("pull_dec"), (A.t - 1) * (L - 1))
                                wait(act, ev("lam_mul"), (A.t - 1) * (L - 1))
                                wait(act, ev("push_dec"), (A.t - 1) * (L - 1))
                                act.activation(dec[A.par][:, :, :].rearrange("p c l -> p (c l)"), w_tanh[:, :], ACT.Copy, bias=0.5,
                                               scale=0.5).then_inc(ev("d_ready"), 1)
                            elif what in "ab":
                                wait(act, ev("a_ready" if what == "a" else "b_ready"), A.t)
                                wait(act, ev("norm_sum"), A.t)
                                act.activation(ab_raw[:, m - 1, :], ps_proj[m], ACT.Copy).then_inc(ev("ab_copied"), 1)
                                act.activation(ab_sq[:, m - 1, :], ps_proj[m], ACT.Square).then_inc(ev("ab_squared"), 1)
                            elif what == "r":
                                wait(act, ev("ar_r"), A.t - 1)
                                act.activation(r_raw[A.par][:, :, :].rearrange("p c l -> p (c l)"), ps_proj[m], ACT.Copy)\
                                    .then_inc(ev("r_ready"), 1)
                            elif what == "k":
                                wait(act, ev("kb_copied"), (A.t - 1) * 2)
                                act.activation(k_raw[A.par][:, :, :].rearrange("p c l -> p (c l)"), ps_proj[m], ACT.Tanh)\
                                    .then_inc(ev("k_ready"), 1)
                            elif what == "v":
                                wait(act, ev(f"vsent{A.par}"), 16 * 8 * A.half)
                                act.activation(v_send[A.par][:, :, :], bt(ps_proj[m]), ACT.Copy).then_inc(ev("v_ready"), 1)
                            else:
                                act.activation(g_tanh[A.par][:, :], ps_proj[m], ACT.Tanh, scale=0.5).then_inc(ev("g_tanh_done"), 1)
                    if B is not None:
                        for n_, j in enumerate(PUSHES):
                            if s == 2 + 2 * n_:
                                wait(act, ev("push_sum"), B.t * (L - 1) + n_ + 1)
                                wait(act, ev("push_rank"), B.t * (L - 1) + n_ + 1)
                                if n_ == 0:
                                    wait(act, ev(f"sent{1 - B.par}"), 16 * 8 * (B.half + B.par))
                                src = ps_sum[:, CB * j:2 * CB * j].rearrange("p (b c s) -> p b c s", b=BATCH, s=j)
                                act.activation(sent_view(G0, NG)[:, :, :, j * (j - 1) // 2:j * (j + 1) // 2], src, ACT.Copy)\
                                    .then_inc(ev("score_out"), 1)
                    if G is not None and s == 12:
                        wait(act, ev("gn_center"), G.t + 1)
                        act.activation(gn_sd[:, :], gn_c[:, :], ACT.Square).then_inc(ev("gn_square"), 1)
                    if s == 14:
                        if G is not None:
                            wait(act, ev("gn_var"), G.t + 1)
                            act.activation(gn_sd[:, :], ps_gn, ACT.Sqrt, bias=eps_gn[:, 0:1]).then_inc(ev("gn_sqrt"), 1)
                        if A is not None:
                            wait(act, ev("norm_sum"), A.t + 1)
                            wait(act, ev("b_ready"), A.t)
                            act.activation(ab_sq[:, :, :].rearrange("p a n -> p (a n)"), ps_sum[:, :], ACT.Sqrt).then_inc(ev("norm_sqrt"), 1)

            run_tiles(act, work)

        @block.gpsimd
        def _(pool):
            pool.memset(ones_ch[:, :], 1.0 / D).then_inc(ev("pconst"), 1)
            pool.memset(ones_hd[:, :], 1.0)
            pool.memset(mean_hd[:, :], 1.0 / K)
            pool.memset(band[:, :], 1.0 / K)
            pool.memset(ident[:, :], 0.0)
            pool.memset(rt_h[:, :], 1.0)
            pool.memset(rt_wt[0][:, :], 1.0)
            pool.memset(rt_wt[1][:, :], 1.0)
            pool.memset(eps_ln[:, :], LN_EPS).then_inc(ev("pconst"), 1)
            pool.memset(eps_gn[:, :], GN_EPS).then_inc(ev("pconst"), 1)
            pool.memset(o_terms[:, :, :], 0.0)
            for i in range(2):
                pool.memset(h1[i][:, :, :], 0.0)
                pool.memset(state[i][:, :, :], 0.0)
            pool.iota(iota_i[:, :], pattern=[[1, EXPERTS]], base=0, channel_multiplier=0).then_inc(ev("pconst"), 1)
            pool.wait_ge(ev("pconst"), 4)
            pool.tensor_copy(iota_f[:, :], iota_i[:, :]).then_inc(ev("pconst"), 1)
            groups = [(ones_hd[:, :].rearrange("p (h k) -> p h k", k=K), [[K, HEADS], [0, K]], 0, K)]
            for f, m in enumerate((mean_hd, band)):
                groups.append((m[:, :].rearrange("p (f h v) -> p f h v", f=2, v=VH), [[0, 2], [VH, HEADS], [0, VH]], 64 * f, VH))
            for v, pattern, at0, size in groups:
                pool.affine_select(out=v, in_=v, compare_op=ALU.is_ge, fill=0.0, base=-at0,
                                   pattern=[[-st, n_] for st, n_ in pattern], channel_multiplier=1).then_inc(ev("band_low"), 1)
            pool.wait_ge(ev("band_low"), 3)
            for v, pattern, at0, size in groups:
                pool.affine_select(out=v, in_=v, compare_op=ALU.is_ge, fill=0.0, base=at0 + size - 1,
                                   pattern=pattern, channel_multiplier=-1).then_inc(ev("band_high"), 1)
            pool.wait_ge(ev("band_high"), 3)
            pool.tensor_tensor(mean_hd[:, :], mean_hd[:, :], band[:, :], ALU.add).then_inc(ev("pconst"), 2)
            pool.affine_select(out=ident[:, :], in_=ident[:, :], compare_op=ALU.not_equal, fill=1.0, base=0,
                               pattern=[[-1, 128]], channel_multiplier=1).then_inc(ev("pconst"), 1)

            pool.wait_ge(ev("pconst"), 8)
            pool.wait_ge(ev("mod_ready"), 1)

            def work(at):
                A, B, R, G, N2 = (at(x) for x in (LAG_PROJ, LAG_CHUNK, LAG_SCAN, LAG_GN, LAG_LN2))
                for s in range(SLOTS):
                    if B is not None and 14 <= s < 14 + L:
                        j = s - 14
                        if j == 0:
                            wait(pool, ev(f"sent{B.par}"), 16 * 8 * (B.half + 1))
                            wait(pool, ev(f"vsent{B.par}"), 16 * 8 * (B.half + 1))
                            wait(pool, ev("state_ready"), (B.t - 1) * C)
                        slot = terms[B.par][:, :, L + 1, :].rearrange("p c (v k) -> p c v k", v=VH)
                        val = bc(vals[B.par][:, :, :].rearrange("p v (c l) -> p c v l", l=L)[:, :, :, j:j + 1], [128, C, VH, K])
                        key = bc(op_view(B.par, K0, L, j, j + 1).rearrange("p k c o -> p c o k"), [128, C, VH, K])
                        if j == 0:
                            pool.tensor_tensor(slot, val, key, ALU.mult).then_inc(ev("u_first"), 1)
                            wait(pool, ev("u_first"), B.t + 1)
                            wait(pool, ev("u_add"), B.t * (L - 1))
                        else:
                            pool.tensor_tensor(u_mul[:, :, :, :], val, key, ALU.mult).then_inc(ev("u_mul_done"), 1)
                            wait(pool, ev("u_mul_done"), B.t * (L - 1) + j)
                            pool.tensor_tensor(slot, slot, u_mul[:, :, :, :], ALU.add).then_inc(ev("u_add"), 1)
                            if j < L - 1:
                                wait(pool, ev("u_add"), B.t * (L - 1) + j)
                    if R is not None:
                        if s == 12:
                            wait(pool, ev("o_reduced"), R.t * L)
                            ot = o_terms[:, :, :].rearrange("p (c j v) x -> p c j v x", c=C, j=L)
                            for c_ in range(L - 1):
                                for j in range(c_, L - 1):
                                    g_at = j * (j + 1) // 2 + c_
                                    sc = bc(op_view(R.par, G0, NG, g_at, g_at + 1)[:, 0, :, :], [128, C, VH])
                                    vv = vals[R.par][:, :, :].rearrange("p v (c l) -> p c v l", l=L)[:, :, :, c_]
                                    last = pool.tensor_tensor(ot[:, :, j, :, K + c_], sc, vv, ALU.mult)
                                last.then_inc(ev("gv_done"), 1)
                    if G is not None and 1 <= s < 1 + L:
                        if s == 1:
                            wait(pool, ev("state_ready"), (G.t + 1) * C)
                            wait(pool, ev("s_terms"), G.t * L)
                            pool.tensor_copy(state[G.par][:, 0, :], state[1 - G.par][:, C, :]).then_inc(ev("state_copied"), 1)
                            wait(pool, ev("state_copied"), G.t + 1)
                            wait(pool, ev("o_reduced"), G.t * L)
                        ot = o_terms[:, :, :].rearrange("p (c j v) x -> p c j v x", c=C, j=L)
                        for j in (s - 1,):
                            c0 = 1 if j == L - 1 else 0
                            st = state[G.par][:, c0:c0 + C, :].rearrange("p c (v k) -> p c v k", v=VH)
                            xv = bc(op_view(G.par, X0, L, j, j + 1).rearrange("p k c o -> p c o k"), [128, C, VH, K])
                            pool.tensor_tensor(ot[:, :, j, :, 0:K], st, xv, ALU.mult).then_inc(ev("s_terms"), 1)
                    if A is not None:
                        if s == 6:
                            wait(pool, ev("h1_ready"), (A.t + 1) * BATCH)
                            wait(pool, ev("mix_ready"), A.t * 7)
                            if not (isinstance(A.t, int) and A.t == 0):
                                pool.tensor_copy(h1[A.par][:, :, 0:1], h1[1 - A.par][:, :, STEPS:STEPS + 1])\
                                    .then_inc(ev("h1_edge"), 1)
                                wait(pool, ev("h1_edge"), A.t)
                            pool.tensor_tensor(shift[:, :, :], h1[A.par][:, :, 0:STEPS], h1[A.par][:, :, 1:STEPS + 1], ALU.subtract)\
                                .then_inc(ev("shift_ready"), 1)
                        if s == 13:
                            wait(pool, ev("r_ready"), A.t + 1)
                            wait(pool, ev("q_copied"), A.t - 1)
                            wait(pool, ev("push_mul"), (A.t - 1) * (L - 1))
                            pool.tensor_copy(ar[A.par][:, 1, :, 1:L], r_raw[A.par][:, :, 0:L - 1]).then_inc(ev("ar_r"), 1)
                    if B is not None:
                        par = B.par
                        if s == 0:
                            wait(pool, ev("a_ready"), B.t + 1)
                            wait(pool, ev("ar_r"), B.t + 1)
                            wait(pool, ev("packed"), B.t * 7)
                            pool.tensor_copy(q[:, :, :, 1:L], ar[par][:, :, :, 1:L]).then_inc(ev("q_copied"), 1)
                            wait(pool, ev("b_ready"), B.t + 1)
                            wait(pool, ev("k_ready"), B.t + 1)
                            pool.tensor_copy(kb[:, 0, :, :], k_raw[par][:, :, :]).then_inc(ev("kb_copied"), 1)
                            pool.tensor_copy(kb[:, 1, :, :], b_raw[par][:, :, :]).then_inc(ev("kb_copied"), 1)
                            wait(pool, ev("q_copied"), B.t + 1)
                            wait(pool, ev("kb_copied"), (B.t + 1) * 2)
                        for n_, j in enumerate(PULLS):
                            if s == 0 + 2 * n_:
                                w_ = L - 1 - j
                                if n_ > 0:
                                    wait(pool, ev("pull_add"), B.t * (L - 1) + n_)
                                if n_ == 0:
                                    wait(pool, ev("pull_sum"), B.t * (L - 1))
                                pool.tensor_tensor(cols(q_mul, 2, CB, w_), q[:, :, :, j + 1:L], per_chunk2(b_raw[par], j, w_), ALU.mult)\
                                    .then_inc(ev("pull_mul"), 1)
                                pool.tensor_tensor(cols(q_dec, 2, CB, w_), q[:, :, :, j + 1:L], per_chunk2(dec[par], j, w_), ALU.mult)\
                                    .then_inc(ev("pull_dec"), 1)
                        for n_, j in enumerate(PUSHES):
                            if s == 1 + 2 * n_:
                                if n_ > 0:
                                    wait(pool, ev("push_add"), B.t * (L - 1) + n_)
                                    wait(pool, ev("push_dec"), B.t * (L - 1) + n_)
                                else:
                                    wait(pool, ev("push_sum"), B.t * (L - 1))
                                pool.tensor_tensor(cols(k_mul, 2, CB, j),
                                                   bc(kb[:, 0:1, :, 0:j], [128, 2, CB, j]),
                                                   bc(ar[par][:, :, :, j:j + 1], [128, 2, CB, j]), ALU.mult)\
                                    .then_inc(ev("push_mul"), 1)
                                wait(pool, ev("push_mul"), B.t * (L - 1) + n_ + 1)
                                pool.tensor_tensor(kb[:, :, :, 0:j], kb[:, :, :, 0:j], per_chunk2(dec[par], j, j), ALU.mult)\
                                    .then_inc(ev("push_dec"), 1)
                                src = dec[par][:, :, 0:1] if j == 1 else lam[:, :, j - 1:j]
                                if j > 1:
                                    wait(pool, ev("lam_mul"), B.t * (L - 1) + j - 1)
                                pool.tensor_tensor(lam[:, :, j:j + 1], src, dec[par][:, :, j:j + 1], ALU.mult)\
                                    .then_inc(ev("lam_mul"), 1)
                    if G is not None:
                        if s == 16:
                            wait(pool, ev("gn_norm"), G.t + 1)
                            wait(pool, ev("gn_gated"), G.t)
                            pool.tensor_scalar(gn_a[:, :], gn_c[:, :], vec[:, GNW:GNW + 1], vec[:, GNB:GNB + 1], ALU.mult, ALU.add)\
                                .then_inc(ev("gn_affine"), 1)
                            wait(pool, ev("gn_affine"), G.t + 1)
                            wait(pool, ev("gate_copied"), G.t + 1)
                            wait(pool, ev("wo_done"), G.t)
                            pool.tensor_tensor(gn_g[:, :], gn_a[:, :], gate_late[G.par][:, :], ALU.mult).then_inc(ev("gn_gated"), 1)

            run_tiles(pool, work)

        @block.vector
        def _(dve):
            dve.wait_ge(ev("const"), 3)
            for m in (1, 4):
                dve.tensor_scalar(mod[:, m, :], mod[:, m, :], 1.0, None, ALU.add).then_inc(ev("mod_step"), 1)
            for n_, m in enumerate((2, 5)):
                dve.tensor_scalar(mod_sign[:, n_, :], mod[:, m, :], 0.0, 2.0, ALU.is_ge, ALU.mult).then_inc(ev("mod_step"), 1)
            dve.wait_ge(ev("mod_step"), 4)
            dve.tensor_scalar(mod_sign[:, :, :], mod_sign[:, :, :], -1.0, None, ALU.add).then_inc(ev("mod_step"), 1)
            dve.tensor_scalar(mod_abs[:, :, :], mod_abs[:, :, :], GATE_MIN, None, ALU.max).then_inc(ev("mod_step"), 1)
            dve.wait_ge(ev("mod_step"), 6)
            for n_, m in enumerate((2, 5)):
                dve.tensor_tensor(mod[:, m, :], mod_sign[:, n_, :], mod_abs[:, n_, :], ALU.mult).then_inc(ev("mod_step"), 1)
            dve.wait_ge(ev("mod_step"), 8)
            dve.wait_ge(ev("w_loaded"), 16 * 3)
            dve.tensor_scalar(ga_bo[:, :], mod[:, 2, :], vec[:, BO:BO + 1], None, ALU.mult).then_inc(ev("mod_ready"), 1)
            dve.wait_ge(ev("pconst"), 8)

            def norm(t, ps, src, c, sd, name, stage, consumed=None):
                if stage == 0:
                    wait(dve, ev(f"{name}_mean"), t.t + 1)
                    wait(dve, consumed[0], consumed[1])
                    dve.tensor_tensor(c[:, :], src, ps, ALU.subtract).then_inc(ev(f"{name}_center"), 1)
                else:
                    wait(dve, ev(f"{name}_sqrt"), t.t + 1)
                    dve.reciprocal(sd[:, :], sd[:, :]).then_inc(ev(f"{name}_recip"), 1)
                    dve.wait_ge(ev(f"{name}_recip"), t.t + 1)
                    dve.tensor_tensor(c[:, :], c[:, :], sd[:, :], ALU.mult).then_inc(ev(f"{name}_norm"), 1)

            def chunk(R, c):
                par, n_ = R.par, R.t * C + c
                before = state[1 - par][:, C, :] if c == 0 else state[par][:, c, :]
                wait(dve, ev("state_ready"), n_)
                if c == 0:
                    wait(dve, ev(f"sent{par}"), 16 * 8 * (R.half + 1))
                sv = bc(before.rearrange("p (o v k) -> p o v k", o=1, v=VH), [128, L + 1, VH, K])
                yv = bc(ops[par][:, :, Y0 + c * (L + 1):Y0 + (c + 1) * (L + 1)].rearrange("p k (j o) -> p j o k", o=1), [128, L + 1, VH, K])
                dve.tensor_tensor(terms[par][:, c, 0:L + 1, :].rearrange("p j (v k) -> p j v k", v=VH), sv, yv, ALU.mult)\
                    .then_inc(ev("dots"), 1)
                dve.wait_ge(ev("dots"), n_ + 1)
                dve.tensor_reduce(z[par][:, c, :], terms[par][:, c, 1:L + 1, :].rearrange("p j (v k) -> p (j v) k", v=VH), AX.X, ALU.add)\
                    .then_inc(ev("z_done"), 1)
                dve.wait_ge(ev("z_done"), n_ + 1)
                zv = bc(z[par][:, c, :].rearrange("p (j v o) -> p j v o", j=L, o=1), [128, L, VH, K])
                bv = bc(ops[par][:, :, B0 + c * L:B0 + (c + 1) * L].rearrange("p k (j o) -> p j o k", o=1), [128, L, VH, K])
                dve.tensor_tensor(terms[par][:, c, 1:L + 1, :].rearrange("p j (v k) -> p j v k", v=VH), zv, bv, ALU.mult)\
                    .then_inc(ev("outer"), 1)
                dve.wait_ge(ev("outer"), n_ + 1)
                if c == C - 1:
                    wait(dve, ev("state_copied"), R.t)
                if c == 0:
                    wait(dve, ev("u_add"), (R.t + 1) * (L - 1))
                    wait(dve, ev("s_terms"), (R.t - 1) * L)
                dve.tensor_reduce(state[par][:, c + 1, :], terms[par][:, c, :, :].rearrange("p s a -> p a s"), AX.X, ALU.add)\
                    .then_inc(ev("state_ready"), 1)

            def expert_out(E, e):
                n_ = E.t * (EXPERTS + 1) + e
                wait(dve, ev("y_mm"), n_ + 1)
                if e == 0:
                    wait(dve, ev("rt_ready"), E.t + 1)
                    wait(dve, ev("out_turned"), E.t - 1)
                else:
                    dve.wait_ge(ev("y_acc"), n_ * TG)
                for g in range(TG):
                    cs = slice(g * 128, (g + 1) * 128)
                    if e == 0:
                        dve.tensor_scalar(acc[E.par][0][:, cs], ps_y[E.par][:, cs], rt_w[E.par][:, g, 0:1], None, ALU.mult).then_inc(ev("y_acc"), 1)
                    elif e < EXPERTS:
                        dve.scalar_tensor_tensor(out=acc[E.par][e % 2][:, cs], in0=ps_y[(E.par + e) % 2][:, cs], scalar=rt_w[E.par][:, g, e:e + 1],
                                                 in1=acc[E.par][(e - 1) % 2][:, cs], op0=ALU.mult, op1=ALU.add).then_inc(ev("y_acc"), 1)
                    else:
                        dve.tensor_tensor(acc[E.par][e % 2][:, cs], ps_y[(E.par + e) % 2][:, cs], acc[E.par][(e - 1) % 2][:, cs], ALU.add)\
                            .then_inc(ev("y_acc"), 1)

            def work(at):
                A, B, R, G, N2, E, O = (at(x) for x in (LAG_PROJ, LAG_CHUNK, LAG_SCAN, LAG_GN, LAG_LN2, LAG_FFN, LAG_OUT))
                for s in range(SLOTS):
                    if R is not None and 1 <= s <= 16:
                        for c in range((s - 1) * C // 16, s * C // 16):
                            chunk(R, c)
                    if s == 1:
                        wait(dve, ev("ln1_mean"), at.through(LAG_PROJ))
                        wait(dve, ev("ln2_mean"), at.through(LAG_LN2))
                    if A is not None:
                        if s == 1:
                            norm(A, ps_ln1, x_in[A.par][:, :], ln1_c, ln1_sd, "ln1", 0, (ev("h1_ready"), A.t * BATCH))
                        if s == 5:
                            norm(A, ps_ln1, None, ln1_c, ln1_sd, "ln1", 1)
                        if s in (7, 8):
                            wait(dve, ev("shift_ready"), A.t + 1)
                            for m in range(4) if s == 7 else range(4, 7):
                                wait(dve, ev("proj_done"), (A.t - 1) * 4 + m // 2 + 1)
                                dve.scalar_tensor_tensor(out=bt(mixed[:, m, :]), in0=shift[:, :, :],
                                                         scalar=vec[:, MIX0 + m:MIX0 + m + 1], in1=h1[A.par][:, :, 1:STEPS + 1],
                                                         op0=ALU.mult, op1=ALU.add).then_inc(ev("mix_ready"), 1)
                        if s == 16:
                            wait(dve, ev("norm_sqrt"), A.t + 1)
                            dve.tensor_scalar(ab_sq[:, :, :], ab_sq[:, :, :], NORM_EPS, None, ALU.max).then_inc(ev("norm_max"), 1)
                            dve.wait_ge(ev("norm_max"), A.t + 1)
                            dve.reciprocal(ab_sq[:, :, :], ab_sq[:, :, :]).then_inc(ev("norm_recip"), 1)
                        if s == 17:
                            dve.wait_ge(ev("norm_recip"), A.t + 1)
                            wait(dve, ev("ab_copied"), (A.t + 1) * 2)
                            wait(dve, ev("push_mul"), (A.t - 1) * (L - 1))
                            wait(dve, ev("packed"), (A.t - 1) * 7)
                            dve.tensor_tensor(ar[A.par][:, 0, :, :].rearrange("p c l -> p (c l)"), ab_raw[:, 0, :], ab_sq[:, 0, :], ALU.mult)\
                                .then_inc(ev("a_ready"), 1)
                            wait(dve, ev("pull_mul"), (A.t - 1) * (L - 1))
                            wait(dve, ev("kb_copied"), (A.t - 1) * 2)
                            dve.tensor_tensor(b_raw[A.par][:, :, :].rearrange("p c l -> p (c l)"), ab_raw[:, 1, :], ab_sq[:, 1, :], ALU.mult)\
                                .then_inc(ev("b_ready"), 1)
                    if N2 is not None:
                        if s == 1:
                            norm(N2, ps_ln2, x2[N2.par][:, :], ln2_c, ln2_sd, "ln2", 0, (ev("h2_ready"), N2.t * BATCH))
                        if s == 5:
                            norm(N2, ps_ln2, None, ln2_c, ln2_sd, "ln2", 1)
                    if B is not None:
                        par = B.par
                        for n_, j in enumerate(PULLS):
                            if s == 1 + 2 * n_:
                                w_ = L - 1 - j
                                wait(dve, ev("pull_sum"), B.t * (L - 1) + n_ + 1)
                                dve.tensor_tensor(cols(q_rank, 2, CB, w_), cols(ps_sum, 2, CB, w_), per_chunk2(ar[par][:, 0], j, w_), ALU.mult)\
                                    .then_inc(ev("pull_rank"), 1)
                                dve.wait_ge(ev("pull_rank"), B.t * (L - 1) + n_ + 1)
                                wait(dve, ev("pull_dec"), B.t * (L - 1) + n_ + 1)
                                dve.tensor_tensor(q[:, :, :, j + 1:L], cols(q_rank, 2, CB, w_), cols(q_dec, 2, CB, w_), ALU.add)\
                                    .then_inc(ev("pull_add"), 1)
                        for n_, j in enumerate(PUSHES):
                            if s == 2 + 2 * n_:
                                wait(dve, ev("push_sum"), B.t * (L - 1) + n_ + 1)
                                dve.tensor_tensor(cols(k_rank, CB, j), cols(ps_sum, CB, j), per_chunk(b_raw[par], j, j), ALU.mult)\
                                    .then_inc(ev("push_rank"), 1)
                                dve.wait_ge(ev("push_rank"), B.t * (L - 1) + n_ + 1)
                                wait(dve, ev("push_dec"), B.t * (L - 1) + n_ + 1)
                                dve.tensor_tensor(kb[:, 0, :, 0:j], kb[:, 0, :, 0:j], cols(k_rank, CB, j), ALU.add).then_inc(ev("push_add"), 1)
                    if G is not None:
                        if 4 <= s < 4 + L:
                            j = s - 4
                            wait(dve, ev("s_terms"), G.t * L + j + 1)
                            if j == 0:
                                wait(dve, ev("gv_done"), (G.t + 1) * (L - 1))
                                wait(dve, ev(f"o_back{G.par}"), 16 * 8 * G.half)
                            ot = o_terms[:, :, :].rearrange("p (c j v) x -> p j c v x", c=C, j=L)[:, j]
                            dst = o_scan[G.par][:, :, :].rearrange("p v (c j) -> p j c v", j=L)[:, j]
                            dve.tensor_reduce(dst, ot, AX.X, ALU.add).then_inc(ev("o_reduced"), 1)
                        if s == 11:
                            norm(G, ps_gn, o_ch[G.par][:, :], gn_c, gn_sd, "gn", 0, (ev("gn_affine"), G.t))
                        if s == 15:
                            norm(G, ps_gn, None, gn_c, gn_sd, "gn", 1)
                        if s == 18:
                            wait(dve, ev("wo_done"), G.t + 1)
                            wait(dve, ev("x_biased"), (G.t + 1) * BATCH)
                            wait(dve, ev("x2_saved"), G.t - 1)
                            wait(dve, ev("ln2_mean"), G.t - 1)
                            for b in range(BATCH):
                                cs = slice(b * STEPS, (b + 1) * STEPS)
                                dve.scalar_tensor_tensor(out=x2[G.par][:, cs], in0=ps_gn[:, cs], scalar=mod[:, 2, b:b + 1],
                                                         in1=x_bias[:, cs], op0=ALU.mult, op1=ALU.add).then_inc(ev("x2_ready"), 1)
                    if N2 is not None:
                        if s == 11:
                            wait(dve, ev("rt_logit"), N2.t + 1)
                            lg = ps_rt[:, 0:TG * EXPERTS].rearrange("p (g e) -> p g e", g=TG)
                            dve.tensor_copy(rt_lg[:, :, 0:EXPERTS], lg).then_inc(ev("rt_copied"), 1)
                            dve.wait_ge(ev("rt_copied"), N2.t + 1)
                            dve.sem_inc(ev("passed"))
                            for g in range(TG):
                                dve.max(rt_top[:, g, :], rt_lg[:, g, 0:EXPERTS]).then_inc(ev("rt_topped"), 1)
                            dve.wait_ge(ev("rt_topped"), (N2.t + 1) * TG)
                            dve.tensor_tensor(rt_d[:, :, 0:EXPERTS], rt_lg[:, :, 0:EXPERTS], bc(rt_top[:, :, 0:1], [128, TG, EXPERTS]),
                                              ALU.subtract).then_inc(ev("rt_gap1"), 1)
                            dve.tensor_tensor(rt_d[:, :, EXPERTS:EXPERTS + 1], rt_top[:, :, 1:2], rt_top[:, :, 0:1], ALU.subtract)\
                                .then_inc(ev("rt_gap1"), 1)
                            for g in range(TG):
                                dve.max_index(rt_ix[:, g, :], rt_top[:, g, :], rt_lg[:, g, 0:EXPERTS]).then_inc(ev("rt_indexed"), 1)
                            dve.wait_ge(ev("rt_indexed"), (N2.t + 1) * TG)
                            dve.tensor_copy(rt_ixf[:, :, :], rt_ix[:, :, :]).then_inc(ev("rt_ix_f"), 1)
                        if s == 13:
                            wait(dve, ev("rt_tanh1"), N2.t + 1)
                            dve.tensor_scalar(rt_den[:, :, :], rt_th[:, :, :], -1.0, 1.0, ALU.mult, ALU.add).then_inc(ev("rt_dn"), 1)
                            dve.tensor_scalar(rt_num[:, :, :], rt_th[:, :, :], 1.0, None, ALU.add).then_inc(ev("rt_n"), 1)
                            dve.wait_ge(ev("rt_dn"), N2.t + 1)
                            dve.reciprocal(rt_inv[:, :, :], rt_den[:, :, :]).then_inc(ev("rt_i"), 1)
                            dve.wait_ge(ev("rt_n"), N2.t + 1)
                            dve.wait_ge(ev("rt_i"), N2.t + 1)
                            dve.tensor_tensor(rt_exp[:, :, :], rt_num[:, :, :], rt_inv[:, :, :], ALU.mult).then_inc(ev("rt_e"), 1)
                            dve.wait_ge(ev("rt_e"), N2.t + 1)
                            dve.tensor_reduce(rt_sum[:, :], rt_exp[:, :, 0:EXPERTS], AX.X, ALU.add).then_inc(ev("rt_s"), 1)
                            dve.tensor_scalar(rt_gap[:, :], rt_exp[:, :, EXPERTS], -1.0, 1.0, ALU.mult, ALU.add).then_inc(ev("rt_gapped"), 1)
                            dve.wait_ge(ev("rt_s"), N2.t + 1)
                            dve.reciprocal(rt_sinv[:, :], rt_sum[:, :]).then_inc(ev("rt_si"), 1)
                            dve.wait_ge(ev("rt_si"), N2.t + 1)
                            dve.wait_ge(ev("rt_gapped"), N2.t + 1)
                            dve.tensor_tensor(rt_u[:, :], rt_gap[:, :], rt_sinv[:, :], ALU.mult).then_inc(ev("rt_uu"), 1)
                        if s == 15:
                            wait(dve, ev("rt_tanh2"), N2.t + 1)
                            dve.tensor_scalar(rt_w1[:, :], rt_ut[:, :], 0.5, 0.5, ALU.mult, ALU.add).then_inc(ev("rt_weights"), 1)
                            dve.tensor_scalar(rt_w2[:, :], rt_ut[:, :], -0.5, 0.5, ALU.mult, ALU.add).then_inc(ev("rt_weights"), 1)
                            dve.wait_ge(ev("rt_weights"), (N2.t + 1) * 2)
                            dve.wait_ge(ev("rt_ix_f"), N2.t + 1)
                            for g in range(TG):
                                dve.tensor_scalar(rt_a[:, g, :], iota_f[:, :], rt_ixf[:, g, 0:1], rt_w1[:, g:g + 1], ALU.is_equal, ALU.mult)\
                                    .then_inc(ev("rt_wa"), 1)
                                dve.tensor_scalar(rt_b[:, g, :], iota_f[:, :], rt_ixf[:, g, 1:2], rt_w2[:, g:g + 1], ALU.is_equal, ALU.mult)\
                                    .then_inc(ev("rt_wb"), 1)
                            dve.wait_ge(ev("rt_wa"), (N2.t + 1) * TG)
                            dve.wait_ge(ev("rt_wb"), (N2.t + 1) * TG)
                            dve.tensor_tensor(rt_w[N2.par][:, :, :], rt_a[:, :, :], rt_b[:, :, :], ALU.add).then_inc(ev("rt_ready"), 1)
                    if E is not None:
                        for e in range(EXPERTS + 1):
                            if s == 2 * e + 3:
                                expert_out(E, e)
                    if O is not None and s == 2:
                        wait(dve, ev("out_turned"), O.t + 1)
                        wait(dve, ev("x2_saved"), O.t + 1)
                        wait(dve, ev(f"stored{O.par}"), 16 * O.half)
                        for b in range(BATCH):
                            cs = slice(b * STEPS, (b + 1) * STEPS)
                            dve.scalar_tensor_tensor(out=y_out[O.par][:, cs], in0=ps_out[:, cs], scalar=mod[:, 5, b:b + 1],
                                                     in1=x2_late[O.par][:, cs], op0=ALU.mult, op1=ALU.add).then_inc(ev("out_ready"), 1)

            run_tiles(dve, work)


def kernel(**inputs):
    import concourse.bacc as bacc
    from concourse.bass_utils import run_bass_kernel_spmd

    def a(name):
        return np.asarray(inputs[name])

    attn = "L0_attn_"
    order = np.arange(D).reshape(HEADS, 2, VH).transpose(1, 0, 2).reshape(D)
    w_of = {p: a(attn + "W_" + p) for p in PROJ + ["o"]}
    w_of["v"], w_of["g"], w_of["o"] = w_of["v"][order], w_of["g"][order], w_of["o"][:, order]
    w = np.stack([w_of[p].T for p in PROJ + ["o"]], axis=1)
    vec = np.zeros((128, VECS), np.float32)
    for i, p in enumerate(PROJ):
        vec[:, MIX0 + i] = a(attn + "x_" + p)
    vec[:, BO], vec[:, GNW], vec[:, GNB] = a(attn + "b_o"), a(attn + "gn_w")[order], a(attn + "gn_b")[order]
    vec[:ROUTER, BR1] = a("L0_ffn_br1")
    be1 = np.concatenate([a("L0_ffn_be1"), a("L0_ffn_bs1")[None]])
    vec[:, BE1:] = be1.reshape((EXPERTS + 1) * HB, 128).T
    w1 = np.concatenate([a("L0_ffn_We1"), a("L0_ffn_Ws1")[None]]).transpose(1, 0, 2)
    w2 = np.concatenate([a("L0_ffn_We2"), a("L0_ffn_Ws2")[None]]).reshape(EXPERTS + 1, HB, 128, 128).transpose(2, 0, 1, 3)
    x = a("L0_attn_x").reshape(BATCH, TILES, STEPS, D).transpose(3, 1, 0, 2).reshape(D, TILES * N)
    arrays = {
        "x": x, "w": w, "vec": vec, "cond": a("L0_c").T, "wmod": a("L0_wmod"), "wr1": a("L0_ffn_Wr1"),
        "wr2": np.concatenate([a("L0_ffn_Wr2"), a("L0_ffn_br2")[None]]), "w1": w1, "w2": w2,
        "be2": np.concatenate([a("L0_ffn_be2"), a("L0_ffn_bs2")[None]]),
    }
    arrays = {"in_" + k: np.ascontiguousarray(v) for k, v in arrays.items()}
    nc = bacc.Bacc("TRN2", target_bir_lowering=False, num_devices=1)
    aps = [nc.dram_tensor(k, v.shape, mybir.dt.float32, kind="ExternalInput").ap() for k, v in arrays.items()]
    out = nc.dram_tensor("out", (D, TILES * N), mybir.dt.float32, kind="ExternalOutput").ap()
    build(nc, *aps, out)
    r = run_bass_kernel_spmd(nc, [arrays], core_ids=[0])
    y = r.results[0]["out"]
    return np.ascontiguousarray(y.reshape(D, TILES, BATCH, STEPS).transpose(2, 1, 3, 0).reshape(BATCH, TIME, D))
```

```python
from contextlib import ExitStack

import numpy as np

import concourse.bass as bass
from concourse import mybir

BATCH, TIME, D = 4, 1024, 128
HEADS, K = 16, 8
HIDDEN, EXPERTS = 512, 8
ROUTER = D // 4
STEPS = 64
L = 4
TILES = TIME // STEPS
C = STEPS // L
CB = C * BATCH
N = BATCH * STEPS
TG = N // 128
HB = HIDDEN // 128
VH = K // 2
NG = L * (L - 1) // 2
Y0 = 0
X0 = Y0 + C * (L + 1)
B0 = X0 + STEPS
K0 = B0 + STEPS
G0 = K0 + STEPS
SENT = G0 + C * NG
RX = K + L - 1
SLOTS = 20
LN_EPS, GN_EPS, NORM_EPS, GATE_MIN = 1e-5, 6.4e-4, 1e-6, 0.25
PROJ = ["w", "a", "b", "r", "k", "v", "g"]
PACE = (0, 3, 6, 9)
AT = {
    "pe_turn": 0, "pe_mean": 1, "pe_var": 3, "pe_gn_mean": 11, "pe_gn_var": 14, "pe_wo": 18, "pe_pull": 1,
    "pe_push": 2, "pe_rt_hidden": 10, "pe_rt_logit": 12, "pe_norm": 14, "pe_rt_turn": 18, "pe_proj": 7,
    "pe_mean2": 0, "pe_var2": 4,
    "act_rt_relu": 12, "act_rt_tanh1": 14, "act_rt_tanh2": 16, "act_rt_copy": 19, "act_square": 2, "act_sqrt": 3,
    "act_save": 12, "act_affine": 5, "act_gate": 9, "act_x_bias": 8, "act_pack": 10, "act_gn_square": 11,
    "act_sqrt2": 14, "act_score": 3, "act_proj": 8, "act_square2": 2, "act_affine2": 6,
    "pool_u": 14, "pool_gv": 12, "pool_s": 1, "pool_shift": 5, "pool_split": 11, "pool_ar": 13, "pool_gn": 17,
    "pool_push": 0, "pool_pull": 0, "pool_ab": 17,
    "dve_center": 2, "dve_ln1": 4, "dve_ln2": 5, "dve_mix": 6, "dve_ab_recip": 16, "dve_rt_top": 13,
    "dve_rt_exp": 16, "dve_rt_weights": 17, "dve_pull": 2, "dve_push": 3, "dve_o": 3, "dve_gn_center": 12,
    "dve_gn": 15, "dve_x2": 19, "dve_out": 2, "dve_center2": 1,
}
MIX0, BO, GNW, GNB, BR1, BE1 = 0, 7, 8, 9, 10, 11
VECS = BE1 + (EXPERTS + 1) * HB
LAG_PROJ, LAG_CHUNK, LAG_SCAN, LAG_GN, LAG_LN2, LAG_FFN, LAG_OUT = -2, -1, 0, 1, 2, 3, 4


class Tile:
    def __init__(self, half, par):
        self.half, self.par, self.t = half, par, half * 2 + par


class Round:

    def __init__(self, i, tile_of):
        self.i, self.tile_of = i, tile_of

    def __call__(self, lag):
        return self.tile_of(lag)

    def before(self, lag):
        n = self.i - lag
        return max(0, min(TILES, n)) if isinstance(n, int) else n

    def through(self, lag):
        n = self.i - lag + 1
        return max(0, min(TILES, n)) if isinstance(n, int) else n


def run_tiles(eng, work):
    def fixed(i):
        def tile_of(lag):
            t = i - lag
            return Tile(t // 2, t % 2) if 0 <= t < TILES else None
        return Round(i, tile_of)

    first = LAG_OUT + 2
    last = TILES + LAG_PROJ
    for i in range(LAG_PROJ, first):
        work(fixed(i))
    with eng.Fori(first // 2, last // 2) as pair:
        for u in range(2):
            work(Round(pair * 2 + u, lambda lag, u=u: Tile(pair + (u - lag) // 2, (u - lag) % 2)))
    for i in range(last, TILES + LAG_OUT):
        work(fixed(i))


def build(nc, x_d, w_d, vec_d, cond_d, wmod_d, wr1_d, wr2_d, w1_d, w2_d, be2_d, out_d):
    F32, F32R, U32 = mybir.dt.float32, mybir.dt.float32r, mybir.dt.uint32
    ALU, ACT, AX = mybir.AluOpType, mybir.ActivationFunctionType, mybir.AxisListType
    ctx = ExitStack()
    with ctx:
        def sb(name, shape, dt=F32):
            return ctx.enter_context(nc.sbuf_tensor(name, shape, dt))

        def two(name, shape, dt=F32):
            return [sb(f"{name}{i}", shape, dt) for i in range(2)]

        def sem(name):
            return ctx.enter_context(nc.semaphore(name))

        w_proj = sb("w_proj", [128, 8, 128])
        vec = sb("vec", [128, VECS])
        cond = sb("cond", [128, BATCH])
        cond_act = sb("cond_act", [128, BATCH])
        wr1 = sb("wr1", [128, ROUTER])
        wr2 = sb("wr2", [ROUTER + 1, EXPERTS])
        w1_hi = sb("w1_hi", [128, EXPERTS + 1, HIDDEN], F32R)
        w1_lo = sb("w1_lo", [128, EXPERTS + 1, HIDDEN], F32R)
        w2 = sb("w2", [128, EXPERTS + 1, HB, 128])
        w1 = w2[:, :, :, :].rearrange("p e m n -> p e (m n)")
        be2 = sb("be2", [EXPERTS + 1, 128])
        ones_ch = sb("ones_ch", [128, 128])
        ones_hd = sb("ones_hd", [128, 128])
        mean_hd = sb("mean_hd", [128, 128])
        band = sb("band", [128, 128])
        ident = sb("ident", [128, 128])
        iota_i = sb("iota_i", [128, EXPERTS], mybir.dt.int32)
        iota_f = sb("iota_f", [128, EXPERTS])
        eps_ln = sb("eps_ln", [128, 1])
        eps_gn = sb("eps_gn", [128, 1])
        mod = sb("mod", [128, 6, BATCH])
        mod_sign = sb("mod_sign", [128, 2, BATCH])
        mod_abs = sb("mod_abs", [128, 2, BATCH])
        ga_bo = sb("ga_bo", [128, BATCH])

        x_in = two("x_in", [128, N])
        ln1_c = sb("ln1_c", [128, N])
        ln1_sd = sb("ln1_sd", [128, N])
        h1 = two("h1", [128, BATCH, STEPS + 1])
        shift = sb("shift", [128, BATCH, STEPS])
        mixed = sb("mixed", [128, 7, N])
        g_tanh = two("g_tanh", [128, N])
        gate_late = two("gate_late", [128, N])
        ab_raw = sb("ab_raw", [128, 2, N])
        ab_sq = sb("ab_sq", [128, 2, N])
        dec = two("dec", [128, CB, L])
        b_raw = two("b_raw", [128, CB, L])
        k_raw = two("k_raw", [128, CB, L])
        r_raw = two("r_raw", [128, CB, L])
        ar = two("ar", [128, 2, CB, L])
        v_send = two("v_send", [128, BATCH, STEPS])
        q = sb("q", [128, 2, CB, L])
        q_mul = sb("q_mul", [128, 2 * CB * (L - 1)])
        q_rank = sb("q_rank", [128, 2 * CB * (L - 1)])
        q_dec = sb("q_dec", [128, 2 * CB * (L - 1)])
        kb = sb("kb", [128, 2, CB, L])
        k_mul = sb("k_mul", [128, 2 * CB * (L - 1)])
        k_rank = sb("k_rank", [128, CB * (L - 1)])
        lam = sb("lam", [128, CB, L])
        send = sb("send", [128, BATCH, SENT])
        ops = two("ops", [128, K, SENT])
        vals = two("vals", [128, VH, STEPS])
        terms = sb("terms", [128, C, L + 3, VH * K])
        u_mul = sb("u_mul", [128, C, VH, K])
        z = two("z", [128, C, L * VH])
        state = two("state", [128, C + 1, VH * K])
        o_terms = sb("o_terms", [128, C * L * VH, RX])
        o_scan = two("o_scan", [128, VH, STEPS])
        o_ch = two("o_ch", [128, N])
        gn_c = sb("gn_c", [128, N])
        gn_sd = sb("gn_sd", [128, N])
        x_res = two("x_res", [128, N])
        x2 = two("x2", [128, N])
        x2_late = two("x2_late", [128, N])
        ln2_c = sb("ln2_c", [128, N])
        ln2_sd = sb("ln2_sd", [128, N])
        h2 = sb("h2", [128, N])
        h2_hi = two("h2_hi", [128, N], F32R)
        h2_lo = two("h2_lo", [128, N], F32R)
        rt_h = sb("rt_h", [ROUTER + 1, N])
        rt_lg = sb("rt_lg", [128, TG, EXPERTS + 1])
        rt_top = sb("rt_top", [128, TG, 8])
        rt_ix = sb("rt_ix", [128, TG, 8], U32)
        rt_ixf = sb("rt_ixf", [128, TG, 8])
        rt_d = sb("rt_d", [128, TG, EXPERTS + 1])
        rt_th = sb("rt_th", [128, TG, EXPERTS + 1])
        rt_num = sb("rt_num", [128, TG, EXPERTS + 1])
        rt_den = sb("rt_den", [128, TG, EXPERTS + 1])
        rt_inv = sb("rt_inv", [128, TG, EXPERTS + 1])
        rt_exp = sb("rt_exp", [128, TG, EXPERTS + 1])
        rt_sum = sb("rt_sum", [128, TG])
        rt_sinv = sb("rt_sinv", [128, TG])
        rt_gap = sb("rt_gap", [128, TG])
        rt_u = sb("rt_u", [128, TG])
        rt_ut = sb("rt_ut", [128, TG])
        rt_w1 = sb("rt_w1", [128, TG])
        rt_w2 = sb("rt_w2", [128, TG])
        rt_a = sb("rt_a", [128, TG, EXPERTS])
        rt_w = two("rt_wgt", [128, TG, EXPERTS])
        rt_b = sb("rt_b", [128, TG, EXPERTS])
        rt_wt = two("rt_wt", [EXPERTS + 1, N])
        hid = two("hid", [128, HB, N])
        wmod = hid[0][:, :, :].rearrange("p m n -> p (m n)")[:, 0:6 * 128]
        acc = two("acc", [128, TG * 128])

        bank = [ctx.enter_context(nc.psum_tensor(f"bank{i}", [128, 512], F32)) for i in range(8)]
        ps_hid = [bank[m // 2][:, (m % 2) * N:(m % 2) * N + N] for m in range(HB)]
        ps_y = [bank[2][:, 0:N], bank[3][:, 0:N]]
        ps_proj = [bank[4 + (m // 2) % 2][:, (m % 2) * N:(m % 2) * N + N] for m in range(7)]
        ps_out = bank[4][:, 0:N]
        ps_ln1, ps_ln2, ps_gn = bank[5][:, 0:N], bank[6][:, N:2 * N], bank[6][:, 0:N]
        ps_sum, ps_rt = bank[7], bank[7][:, 0:N]

        S = {}

        def ev(name):
            if name not in S:
                S[name] = sem(name)
            return S[name]

        s_names = """w_loaded small_loaded w1_loaded w2_loaded w1_high w1_low x_loaded0 x_loaded1 xr_loaded0 xr_loaded1 sent0 sent1 vsent0 vsent1 o_back0 o_back1 stored0 stored1
            const pconst band_low band_high mod_step cond_silu mod_mm mod_ready
            ln1_mean ln1_center ln1_square ln1_var ln1_sqrt ln1_recip ln1_norm h1_ready shift_ready mix_ready proj_done
            w_tanh_done d_ready ab_copied ab_squared r_ready k_ready v_ready g_tanh_done gate_copied norm_sum norm_sqrt
            norm_max norm_recip a_ready b_ready
            q_copied kb_copied pull_mul pull_sum pull_rank pull_dec pull_add push_mul push_sum push_rank push_dec push_add
            score_out lam_mul packed ar_r h1_edge
            u_first u_mul_done u_add gv_done dots z_done outer state_ready state_copied s_terms o_reduced
            gn_mean gn_center gn_square gn_var gn_sqrt gn_recip gn_norm gn_affine gn_gated wo_done x_biased x2_ready x2_saved
            ln2_mean ln2_center ln2_square ln2_var ln2_sqrt ln2_recip ln2_norm h2_ready h2_high h2_low
            rt_hid rt_relu rt_logit rt_copied rt_topped rt_indexed rt_ix_f rt_gap1 rt_tanh1 rt_n rt_dn rt_i rt_e rt_s rt_si
            rt_gapped rt_uu rt_tanh2 rt_weights rt_wa rt_wb rt_ready rt_turned rt_wt_ready
            hid_mm hid_act y_mm y_acc out_turned out_ready passed""".split()
        for n_ in s_names:
            ev(n_)

        def wait(eng, sem_, value):
            if isinstance(value, int):
                if value > 0:
                    eng.wait_ge(sem_, value)
                return
            eng.wait_ge(sem_, value)
            if eng.engine in (nc.gpsimd.engine, nc.sync.engine):
                eng.sem_inc(ev("passed"))

        def bt(ap):
            return ap.rearrange("p (b t) -> p b t", b=BATCH)

        def bc(ap, shape):
            return ap.to_broadcast(shape)

        def per_chunk(ap, j, n):
            return bc(ap[:, :, j:j + 1], [128, CB, n])

        def per_chunk2(ap, j, n):
            return bc(ap[:, :, j:j + 1].rearrange("p (o c) l -> p o c l", o=1), [128, 2, CB, n])

        def cols(ap, *dims):
            m = int(np.prod(dims))
            v = ap[:, 0:m]
            if len(dims) == 2:
                return v.rearrange("p (a b) -> p a b", a=dims[0])
            return v.rearrange("p (a b c) -> p a b c", a=dims[0], b=dims[1])

        def sent_view(at, width):
            return send[:, :, at:at + C * width].rearrange("p b (c w) -> p b c w", w=width)

        def bcl(ap, lo, hi):
            return ap[:, :, lo:hi].rearrange("p (b c) l -> p b c l", b=BATCH)

        def op_view(par, at, width, lo, hi):
            return ops[par][:, :, at:at + C * width].rearrange("p k (c w) -> p k c w", w=width)[:, :, :, lo:hi]

        PULLS = list(range(L - 2, -1, -1))
        PUSHES = list(range(1, L))
        block = ctx.enter_context(nc.Block())

        @block.sync
        def _(sp):
            for dst, src in ((cond[:, :], cond_d[:, :]), (wmod[:, :], wmod_d[:, :]), (vec[:, :], vec_d[:, :])):
                sp.dma_start(dst, src).then_inc(ev("w_loaded"), 16)
            for dst, src, name in ((x_in[0][:, :], x_d[:, 0:N], "x_loaded0"), (w_proj[:, :, :], w_d[:, :, :], "small_loaded"),
                      (wr1[:, :], wr1_d[:, :], "small_loaded"), (wr2[:, :], wr2_d[:, :], "small_loaded"),
                      (be2[:, :], be2_d[:, :], "small_loaded")):
                sp.dma_start(dst, src).then_inc(ev(name), 16)

            def work(at):
                t = at(LAG_PROJ)
                if t is not None and not (isinstance(t.t, int) and t.t == 0):
                    wait(sp, ev("ln1_center"), t.t - 1)
                    sp.dma_start(x_in[t.par][:, :], x_d[:, bass.ds(t.t * N, N)]).then_inc(ev(f"x_loaded{t.par}"), 16)
                if t is not None and isinstance(t.t, int) and t.t == 0:
                    sp.dma_start(w1[:, :, :], w1_d[:, :, :]).then_inc(ev("w1_loaded"), 16)
                if isinstance(at.i, int) and at.i == LAG_PROJ + 2:
                    sp.wait_ge(ev("w1_low"), EXPERTS + 1)
                    sp.dma_start(w2[:, :, :, :], w2_d[:, :, :, :]).then_inc(ev("w2_loaded"), 16)
                t = at(LAG_CHUNK)
                if t is not None:
                    wait(sp, ev("v_ready"), t.t + 1)
                    wait(sp, ev("gv_done"), (t.t - 1) * (L - 1))
                    for b in range(BATCH):
                        for hf in range(2):
                            p0 = 32 * b + 16 * hf
                            sp.dma_start(vals[t.par][p0:p0 + 16, :, :], v_send[t.par][64 * hf:64 * hf + 64, b, :]).then_inc(ev(f"vsent{t.par}"), 16)
                t = at(LAG_OUT)
                if t is not None:
                    wait(sp, ev("out_ready"), (t.t + 1) * BATCH)
                    sp.dma_start(out_d[:, bass.ds(t.t * N, N)], x2_late[t.par][:, :]).then_inc(ev(f"stored{t.par}"), 16)
                t = at(LAG_GN)
                if t is not None:
                    wait(sp, ev("x2_ready"), (t.t - 1) * BATCH)
                    sp.dma_start(x_res[t.par][:, :], x_d[:, bass.ds(t.t * N, N)]).then_inc(ev(f"xr_loaded{t.par}"), 16)
                    wait(sp, ev("o_reduced"), (t.t + 1) * L)
                    wait(sp, ev("gn_center"), t.t - 1)
                    for b in range(BATCH):
                        for hf in range(2):
                            p0 = 32 * b + 16 * hf
                            sp.dma_start(o_ch[t.par][64 * hf:64 * hf + 64, b * STEPS:(b + 1) * STEPS], o_scan[t.par][p0:p0 + 16, :, :]).then_inc(ev(f"o_back{t.par}"), 16)
                t = at(LAG_CHUNK)
                if t is not None:
                    wait(sp, ev("packed"), (t.t + 1) * 7)
                    wait(sp, ev("score_out"), (t.t + 1) * (L - 1))
                    wait(sp, ev("outer"), (t.t - 1) * C)
                    wait(sp, ev("s_terms"), (t.t - 1) * L)
                    for b in range(BATCH):
                        for hf in range(2):
                            p0 = 32 * b + 16 * hf
                            sp.dma_start(ops[t.par][p0:p0 + 16, :, :],
                                         send[:, b, :]).then_inc(ev(f"sent{t.par}"), 16)

            run_tiles(sp, work)
            sp.wait_ge(ev("stored0"), 16 * (TILES // 2))
            sp.wait_ge(ev("stored1"), 16 * (TILES // 2))

        @block.tensor
        def _(pe):
            pe.wait_ge(ev("w_loaded"), 16 * 3)
            pe.wait_ge(ev("small_loaded"), 16 * 4)
            pe.wait_ge(ev("pconst"), 8)
            pe.wait_ge(ev("cond_silu"), 1)
            for m in range(6):
                last = pe.matmul(ps_rt[:, m * BATCH:(m + 1) * BATCH], wmod[:, m * 128:(m + 1) * 128], cond_act[:, :],
                                 start=True, stop=True)
            last.then_inc(ev("mod_mm"), 1)

            def stats(ps, src, ones, name):
                pe.matmul(ps, ones, src, start=True, stop=True).then_inc(ev(name), 1)

            def hidden(t, e):
                if e == 0:
                    wait(pe, ev("h2_low"), t.t + 1)
                    if isinstance(t.t, int) and t.t == 0:
                        pe.wait_ge(ev("w2_loaded"), 16)
                        pe.wait_ge(ev("w1_low"), EXPERTS + 1)
                for m in range(HB):
                    if m % 2 == 0:
                        wait(pe, ev("hid_act"), (t.t * (EXPERTS + 1) + e - 1) * HB + m + 2)
                    cs = slice(m * 128, (m + 1) * 128)
                    pe.matmul(ps_hid[m], w1_lo[:, e, cs], h2_hi[t.par][:, :], start=True, stop=False)
                    pe.matmul(ps_hid[m], w1_hi[:, e, cs], h2_lo[t.par][:, :], start=False, stop=False)
                    last = pe.matmul(ps_hid[m], w1_hi[:, e, cs], h2_hi[t.par][:, :], start=False, stop=True)
                    if m % 2 == 1:
                        last.then_inc(ev("hid_mm"), 1)

            def down(t, e):
                last_e = EXPERTS
                wait(pe, ev("y_acc"), (t.t * (EXPERTS + 1) + e - 1) * TG)
                for g in range(TG):
                    out = ps_y[(t.par + e) % 2][:, g * 128:(g + 1) * 128]
                    for m in range(HB):
                        if g == 0:
                            wait(pe, ev("hid_act"), (t.t * (EXPERTS + 1) + e) * HB + m + 1)
                        last = pe.matmul(out, hid[(t.par + e) % 2][:, m, g * 128:(g + 1) * 128], w2[:, e, m, :],
                                         start=(m == 0), stop=(m == HB - 1 and e != last_e))
                    if e == last_e:
                        wait(pe, ev("rt_wt_ready"), t.t + 1)
                        last = pe.matmul(out, rt_wt[t.par][:, g * 128:(g + 1) * 128], be2[:, :], start=False, stop=True)
                last.then_inc(ev("y_mm"), 1)

            def work(at):
                A, B, G, N2, E, O = (at(x) for x in (LAG_PROJ, LAG_CHUNK, LAG_GN, LAG_LN2, LAG_FFN, LAG_OUT))
                for s in range(SLOTS):
                    if E is not None:
                        if s == 0:
                            hidden(E, 0)
                        if s % 2 == 1 and (s + 1) // 2 <= EXPERTS:
                            hidden(E, (s + 1) // 2)
                        if s % 2 == 0 and 2 <= s:
                            down(E, (s - 2) // 2)
                    if O is not None and s == AT["pe_turn"]:
                        wait(pe, ev("y_acc"), (O.t + 1) * (EXPERTS + 1) * TG)
                        wait(pe, ev("v_ready"), at.before(LAG_PROJ))
                        for g in range(TG):
                            last = pe.matmul(ps_out[:, g * 128:(g + 1) * 128],
                                             acc[O.par][:, g * 128:(g + 1) * 128], ident[:, :],
                                             start=True, stop=True)
                        last.then_inc(ev("out_turned"), 1)
                    if A is not None and s == AT["pe_mean"]:
                        wait(pe, ev(f"x_loaded{A.par}"), 16 * (A.half + 1))
                        wait(pe, ev("g_tanh_done"), A.t)
                        stats(ps_ln1, x_in[A.par][:, :], ones_ch[:, :], "ln1_mean")
                    if A is not None and s == AT["pe_var"]:
                        wait(pe, ev("ln1_center"), A.t + 1)
                        wait(pe, ev("ln1_square"), A.t + 1)
                        stats(ps_ln1, ln1_sd[:, :], ones_ch[:, :], "ln1_var")
                    if N2 is not None and s == AT["pe_mean2"]:
                        wait(pe, ev("x2_ready"), at.before(LAG_GN) * BATCH)
                        wait(pe, ev("ln2_sqrt"), N2.t)
                        stats(ps_ln2, x2[N2.par][:, :], ones_ch[:, :], "ln2_mean")
                    if N2 is not None and s == AT["pe_var2"]:
                        wait(pe, ev("ln2_center"), N2.t + 1)
                        wait(pe, ev("ln2_square"), N2.t + 1)
                        stats(ps_ln2, ln2_sd[:, :], ones_ch[:, :], "ln2_var")
                    if G is not None:
                        if s == AT["pe_gn_mean"]:
                            wait(pe, ev(f"o_back{G.par}"), 16 * 8 * (G.half + 1))
                            wait(pe, ev("ln2_sqrt"), at.through(LAG_LN2))
                            wait(pe, ev("x2_ready"), G.t * BATCH)
                            stats(ps_gn, o_ch[G.par][:, :], mean_hd[:, :], "gn_mean")
                        if s == AT["pe_gn_var"]:
                            wait(pe, ev("gn_square"), G.t + 1)
                            wait(pe, ev("gn_center"), G.t + 1)
                            stats(ps_gn, gn_sd[:, :], mean_hd[:, :], "gn_var")
                        if s == AT["pe_wo"]:
                            wait(pe, ev("gn_gated"), G.t + 1)
                            wait(pe, ev("gn_sqrt"), G.t + 1)
                            stats(ps_gn, gn_c[:, :], w_proj[:, 7, :], "wo_done")
                    if A is not None and 0 <= s - AT["pe_proj"] < 4:
                        for m in ((0, 1), (2, 3), (4, 5), (6,))[s - AT["pe_proj"]]:
                            wait(pe, ev("mix_ready"), A.t * 7 + m + 1)
                            if m == 0:
                                wait(pe, ev("v_ready"), A.t)
                                wait(pe, ev("out_ready"), at.through(LAG_OUT) * BATCH)
                            if m == 2:
                                wait(pe, ev("ln1_sqrt"), A.t + 1)
                            if m == 4:
                                wait(pe, ev("ab_squared"), A.t * 2 + 1)
                            if m == 6:
                                wait(pe, ev("r_ready"), A.t + 1)
                            last = pe.matmul(ps_proj[m], w_proj[:, m, :], mixed[:, m, :], start=True, stop=True)
                        last.then_inc(ev("proj_done"), 1)
                    if B is not None:
                        for n_, j in enumerate(PULLS):
                            if s == AT["pe_pull"] + PACE[n_]:
                                m = 2 * CB * (L - 1 - j)
                                wait(pe, ev("pull_mul"), B.t * (L - 1) + n_ + 1)
                                if n_ == 0:
                                    wait(pe, ev("norm_sqrt"), at.before(LAG_PROJ))
                                    wait(pe, ev("rt_wt_ready"), at.before(LAG_LN2))
                                wait(pe, ev("score_out"), B.t * (L - 1) + n_)
                                pe.matmul(ps_sum[:, 0:m], ones_hd[:, :], q_mul[:, 0:m], start=True, stop=True)\
                                    .then_inc(ev("pull_sum"), 1)
                        for n_, j in enumerate(PUSHES):
                            if s == AT["pe_push"] + PACE[n_]:
                                m = 2 * CB * j
                                wait(pe, ev("push_mul"), B.t * (L - 1) + n_ + 1)
                                wait(pe, ev("pull_rank"), B.t * (L - 1) + n_ + 1)
                                pe.matmul(ps_sum[:, 0:m], ones_hd[:, :], k_mul[:, 0:m], start=True, stop=True)\
                                    .then_inc(ev("push_sum"), 1)
                    if N2 is not None:
                        if s == AT["pe_rt_hidden"]:
                            wait(pe, ev("h2_ready"), (N2.t + 1) * BATCH)
                            wait(pe, ev("score_out"), at.through(LAG_CHUNK) * (L - 1))
                            wait(pe, ev("norm_sqrt"), at.before(LAG_PROJ))
                            wait(pe, ev("rt_wt_ready"), N2.t)
                            pe.matmul(ps_rt[0:ROUTER, :], wr1[:, :], h2[:, :], start=True, stop=True)\
                                .then_inc(ev("rt_hid"), 1)
                        if s == AT["pe_rt_logit"]:
                            wait(pe, ev("rt_relu"), N2.t + 1)
                            for g in range(TG):
                                last = pe.matmul(ps_rt[:, g * EXPERTS:(g + 1) * EXPERTS], rt_h[:, g * 128:(g + 1) * 128],
                                                 wr2[:, :], start=True, stop=True)
                            last.then_inc(ev("rt_logit"), 1)
                    if A is not None and s == AT["pe_norm"]:
                        wait(pe, ev("ab_squared"), (A.t + 1) * 2)
                        wait(pe, ev("score_out"), at.through(LAG_CHUNK) * (L - 1))
                        wait(pe, ev("rt_copied"), at.through(LAG_LN2))
                        wait(pe, ev("rt_wt_ready"), at.before(LAG_LN2))
                        pe.matmul(ps_sum[:, :], ones_hd[:, :], ab_sq[:, :, :].rearrange("p a n -> p (a n)"),
                                  start=True, stop=True).then_inc(ev("norm_sum"), 1)
                    if N2 is not None and s == AT["pe_rt_turn"]:
                        wait(pe, ev("rt_ready"), N2.t + 1)
                        wait(pe, ev("norm_sqrt"), at.through(LAG_PROJ))
                        for g in range(TG):
                            last = pe.matmul(ps_rt[0:EXPERTS, g * 128:(g + 1) * 128], rt_w[N2.par][:, g, :], ident[:, :],
                                             start=True, stop=True)
                        last.then_inc(ev("rt_turned"), 1)

            run_tiles(pe, work)

        @block.scalar
        def _(act):
            act.wait_ge(ev("w_loaded"), 16 * 3)
            act.activation(cond_act[:, :], cond[:, :], ACT.Silu).then_inc(ev("cond_silu"), 1)
            act.wait_ge(ev("mod_mm"), 1)
            act.activation(mod[:, :, :].rearrange("p m b -> p (m b)"), ps_rt[:, 0:6 * BATCH], ACT.Copy).then_inc(ev("const"), 1)
            act.wait_ge(ev("const"), 1)
            for n_, m in enumerate((2, 5)):
                act.activation(mod_abs[:, n_, :], mod[:, m, :], ACT.Abs).then_inc(ev("const"), 1)
            act.wait_ge(ev("pconst"), 8)
            act.wait_ge(ev("mod_ready"), 1)

            def work(at):
                A, B, R, G, N2, E = (at(x) for x in (LAG_PROJ, LAG_CHUNK, LAG_SCAN, LAG_GN, LAG_LN2, LAG_FFN))

                def affine(dst, src, scale, bias, name):
                    for b in range(BATCH):
                        act.activation(dst(b), src[:, b * STEPS:(b + 1) * STEPS], ACT.Identity, bias=bias[:, b:b + 1],
                                       scale=1.0 if scale is None else scale[:, b:b + 1]).then_inc(ev(name), 1)

                def silu(e):
                    for m in range(HB):
                        if m % 2 == 0:
                            wait(act, ev("hid_mm"), (E.t * (EXPERTS + 1) + e) * 2 + m // 2 + 1)
                        wait(act, ev("y_mm"), E.t * (EXPERTS + 1) + e - 1)
                        act.activation(hid[(E.par + e) % 2][:, m, :], ps_hid[m], ACT.Silu,
                                       bias=vec[:, BE1 + e * HB + m:BE1 + e * HB + m + 1]).then_inc(ev("hid_act"), 1)


                if isinstance(at.i, int) and at.i == LAG_PROJ + 1:
                    act.wait_ge(ev("w1_loaded"), 16)
                    for e in range(EXPERTS + 1):
                        act.activation(w1_hi[:, e, :], w1[:, e, :], ACT.Copy).then_inc(ev("w1_high"), 1)
                for s in range(SLOTS):
                    if E is not None:
                        if s == 0:
                            silu(0)
                        if s % 2 == 1 and (s + 1) // 2 <= EXPERTS:
                            silu((s + 1) // 2)
                    if N2 is not None:
                        if s == AT["act_rt_relu"]:
                            wait(act, ev("rt_hid"), N2.t + 1)
                            wait(act, ev("rt_logit"), N2.t)
                            act.activation(rt_h[0:ROUTER, :], ps_rt[0:ROUTER, :], ACT.Relu, bias=vec[0:ROUTER, BR1:BR1 + 1])\
                                .then_inc(ev("rt_relu"), 1)
                        if s == AT["act_rt_tanh1"]:
                            wait(act, ev("rt_gap1"), (N2.t + 1) * 2)
                            act.activation(rt_th[:, :, :], rt_d[:, :, :], ACT.Tanh, scale=0.5).then_inc(ev("rt_tanh1"), 1)
                        if s == AT["act_rt_tanh2"]:
                            wait(act, ev("rt_uu"), N2.t + 1)
                            act.activation(rt_ut[:, :], rt_u[:, :], ACT.Tanh, scale=0.25).then_inc(ev("rt_tanh2"), 1)
                        if s == AT["act_rt_copy"]:
                            wait(act, ev("rt_turned"), N2.t + 1)
                            wait(act, ev("y_mm"), (N2.t - 1) * (EXPERTS + 1))
                            act.activation(rt_wt[N2.par][0:EXPERTS, :], ps_rt[0:EXPERTS, :], ACT.Copy).then_inc(ev("rt_wt_ready"), 1)
                    if A is not None and s == AT["act_square"]:
                        wait(act, ev("ln1_center"), A.t + 1)
                        act.activation(ln1_sd[:, :], ln1_c[:, :], ACT.Square).then_inc(ev("ln1_square"), 1)
                    if s == AT["act_square2"]:
                        if N2 is not None:
                            wait(act, ev("ln2_center"), N2.t + 1)
                            act.activation(ln2_sd[:, :], ln2_c[:, :], ACT.Square).then_inc(ev("ln2_square"), 1)
                    if s == AT["act_sqrt"]:
                        if A is not None:
                            wait(act, ev("ln1_var"), A.t + 1)
                            act.activation(ln1_sd[:, :], ps_ln1, ACT.Sqrt, bias=eps_ln[:, 0:1]).then_inc(ev("ln1_sqrt"), 1)
                        if N2 is not None:
                            wait(act, ev("ln2_var"), N2.t + 1)
                            act.activation(ln2_sd[:, :], ps_ln2, ACT.Sqrt, bias=eps_ln[:, 0:1]).then_inc(ev("ln2_sqrt"), 1)
                    if N2 is not None and s == AT["act_save"]:
                        wait(act, ev("x2_ready"), (N2.t + 1) * BATCH)
                        wait(act, ev(f"stored{N2.par}"), 16 * N2.half)
                        act.activation(x2_late[N2.par][:, :], x2[N2.par][:, :], ACT.Copy).then_inc(ev("x2_saved"), 1)
                    if s == AT["act_affine"]:
                        if A is not None:
                            wait(act, ev("ln1_norm"), A.t + 1)
                            wait(act, ev("mix_ready"), (A.t - 1) * 7)
                            wait(act, ev("h1_edge"), A.t - 1)
                            wait(act, ev("shift_ready"), A.t - 1)
                            affine(lambda b: h1[A.par][:, b, 1:STEPS + 1], ln1_c, mod[:, 1, :], mod[:, 0, :], "h1_ready")
                    if s == AT["act_affine2"]:
                        if N2 is not None:
                            wait(act, ev("ln2_norm"), N2.t + 1)
                            wait(act, ev("rt_hid"), N2.t)
                            wait(act, ev("h2_low"), N2.t)
                            affine(lambda b: h2[:, b * STEPS:(b + 1) * STEPS], ln2_c, mod[:, 4, :], mod[:, 3, :], "h2_ready")
                            wait(act, ev("h2_ready"), (N2.t + 1) * BATCH)
                            wait(act, ev("hid_mm"), (N2.t - 1) * (EXPERTS + 1) * 2)
                            wait(act, ev("h2_low"), N2.t - 1)
                            act.activation(h2_hi[N2.par][:, :], h2[:, :], ACT.Copy).then_inc(ev("h2_high"), 1)
                    if R is not None and s == AT["act_gate"]:
                        wait(act, ev("g_tanh_done"), R.t + 1)
                        wait(act, ev("gn_gated"), R.t - 1)
                        act.activation(gate_late[R.par][:, :], g_tanh[R.par][:, :], ACT.Copy, bias=0.5, scale=0.5)\
                            .then_inc(ev("gate_copied"), 1)
                    if G is not None and s == AT["act_x_bias"]:
                        wait(act, ev(f"xr_loaded{G.par}"), 16 * (G.half + 1))
                        affine(lambda b: x_res[G.par][:, b * STEPS:(b + 1) * STEPS], x_res[G.par], None, ga_bo, "x_biased")
                    if B is not None and s == AT["act_pack"]:
                        wait(act, ev("lam_mul"), (B.t + 1) * (L - 1))
                        act.activation(sent_view(Y0, L + 1)[:, :, :, 0:1], bcl(lam, L - 1, L), ACT.Copy).then_inc(ev("packed"), 1)
                        act.activation(sent_view(X0, L)[:, :, :, L - 1:L], bcl(r_raw[B.par], L - 1, L), ACT.Copy).then_inc(ev("packed"), 1)
                        act.activation(sent_view(Y0, L + 1)[:, :, :, 1:2], bcl(ar[B.par][:, 0], 0, 1), ACT.Copy).then_inc(ev("packed"), 1)
                        wait(act, ev("pull_add"), (B.t + 1) * (L - 1))
                        act.activation(sent_view(Y0, L + 1)[:, :, :, 2:L + 1], bcl(q[:, 0], 1, L), ACT.Copy).then_inc(ev("packed"), 1)
                        act.activation(sent_view(X0, L)[:, :, :, 0:L - 1], bcl(q[:, 1], 1, L), ACT.Copy).then_inc(ev("packed"), 1)
                        wait(act, ev("push_add"), (B.t + 1) * (L - 1))
                        wait(act, ev("push_dec"), (B.t + 1) * (L - 1))
                        act.activation(sent_view(K0, L), bcl(kb[:, 0], 0, L), ACT.Copy).then_inc(ev("packed"), 1)
                        act.activation(sent_view(B0, L), bcl(kb[:, 1], 0, L), ACT.Copy).then_inc(ev("packed"), 1)
                    if A is not None and 0 <= s - AT["act_proj"] < 4:
                        for m in ((0, 1), (2, 3), (4, 5), (6,))[s - AT["act_proj"]]:
                            what = PROJ[m]
                            wait(act, ev("proj_done"), A.t * 4 + m // 2 + 1)
                            if what == "w":
                                wait(act, ev("pull_dec"), (A.t - 1) * (L - 1))
                                wait(act, ev("lam_mul"), (A.t - 1) * (L - 1))
                                wait(act, ev("push_dec"), (A.t - 1) * (L - 1))
                                d = dec[A.par][:, :, :].rearrange("p c l -> p (c l)")
                                act.activation(d, ps_proj[m], ACT.Tanh, scale=-0.5).then_inc(ev("w_tanh_done"), 1)
                                act.wait_ge(ev("w_tanh_done"), A.t + 1)
                                act.activation(d, d, ACT.Copy, bias=0.5, scale=0.5).then_inc(ev("d_ready"), 1)
                            elif what in "ab":
                                wait(act, ev("a_ready" if what == "a" else "b_ready"), A.t)
                                wait(act, ev("norm_sum"), A.t)
                                act.activation(ab_raw[:, m - 1, :], ps_proj[m], ACT.Copy).then_inc(ev("ab_copied"), 1)
                                act.activation(ab_sq[:, m - 1, :], ps_proj[m], ACT.Square).then_inc(ev("ab_squared"), 1)
                            elif what == "r":
                                wait(act, ev("ar_r"), A.t - 1)
                                act.activation(r_raw[A.par][:, :, :].rearrange("p c l -> p (c l)"), ps_proj[m], ACT.Copy)\
                                    .then_inc(ev("r_ready"), 1)
                            elif what == "k":
                                wait(act, ev("kb_copied"), (A.t - 1) * 2)
                                act.activation(k_raw[A.par][:, :, :].rearrange("p c l -> p (c l)"), ps_proj[m], ACT.Tanh)\
                                    .then_inc(ev("k_ready"), 1)
                            elif what == "v":
                                wait(act, ev(f"vsent{A.par}"), 16 * 8 * A.half)
                                act.activation(v_send[A.par][:, :, :], bt(ps_proj[m]), ACT.Copy).then_inc(ev("v_ready"), 1)
                            else:
                                act.activation(g_tanh[A.par][:, :], ps_proj[m], ACT.Tanh, scale=0.5).then_inc(ev("g_tanh_done"), 1)
                    if B is not None:
                        for n_, j in enumerate(PUSHES):
                            if s == AT["act_score"] + PACE[n_]:
                                wait(act, ev("push_sum"), B.t * (L - 1) + n_ + 1)
                                wait(act, ev("push_rank"), B.t * (L - 1) + n_ + 1)
                                if n_ == 0:
                                    wait(act, ev(f"sent{1 - B.par}"), 16 * 8 * (B.half + B.par))
                                src = ps_sum[:, CB * j:2 * CB * j].rearrange("p (b c s) -> p b c s", b=BATCH, s=j)
                                act.activation(sent_view(G0, NG)[:, :, :, j * (j - 1) // 2:j * (j + 1) // 2], src, ACT.Copy)\
                                    .then_inc(ev("score_out"), 1)
                    if G is not None and s == AT["act_gn_square"]:
                        wait(act, ev("gn_center"), G.t + 1)
                        wait(act, ev("gn_norm"), G.t)
                        act.activation(gn_sd[:, :], gn_c[:, :], ACT.Square).then_inc(ev("gn_square"), 1)
                    if s == AT["act_sqrt2"]:
                        if G is not None:
                            wait(act, ev("gn_var"), G.t + 1)
                            act.activation(gn_sd[:, :], ps_gn, ACT.Sqrt, bias=eps_gn[:, 0:1]).then_inc(ev("gn_sqrt"), 1)
                        if A is not None:
                            wait(act, ev("norm_sum"), A.t + 1)
                            wait(act, ev("b_ready"), A.t)
                            act.activation(ab_sq[:, :, :].rearrange("p a n -> p (a n)"), ps_sum[:, :], ACT.Sqrt).then_inc(ev("norm_sqrt"), 1)

            run_tiles(act, work)

        @block.gpsimd
        def _(pool):
            pool.memset(ones_ch[:, :], 1.0 / D).then_inc(ev("pconst"), 1)
            pool.memset(ones_hd[:, :], 1.0)
            pool.memset(mean_hd[:, :], 1.0 / K)
            pool.memset(band[:, :], 1.0 / K)
            pool.memset(ident[:, :], 0.0)
            pool.memset(rt_h[:, :], 1.0)
            pool.memset(rt_wt[0][:, :], 1.0)
            pool.memset(rt_wt[1][:, :], 1.0)
            pool.memset(eps_ln[:, :], LN_EPS).then_inc(ev("pconst"), 1)
            pool.memset(eps_gn[:, :], GN_EPS).then_inc(ev("pconst"), 1)
            pool.memset(o_terms[:, :, :], 0.0)
            for i in range(2):
                pool.memset(h1[i][:, :, :], 0.0)
                pool.memset(state[i][:, :, :], 0.0)
            pool.iota(iota_i[:, :], pattern=[[1, EXPERTS]], base=0, channel_multiplier=0).then_inc(ev("pconst"), 1)
            pool.wait_ge(ev("pconst"), 4)
            pool.tensor_copy(iota_f[:, :], iota_i[:, :]).then_inc(ev("pconst"), 1)
            groups = [(ones_hd[:, :].rearrange("p (h k) -> p h k", k=K), [[K, HEADS], [0, K]], 0, K)]
            for f, m in enumerate((mean_hd, band)):
                groups.append((m[:, :].rearrange("p (f h v) -> p f h v", f=2, v=VH), [[0, 2], [VH, HEADS], [0, VH]], 64 * f, VH))
            for v, pattern, at0, size in groups:
                pool.affine_select(out=v, in_=v, compare_op=ALU.is_ge, fill=0.0, base=-at0,
                                   pattern=[[-st, n_] for st, n_ in pattern], channel_multiplier=1).then_inc(ev("band_low"), 1)
            pool.wait_ge(ev("band_low"), 3)
            for v, pattern, at0, size in groups:
                pool.affine_select(out=v, in_=v, compare_op=ALU.is_ge, fill=0.0, base=at0 + size - 1,
                                   pattern=pattern, channel_multiplier=-1).then_inc(ev("band_high"), 1)
            pool.wait_ge(ev("band_high"), 3)
            pool.tensor_tensor(mean_hd[:, :], mean_hd[:, :], band[:, :], ALU.add).then_inc(ev("pconst"), 2)
            pool.affine_select(out=ident[:, :], in_=ident[:, :], compare_op=ALU.not_equal, fill=1.0, base=0,
                               pattern=[[-1, 128]], channel_multiplier=1).then_inc(ev("pconst"), 1)

            pool.wait_ge(ev("pconst"), 8)
            pool.wait_ge(ev("mod_ready"), 1)

            def add_pull(B, n_):
                w_ = L - 1 - PULLS[n_]
                wait(pool, ev("pull_rank"), B.t * (L - 1) + n_ + 1)
                wait(pool, ev("pull_dec"), B.t * (L - 1) + n_ + 1)
                wait(pool, ev("pull_mul"), B.t * (L - 1) + n_ + 1)
                pool.tensor_tensor(q[:, :, :, PULLS[n_] + 1:L], cols(q_rank, 2, CB, w_), cols(q_dec, 2, CB, w_), ALU.add)\
                    .then_inc(ev("pull_add"), 1)

            def add_push(B, n_):
                j = PUSHES[n_]
                wait(pool, ev("push_rank"), B.t * (L - 1) + n_ + 1)
                wait(pool, ev("push_dec"), B.t * (L - 1) + n_ + 1)
                pool.tensor_tensor(kb[:, 0, :, 0:j], kb[:, 0, :, 0:j], cols(k_rank, CB, j), ALU.add).then_inc(ev("push_add"), 1)

            def work(at):
                A, B, R, G, N2 = (at(x) for x in (LAG_PROJ, LAG_CHUNK, LAG_SCAN, LAG_GN, LAG_LN2))
                if isinstance(at.i, int) and at.i == LAG_PROJ + 1:
                    for e in range(EXPERTS + 1):
                        pool.wait_ge(ev("w1_high"), e + 1)
                        pool.tensor_tensor(w1_lo[:, e, :], w1[:, e, :], w1_hi[:, e, :], ALU.subtract).then_inc(ev("w1_low"), 1)
                for s in range(SLOTS):
                    if N2 is not None and s == AT["pool_split"]:
                        wait(pool, ev("h2_ready"), (N2.t + 1) * BATCH)
                        wait(pool, ev("hid_mm"), (N2.t - 1) * (EXPERTS + 1) * 2)
                        wait(pool, ev("h2_high"), N2.t + 1)
                        pool.tensor_tensor(h2_lo[N2.par][:, :], h2[:, :], h2_hi[N2.par][:, :], ALU.subtract).then_inc(ev("h2_low"), 1)
                    if G is not None:
                        if s == AT["pool_gn"]:
                            wait(pool, ev("gn_recip"), G.t + 1)
                            wait(pool, ev("gn_affine"), G.t)
                            pool.tensor_tensor(gn_c[:, :], gn_c[:, :], gn_sd[:, :], ALU.mult).then_inc(ev("gn_norm"), 1)
                            wait(pool, ev("gn_norm"), G.t + 1)
                            wait(pool, ev("gn_gated"), G.t)
                            pool.tensor_scalar(gn_c[:, :], gn_c[:, :], vec[:, GNW:GNW + 1], vec[:, GNB:GNB + 1], ALU.mult, ALU.add)\
                                .then_inc(ev("gn_affine"), 1)
                            wait(pool, ev("gn_affine"), G.t + 1)
                            wait(pool, ev("gate_copied"), G.t + 1)
                            wait(pool, ev("wo_done"), G.t)
                            pool.tensor_tensor(gn_c[:, :], gn_c[:, :], gate_late[G.par][:, :], ALU.mult).then_inc(ev("gn_gated"), 1)
                    if B is not None and 0 <= s - AT["pool_u"] < L:
                        j = s - AT["pool_u"]
                        if j == 0:
                            wait(pool, ev(f"sent{B.par}"), 16 * 8 * (B.half + 1))
                            wait(pool, ev(f"vsent{B.par}"), 16 * 8 * (B.half + 1))
                            wait(pool, ev("state_ready"), (B.t - 1) * C)
                        slot = terms[:, :, (L + 2) * B.par, :].rearrange("p c (v k) -> p c v k", v=VH)
                        val = bc(vals[B.par][:, :, :].rearrange("p v (c l) -> p c v l", l=L)[:, :, :, j:j + 1], [128, C, VH, K])
                        key = bc(op_view(B.par, K0, L, j, j + 1).rearrange("p k c o -> p c o k"), [128, C, VH, K])
                        if j == 0:
                            pool.tensor_tensor(slot, val, key, ALU.mult).then_inc(ev("u_first"), 1)
                            wait(pool, ev("u_first"), B.t + 1)
                            wait(pool, ev("u_add"), B.t * (L - 1))
                        else:
                            pool.tensor_tensor(u_mul[:, :, :, :], val, key, ALU.mult).then_inc(ev("u_mul_done"), 1)
                            wait(pool, ev("u_mul_done"), B.t * (L - 1) + j)
                            pool.tensor_tensor(slot, slot, u_mul[:, :, :, :], ALU.add).then_inc(ev("u_add"), 1)
                            if j < L - 1:
                                wait(pool, ev("u_add"), B.t * (L - 1) + j)
                    if R is not None:
                        if s == AT["pool_gv"]:
                            wait(pool, ev("o_reduced"), R.t * L)
                            ot = o_terms[:, :, :].rearrange("p (c j v) x -> p c j v x", c=C, j=L)
                            for c_ in range(L - 1):
                                for j in range(c_, L - 1):
                                    g_at = j * (j + 1) // 2 + c_
                                    sc = bc(op_view(R.par, G0, NG, g_at, g_at + 1)[:, 0, :, :], [128, C, VH])
                                    vv = vals[R.par][:, :, :].rearrange("p v (c l) -> p c v l", l=L)[:, :, :, c_]
                                    last = pool.tensor_tensor(ot[:, :, j, :, K + c_], sc, vv, ALU.mult)
                                last.then_inc(ev("gv_done"), 1)
                    if G is not None and 0 <= s - AT["pool_s"] < L:
                        if s == AT["pool_s"]:
                            wait(pool, ev("state_ready"), (G.t + 1) * C)
                            wait(pool, ev("s_terms"), G.t * L)
                            pool.tensor_copy(state[G.par][:, 0, :], state[1 - G.par][:, C, :]).then_inc(ev("state_copied"), 1)
                            wait(pool, ev("state_copied"), G.t + 1)
                            wait(pool, ev("o_reduced"), G.t * L)
                        ot = o_terms[:, :, :].rearrange("p (c j v) x -> p c j v x", c=C, j=L)
                        for j in (s - AT["pool_s"],):
                            c0 = 1 if j == L - 1 else 0
                            st = state[G.par][:, c0:c0 + C, :].rearrange("p c (v k) -> p c v k", v=VH)
                            xv = bc(op_view(G.par, X0, L, j, j + 1).rearrange("p k c o -> p c o k"), [128, C, VH, K])
                            pool.tensor_tensor(ot[:, :, j, :, 0:K], st, xv, ALU.mult).then_inc(ev("s_terms"), 1)
                    if A is not None:
                        if s == AT["pool_shift"]:
                            wait(pool, ev("h1_ready"), (A.t + 1) * BATCH)
                            wait(pool, ev("mix_ready"), A.t * 7)
                            if not (isinstance(A.t, int) and A.t == 0):
                                pool.tensor_copy(h1[A.par][:, :, 0:1], h1[1 - A.par][:, :, STEPS:STEPS + 1])\
                                    .then_inc(ev("h1_edge"), 1)
                                wait(pool, ev("h1_edge"), A.t)
                            pool.tensor_tensor(shift[:, :, :], h1[A.par][:, :, 0:STEPS], h1[A.par][:, :, 1:STEPS + 1], ALU.subtract)\
                                .then_inc(ev("shift_ready"), 1)
                        if s == AT["pool_ab"]:
                            wait(pool, ev("norm_recip"), (A.t + 1) * 2)
                            wait(pool, ev("ab_copied"), (A.t + 1) * 2)
                            wait(pool, ev("push_mul"), (A.t - 1) * (L - 1))
                            wait(pool, ev("q_copied"), A.t - 1)
                            wait(pool, ev("pull_rank"), (A.t - 1) * (L - 1))
                            wait(pool, ev("packed"), (A.t - 1) * 7)
                            pool.tensor_tensor(ar[A.par][:, 0, :, :].rearrange("p c l -> p (c l)"), ab_raw[:, 0, :], ab_sq[:, 0, :], ALU.mult)\
                                .then_inc(ev("a_ready"), 1)
                            wait(pool, ev("push_rank"), (A.t - 1) * (L - 1))
                            wait(pool, ev("pull_mul"), (A.t - 1) * (L - 1))
                            wait(pool, ev("kb_copied"), (A.t - 1) * 2)
                            pool.tensor_tensor(b_raw[A.par][:, :, :].rearrange("p c l -> p (c l)"), ab_raw[:, 1, :], ab_sq[:, 1, :], ALU.mult)\
                                .then_inc(ev("b_ready"), 1)
                        if s == AT["pool_ar"]:
                            wait(pool, ev("r_ready"), A.t + 1)
                            wait(pool, ev("q_copied"), A.t - 1)
                            wait(pool, ev("push_mul"), (A.t - 1) * (L - 1))
                            pool.tensor_copy(ar[A.par][:, 1, :, 1:L], r_raw[A.par][:, :, 0:L - 1]).then_inc(ev("ar_r"), 1)
                    if B is not None:
                        par = B.par
                        if s == AT["pool_pull"]:
                            wait(pool, ev("a_ready"), B.t + 1)
                            wait(pool, ev("ar_r"), B.t + 1)
                            wait(pool, ev("packed"), B.t * 7)
                            pool.tensor_copy(q[:, :, :, 1:L], ar[par][:, :, :, 1:L]).then_inc(ev("q_copied"), 1)
                            wait(pool, ev("b_ready"), B.t + 1)
                            wait(pool, ev("k_ready"), B.t + 1)
                            pool.tensor_copy(kb[:, 0, :, :], k_raw[par][:, :, :]).then_inc(ev("kb_copied"), 1)
                            pool.tensor_copy(kb[:, 1, :, :], b_raw[par][:, :, :]).then_inc(ev("kb_copied"), 1)
                            wait(pool, ev("q_copied"), B.t + 1)
                            wait(pool, ev("kb_copied"), (B.t + 1) * 2)
                        for n_, j in enumerate(PULLS):
                            if s == AT["pool_pull"] + PACE[n_]:
                                w_ = L - 1 - j
                                if n_ > 0:
                                    add_pull(B, n_ - 1)
                                    wait(pool, ev("pull_add"), B.t * (L - 1) + n_)
                                wait(pool, ev("pull_sum"), B.t * (L - 1) + n_)
                                pool.tensor_tensor(cols(q_mul, 2, CB, w_), q[:, :, :, j + 1:L], per_chunk2(b_raw[par], j, w_), ALU.mult)\
                                    .then_inc(ev("pull_mul"), 1)
                                pool.tensor_tensor(cols(q_dec, 2, CB, w_), q[:, :, :, j + 1:L], per_chunk2(dec[par], j, w_), ALU.mult)\
                                    .then_inc(ev("pull_dec"), 1)
                        if s == AT["pool_pull"] + PACE[L - 1]:
                            add_pull(B, L - 2)
                        if s == AT["pool_push"] + PACE[L - 1]:
                            add_push(B, L - 2)
                        for n_, j in enumerate(PUSHES):
                            if s == AT["pool_push"] + PACE[n_]:
                                if n_ > 0:
                                    add_push(B, n_ - 1)
                                    wait(pool, ev("push_add"), B.t * (L - 1) + n_)
                                    wait(pool, ev("push_dec"), B.t * (L - 1) + n_)
                                wait(pool, ev("push_sum"), B.t * (L - 1) + n_)
                                pool.tensor_tensor(cols(k_mul, 2, CB, j),
                                                   bc(kb[:, 0:1, :, 0:j], [128, 2, CB, j]),
                                                   bc(ar[par][:, :, :, j:j + 1], [128, 2, CB, j]), ALU.mult)\
                                    .then_inc(ev("push_mul"), 1)
                                wait(pool, ev("push_mul"), B.t * (L - 1) + n_ + 1)
                                pool.tensor_tensor(kb[:, :, :, 0:j], kb[:, :, :, 0:j], per_chunk2(dec[par], j, j), ALU.mult)\
                                    .then_inc(ev("push_dec"), 1)
                                src = dec[par][:, :, 0:1] if j == 1 else lam[:, :, j - 1:j]
                                if j > 1:
                                    wait(pool, ev("lam_mul"), B.t * (L - 1) + j - 1)
                                pool.tensor_tensor(lam[:, :, j:j + 1], src, dec[par][:, :, j:j + 1], ALU.mult)\
                                    .then_inc(ev("lam_mul"), 1)
            run_tiles(pool, work)

        @block.vector
        def _(dve):
            dve.wait_ge(ev("const"), 3)
            for m in (1, 4):
                dve.tensor_scalar(mod[:, m, :], mod[:, m, :], 1.0, None, ALU.add).then_inc(ev("mod_step"), 1)
            for n_, m in enumerate((2, 5)):
                dve.tensor_scalar(mod_sign[:, n_, :], mod[:, m, :], 0.0, 2.0, ALU.is_ge, ALU.mult).then_inc(ev("mod_step"), 1)
            dve.wait_ge(ev("mod_step"), 4)
            dve.tensor_scalar(mod_sign[:, :, :], mod_sign[:, :, :], -1.0, None, ALU.add).then_inc(ev("mod_step"), 1)
            dve.tensor_scalar(mod_abs[:, :, :], mod_abs[:, :, :], GATE_MIN, None, ALU.max).then_inc(ev("mod_step"), 1)
            dve.wait_ge(ev("mod_step"), 6)
            for n_, m in enumerate((2, 5)):
                dve.tensor_tensor(mod[:, m, :], mod_sign[:, n_, :], mod_abs[:, n_, :], ALU.mult).then_inc(ev("mod_step"), 1)
            dve.wait_ge(ev("mod_step"), 8)
            dve.wait_ge(ev("w_loaded"), 16 * 3)
            dve.tensor_scalar(ga_bo[:, :], mod[:, 2, :], vec[:, BO:BO + 1], None, ALU.mult).then_inc(ev("mod_ready"), 1)
            dve.wait_ge(ev("pconst"), 8)

            def norm(t, ps, src, c, sd, name, stage, consumed=None):
                if stage == 0:
                    wait(dve, ev(f"{name}_mean"), t.t + 1)
                    wait(dve, consumed[0], consumed[1])
                    dve.tensor_tensor(c[:, :], src, ps, ALU.subtract).then_inc(ev(f"{name}_center"), 1)
                elif stage == 1:
                    wait(dve, ev(f"{name}_sqrt"), t.t + 1)
                    dve.reciprocal(sd[:, :], sd[:, :]).then_inc(ev(f"{name}_recip"), 1)
                else:
                    dve.wait_ge(ev(f"{name}_recip"), t.t + 1)
                    dve.tensor_tensor(c[:, :], c[:, :], sd[:, :], ALU.mult).then_inc(ev(f"{name}_norm"), 1)

            def chunk(R, c, part):
                par, n_ = R.par, R.t * C + c
                if part == 0:
                    before = state[1 - par][:, C, :] if c == 0 else state[par][:, c, :]
                    wait(dve, ev("state_ready"), n_)
                    if c == 0:
                        wait(dve, ev(f"sent{par}"), 16 * 8 * (R.half + 1))
                    sv = bc(before.rearrange("p (o v k) -> p o v k", o=1, v=VH), [128, L + 1, VH, K])
                    yv = bc(ops[par][:, :, Y0 + c * (L + 1):Y0 + (c + 1) * (L + 1)].rearrange("p k (j o) -> p j o k", o=1), [128, L + 1, VH, K])
                    dve.tensor_tensor(terms[:, c, 1:L + 2, :].rearrange("p j (v k) -> p j v k", v=VH), sv, yv, ALU.mult)\
                        .then_inc(ev("dots"), 1)
                elif part == 1:
                    dve.wait_ge(ev("dots"), n_ + 1)
                    dve.tensor_reduce(z[par][:, c, :], terms[:, c, 2:L + 2, :].rearrange("p j (v k) -> p (j v) k", v=VH), AX.X, ALU.add)\
                        .then_inc(ev("z_done"), 1)
                elif part == 2:
                    dve.wait_ge(ev("z_done"), n_ + 1)
                    zv = bc(z[par][:, c, :].rearrange("p (j v o) -> p j v o", j=L, o=1), [128, L, VH, K])
                    bv = bc(ops[par][:, :, B0 + c * L:B0 + (c + 1) * L].rearrange("p k (j o) -> p j o k", o=1), [128, L, VH, K])
                    dve.tensor_tensor(terms[:, c, 2:L + 2, :].rearrange("p j (v k) -> p j v k", v=VH), zv, bv, ALU.mult)\
                        .then_inc(ev("outer"), 1)
                else:
                    dve.wait_ge(ev("outer"), n_ + 1)
                    if c == C - 1:
                        wait(dve, ev("state_copied"), R.t)
                    if c == 0:
                        wait(dve, ev("u_add"), (R.t + 1) * (L - 1))
                        wait(dve, ev("s_terms"), (R.t - 1) * L)
                    dve.tensor_reduce(state[par][:, c + 1, :], terms[:, c, par:par + L + 2, :].rearrange("p s a -> p a s"), AX.X, ALU.add)\
                        .then_inc(ev("state_ready"), 1)

            def expert_out(E, e, g):
                n_, cs = E.t * (EXPERTS + 1) + e, slice(g * 128, (g + 1) * 128)
                if g == 0:
                    wait(dve, ev("y_mm"), n_ + 1)
                    if e == 0:
                        wait(dve, ev("rt_ready"), E.t + 1)
                        wait(dve, ev("out_turned"), E.t - 1)
                    else:
                        dve.wait_ge(ev("y_acc"), n_ * TG)
                y, w_, to, so_far = ps_y[(E.par + e) % 2][:, cs], rt_w[E.par], acc[E.par][:, cs], acc[E.par][:, cs]
                if e == 0:
                    dve.tensor_scalar(to, y, w_[:, g, 0:1], None, ALU.mult).then_inc(ev("y_acc"), 1)
                elif e < EXPERTS:
                    dve.scalar_tensor_tensor(out=to, in0=y, scalar=w_[:, g, e:e + 1], in1=so_far, op0=ALU.mult, op1=ALU.add)\
                        .then_inc(ev("y_acc"), 1)
                else:
                    dve.tensor_tensor(to, y, so_far, ALU.add).then_inc(ev("y_acc"), 1)

            def mix(A, m):
                wait(dve, ev("proj_done"), (A.t - 1) * 4 + m // 2 + 1)
                dve.scalar_tensor_tensor(out=bt(mixed[:, m, :]), in0=shift[:, :, :],
                                         scalar=vec[:, MIX0 + m:MIX0 + m + 1], in1=h1[A.par][:, :, 1:STEPS + 1],
                                         op0=ALU.mult, op1=ALU.add).then_inc(ev("mix_ready"), 1)

            def router_top(N2):
                wait(dve, ev("rt_logit"), N2.t + 1)
                lg = ps_rt[:, 0:TG * EXPERTS].rearrange("p (g e) -> p g e", g=TG)
                dve.tensor_copy(rt_lg[:, :, 0:EXPERTS], lg).then_inc(ev("rt_copied"), 1)
                dve.wait_ge(ev("rt_copied"), N2.t + 1)
                dve.sem_inc(ev("passed"))
                for g in range(TG):
                    dve.max(rt_top[:, g, :], rt_lg[:, g, 0:EXPERTS]).then_inc(ev("rt_topped"), 1)
                dve.wait_ge(ev("rt_topped"), (N2.t + 1) * TG)
                dve.tensor_tensor(rt_d[:, :, 0:EXPERTS], rt_lg[:, :, 0:EXPERTS], bc(rt_top[:, :, 0:1], [128, TG, EXPERTS]),
                                  ALU.subtract).then_inc(ev("rt_gap1"), 1)
                dve.tensor_tensor(rt_d[:, :, EXPERTS:EXPERTS + 1], rt_top[:, :, 1:2], rt_top[:, :, 0:1], ALU.subtract)\
                    .then_inc(ev("rt_gap1"), 1)
                for g in range(TG):
                    dve.max_index(rt_ix[:, g, :], rt_top[:, g, :], rt_lg[:, g, 0:EXPERTS]).then_inc(ev("rt_indexed"), 1)
                dve.wait_ge(ev("rt_indexed"), (N2.t + 1) * TG)
                dve.tensor_copy(rt_ixf[:, :, :], rt_ix[:, :, :]).then_inc(ev("rt_ix_f"), 1)

            def router_exp(N2, part):
                if part == 0:
                    wait(dve, ev("rt_tanh1"), N2.t + 1)
                    dve.tensor_scalar(rt_den[:, :, :], rt_th[:, :, :], -1.0, 1.0, ALU.mult, ALU.add).then_inc(ev("rt_dn"), 1)
                    dve.tensor_scalar(rt_num[:, :, :], rt_th[:, :, :], 1.0, None, ALU.add).then_inc(ev("rt_n"), 1)
                    dve.wait_ge(ev("rt_dn"), N2.t + 1)
                    dve.reciprocal(rt_inv[:, :, :], rt_den[:, :, :]).then_inc(ev("rt_i"), 1)
                elif part == 1:
                    dve.wait_ge(ev("rt_n"), N2.t + 1)
                    dve.wait_ge(ev("rt_i"), N2.t + 1)
                    dve.tensor_tensor(rt_exp[:, :, :], rt_num[:, :, :], rt_inv[:, :, :], ALU.mult).then_inc(ev("rt_e"), 1)
                elif part == 2:
                    dve.wait_ge(ev("rt_e"), N2.t + 1)
                    dve.tensor_reduce(rt_sum[:, :], rt_exp[:, :, 0:EXPERTS], AX.X, ALU.add).then_inc(ev("rt_s"), 1)
                    dve.tensor_scalar(rt_gap[:, :], rt_exp[:, :, EXPERTS], -1.0, 1.0, ALU.mult, ALU.add).then_inc(ev("rt_gapped"), 1)
                else:
                    dve.wait_ge(ev("rt_s"), N2.t + 1)
                    dve.reciprocal(rt_sinv[:, :], rt_sum[:, :]).then_inc(ev("rt_si"), 1)
                    dve.wait_ge(ev("rt_si"), N2.t + 1)
                    dve.wait_ge(ev("rt_gapped"), N2.t + 1)
                    dve.tensor_tensor(rt_u[:, :], rt_gap[:, :], rt_sinv[:, :], ALU.mult).then_inc(ev("rt_uu"), 1)

            def router_weights(N2, part):
                if part == 0:
                    wait(dve, ev("rt_tanh2"), N2.t + 1)
                    dve.tensor_scalar(rt_w1[:, :], rt_ut[:, :], 0.5, 0.5, ALU.mult, ALU.add).then_inc(ev("rt_weights"), 1)
                    dve.tensor_scalar(rt_w2[:, :], rt_ut[:, :], -0.5, 0.5, ALU.mult, ALU.add).then_inc(ev("rt_weights"), 1)
                elif part == 1:
                    dve.wait_ge(ev("rt_weights"), (N2.t + 1) * 2)
                    dve.wait_ge(ev("rt_ix_f"), N2.t + 1)
                    for g in range(TG):
                        dve.tensor_scalar(rt_a[:, g, :], iota_f[:, :], rt_ixf[:, g, 0:1], rt_w1[:, g:g + 1], ALU.is_equal, ALU.mult)\
                            .then_inc(ev("rt_wa"), 1)
                        dve.tensor_scalar(rt_b[:, g, :], iota_f[:, :], rt_ixf[:, g, 1:2], rt_w2[:, g:g + 1], ALU.is_equal, ALU.mult)\
                            .then_inc(ev("rt_wb"), 1)
                elif part == 2:
                    dve.wait_ge(ev("rt_wa"), (N2.t + 1) * TG)
                    dve.wait_ge(ev("rt_wb"), (N2.t + 1) * TG)
                    dve.tensor_tensor(rt_w[N2.par][:, :, :], rt_a[:, :, :], rt_b[:, :, :], ALU.add).then_inc(ev("rt_ready"), 1)

            def work(at):
                A, B, R, G, N2, E, O = (at(x) for x in (LAG_PROJ, LAG_CHUNK, LAG_SCAN, LAG_GN, LAG_LN2, LAG_FFN, LAG_OUT))
                for s in range(SLOTS):
                    for part in range(4):
                        if R is not None and 1 <= s <= C:
                            chunk(R, s - 1, part)
                        if E is not None and s % 2 == 1 and s >= 3 and part < TG:
                            expert_out(E, (s - 3) // 2, part)
                        if A is not None:
                            if s == AT["dve_center"] and part == 1:
                                norm(A, ps_ln1, x_in[A.par][:, :], ln1_c, ln1_sd, "ln1", 0, (ev("h1_ready"), A.t * BATCH))
                            if s == AT["dve_ln1"] and part == 2:
                                norm(A, ps_ln1, None, ln1_c, ln1_sd, "ln1", 1)
                            if s == AT["dve_ln1"] and part == 3:
                                norm(A, ps_ln1, None, ln1_c, ln1_sd, "ln1", 2)
                            if s in (AT["dve_mix"], AT["dve_mix"] + 1):
                                m = (s - AT["dve_mix"]) * 4 + part
                                if part == 0:
                                    wait(dve, ev("shift_ready"), A.t + 1)
                                if m < 7:
                                    mix(A, m)
                            if s == AT["dve_ab_recip"] and part == 0:
                                wait(dve, ev("norm_sqrt"), A.t + 1)
                                dve.tensor_scalar(ab_sq[:, :, :], ab_sq[:, :, :], NORM_EPS, None, ALU.max).then_inc(ev("norm_max"), 1)
                            if s == AT["dve_ab_recip"] and part in (1, 2):
                                if part == 1:
                                    dve.wait_ge(ev("norm_max"), A.t + 1)
                                dve.reciprocal(ab_sq[:, part - 1, :], ab_sq[:, part - 1, :]).then_inc(ev("norm_recip"), 1)
                        if N2 is not None:
                            if s == AT["dve_center2"] and part == 2:
                                norm(N2, ps_ln2, x2[N2.par][:, :], ln2_c, ln2_sd, "ln2", 0, (ev("h2_ready"), N2.t * BATCH))
                            if s == AT["dve_ln2"] and part == 0:
                                norm(N2, ps_ln2, None, ln2_c, ln2_sd, "ln2", 1)
                            if s == AT["dve_ln2"] and part == 1:
                                norm(N2, ps_ln2, None, ln2_c, ln2_sd, "ln2", 2)
                            if s == AT["dve_rt_top"] and part == 2:
                                router_top(N2)
                            if s == AT["dve_rt_exp"]:
                                router_exp(N2, part)
                            if s == AT["dve_rt_weights"]:
                                router_weights(N2, part)
                        if B is not None:
                            par = B.par
                            for n_, j in enumerate(PULLS):
                                if s == AT["dve_pull"] + PACE[n_] and part == 0:
                                    w_ = L - 1 - j
                                    wait(dve, ev("pull_sum"), B.t * (L - 1) + n_ + 1)
                                    wait(dve, ev("pull_add"), B.t * (L - 1) + n_)
                                    dve.tensor_tensor(cols(q_rank, 2, CB, w_), cols(ps_sum, 2, CB, w_), per_chunk2(ar[par][:, 0], j, w_), ALU.mult)\
                                        .then_inc(ev("pull_rank"), 1)
                            for n_, j in enumerate(PUSHES):
                                if s == AT["dve_push"] + PACE[n_] and part == 0:
                                    wait(dve, ev("push_sum"), B.t * (L - 1) + n_ + 1)
                                    wait(dve, ev("push_add"), B.t * (L - 1) + n_)
                                    dve.tensor_tensor(cols(k_rank, CB, j), cols(ps_sum, CB, j), per_chunk(b_raw[par], j, j), ALU.mult)\
                                        .then_inc(ev("push_rank"), 1)
                        if G is not None:
                            if 0 <= s - AT["dve_o"] < L and part == 2:
                                j = s - AT["dve_o"]
                                wait(dve, ev("s_terms"), G.t * L + j + 1)
                                if j == 0:
                                    wait(dve, ev("gv_done"), (G.t + 1) * (L - 1))
                                    wait(dve, ev(f"o_back{G.par}"), 16 * 8 * G.half)
                                ot = o_terms[:, :, :].rearrange("p (c j v) x -> p j c v x", c=C, j=L)[:, j]
                                dst = o_scan[G.par][:, :, :].rearrange("p v (c j) -> p j c v", j=L)[:, j]
                                dve.tensor_reduce(dst, ot, AX.X, ALU.add).then_inc(ev("o_reduced"), 1)
                            if s == AT["dve_gn_center"] and part == 0:
                                norm(G, ps_gn, o_ch[G.par][:, :], gn_c, gn_sd, "gn", 0, (ev("wo_done"), G.t))
                            if s == AT["dve_gn"] and part == 3:
                                norm(G, ps_gn, None, gn_c, gn_sd, "gn", 1)
                            if s == AT["dve_x2"]:
                                if part == 0:
                                    wait(dve, ev("wo_done"), G.t + 1)
                                    wait(dve, ev("x_biased"), (G.t + 1) * BATCH)
                                    wait(dve, ev("x2_saved"), G.t - 1)
                                    wait(dve, ev("ln2_mean"), G.t - 1)
                                cs = slice(part * STEPS, (part + 1) * STEPS)
                                dve.scalar_tensor_tensor(out=x2[G.par][:, cs], in0=ps_gn[:, cs], scalar=mod[:, 2, part:part + 1],
                                                         in1=x_res[G.par][:, cs], op0=ALU.mult, op1=ALU.add).then_inc(ev("x2_ready"), 1)
                        if O is not None and s == AT["dve_out"]:
                            if part == 0:
                                wait(dve, ev("out_turned"), O.t + 1)
                                wait(dve, ev("x2_saved"), O.t + 1)
                            cs = slice(part * STEPS, (part + 1) * STEPS)
                            dve.scalar_tensor_tensor(out=x2_late[O.par][:, cs], in0=ps_out[:, cs], scalar=mod[:, 5, part:part + 1],
                                                     in1=x2_late[O.par][:, cs], op0=ALU.mult, op1=ALU.add).then_inc(ev("out_ready"), 1)

            run_tiles(dve, work)


def kernel(**inputs):
    import concourse.bacc as bacc
    from concourse.bass_utils import run_bass_kernel_spmd

    def a(name):
        return np.asarray(inputs[name])

    attn = "L0_attn_"
    order = np.arange(D).reshape(HEADS, 2, VH).transpose(1, 0, 2).reshape(D)
    w_of = {p: a(attn + "W_" + p) for p in PROJ + ["o"]}
    w_of["v"], w_of["g"], w_of["o"] = w_of["v"][order], w_of["g"][order], w_of["o"][:, order]
    w = np.stack([w_of[p].T for p in PROJ + ["o"]], axis=1)
    vec = np.zeros((128, VECS), np.float32)
    for i, p in enumerate(PROJ):
        vec[:, MIX0 + i] = a(attn + "x_" + p)
    vec[:, BO], vec[:, GNW], vec[:, GNB] = a(attn + "b_o"), a(attn + "gn_w")[order], a(attn + "gn_b")[order]
    vec[:ROUTER, BR1] = a("L0_ffn_br1")
    be1 = np.concatenate([a("L0_ffn_be1"), a("L0_ffn_bs1")[None]])
    vec[:, BE1:] = be1.reshape((EXPERTS + 1) * HB, 128).T
    w1 = np.concatenate([a("L0_ffn_We1"), a("L0_ffn_Ws1")[None]]).transpose(1, 0, 2)
    w2 = np.concatenate([a("L0_ffn_We2"), a("L0_ffn_Ws2")[None]]).reshape(EXPERTS + 1, HB, 128, 128).transpose(2, 0, 1, 3)
    x = a("L0_attn_x").reshape(BATCH, TILES, STEPS, D).transpose(3, 1, 0, 2).reshape(D, TILES * N)
    arrays = {
        "x": x, "w": w, "vec": vec, "cond": a("L0_c").T, "wmod": a("L0_wmod"), "wr1": a("L0_ffn_Wr1"),
        "wr2": np.concatenate([a("L0_ffn_Wr2"), a("L0_ffn_br2")[None]]), "w1": w1, "w2": w2,
        "be2": np.concatenate([a("L0_ffn_be2"), a("L0_ffn_bs2")[None]]),
    }
    arrays = {"in_" + k: np.ascontiguousarray(v) for k, v in arrays.items()}
    nc = bacc.Bacc("TRN2", target_bir_lowering=False, num_devices=1)
    aps = [nc.dram_tensor(k, v.shape, mybir.dt.float32, kind="ExternalInput").ap() for k, v in arrays.items()]
    out = nc.dram_tensor("out", (D, TILES * N), mybir.dt.float32, kind="ExternalOutput").ap()
    build(nc, *aps, out)
    r = run_bass_kernel_spmd(nc, [arrays], core_ids=[0])
    y = r.results[0]["out"]
    return np.ascontiguousarray(y.reshape(D, TILES, BATCH, STEPS).transpose(2, 1, 3, 0).reshape(BATCH, TIME, D))
```
